# Optimizing a Trainium2 kernel written in Bass

```python
import numpy as np
import jax
import jax.numpy as jnp

def _softmax(x, axis=-1):
    return jax.nn.softmax(x, axis=axis)

def _gelu(x):
    return jax.nn.gelu(x, approximate=True)

def _silu(x):
    return jax.nn.silu(x)

def _sigmoid(x):
    return jax.nn.sigmoid(x)

def _layernorm(x, axis=-1, eps=1e-05):
    m = jnp.mean(x, axis=axis, keepdims=True)
    v = jnp.var(x, axis=axis, keepdims=True)
    return (x - m) / jnp.sqrt(v + eps)

def _scatter_add(tgt, idx, src, axis=0):
    return tgt.at[idx].add(src)

def _segment_sum(src, seg, n):
    return jax.ops.segment_sum(src, seg, n)
kernel_name = 'mk_decoder_postln_d1_seqx_r4_51b656'

def setup_inputs(seed: int=0):
    np.random.seed(seed)
    _w = jnp.asarray

    def _rec_inputs():
        import jax
        import jax.numpy as jnp
        _rk = jax.random.key(seed)
        x = -0.0005146 + 1 * jax.random.normal(jax.random.fold_in(_rk, 1), (8, 256, 256), jnp.float32)
        _lenS = 256 - jax.random.randint(jax.random.fold_in(_rk, 7), (8,), 0, max(1, 256 // 4) + 1, jnp.int32)
        _lenS2 = 77 - jax.random.randint(jax.random.fold_in(_rk, 8), (8,), 0, max(1, 77 // 4) + 1, jnp.int32)
        _ctx_768P = jax.random.normal(jax.random.fold_in(_rk, 11), (8, 16, 192), jnp.float32)
        _ctx_768c = jax.random.dirichlet(jax.random.fold_in(_rk, 511), 0.3 * jnp.ones((16,), jnp.float32), (8, 77))
        _ctx_768t = jnp.einsum('bsk,bkd->bsd', _ctx_768c, _ctx_768P)
        _ctx_768t = _ctx_768t * jax.lax.rsqrt(jnp.mean(jnp.square(_ctx_768t)) + 1e-12) * 0.953939
        ctx_768 = -0.00040386 + 0.999972 * (_ctx_768t + 0.3 * jax.random.normal(jax.random.fold_in(_rk, 611), (8, 77, 192), jnp.float32))
        _validS = jnp.arange(256)[None, :] < _lenS[:, None]
        _validS2 = jnp.arange(77)[None, :] < _lenS2[:, None]
        _causal = jnp.tril(jnp.ones((256, 256), dtype=bool))
        mask_BxS2_bk0 = jnp.logical_not(jnp.broadcast_to(_validS2[:, :], (8, 77)))
        return (x, ctx_768, mask_BxS2_bk0)
    x, ctx_768, mask_BxS2_bk0 = _rec_inputs()

    def _L0_attn_setup():
        import jax, jax.numpy as jnp
        import numpy as np
        HEADS = 16
        KV_HEADS = 4
        DIM_HEAD = 64
        SCALE = DIM_HEAD ** (-0.5)

        def _rotate_half(x):
            x1, x2 = jnp.split(x, 2, axis=-1)
            return jnp.concatenate((-x2, x1), axis=-1)

        def _rope_freqs(n, d):
            inv_freq = 1.0 / 10000.0 ** (jnp.arange(0, d, 2, dtype=jnp.float32) / d)
            freqs = jnp.einsum('i,j->ij', jnp.arange(n, dtype=jnp.float32), inv_freq)
            return jnp.concatenate((freqs, freqs), axis=-1)
        key = jax.random.key(seed)
        ks = jax.random.split(key, 4)
        b, n, dim = (2, 512, 256)
        inner = HEADS * DIM_HEAD
        s = dim ** (-0.5)
        return {'x': jax.random.normal(ks[0], (b, n, dim), jnp.float32), 'Wq': jax.random.normal(ks[1], (dim, inner), jnp.float32) * s, 'Wkv': jax.random.normal(ks[2], (dim, DIM_HEAD * KV_HEADS * 2), jnp.float32) * s, 'Wo': jax.random.normal(ks[3], (inner, dim), jnp.float32) * s, 'bo': jnp.zeros((dim,), jnp.float32)}
    _L0_attn_all = _L0_attn_setup()
    _L0_attn_in = {k: v for k, v in _L0_attn_all.items() if k in ('Wq', 'Wkv', 'Wo', 'bo')}
    del _L0_attn_all

    def _L0_xattn_setup():
        import jax, jax.numpy as jnp
        import numpy as np
        DIM_IN, DIM_LAT, DIM_HEAD = (192, 256, 64)
        INNER = max(DIM_LAT, DIM_IN)
        HEADS = INNER // DIM_HEAD
        SCALE = DIM_HEAD ** (-0.5)
        RMS_EPS = 1e-08
        LN_EPS = 1e-05

        def layernorm(x, g, b):
            mu = jnp.mean(x, axis=-1, keepdims=True)
            var = jnp.mean((x - mu) ** 2, axis=-1, keepdims=True)
            return (x - mu) * jax.lax.rsqrt(var + LN_EPS) * g + b

        def rmsnorm(x, gamma):
            norm = jnp.sqrt(jnp.sum(x * x, axis=-1, keepdims=True)) * x.shape[-1] ** (-0.5)
            return x / jnp.maximum(norm, RMS_EPS) * gamma
        key = jax.random.key(seed)
        ks = jax.random.split(key, 12)
        b, n, m = (4, 1024, 128)
        x = jax.random.normal(ks[0], (b, n, DIM_IN), jnp.float32)
        latents = jax.random.normal(ks[1], (b, m, DIM_LAT), jnp.float32)
        mask = jax.random.randint(ks[2], (b, n), 0, 2).astype(bool)
        s = lambda k, sh, fan: jax.random.normal(k, sh, jnp.float32) * fan ** (-0.5)
        return {'x': x, 'latents': latents, 'mask': mask, 'ln_x_g': jnp.ones((DIM_IN,), jnp.float32), 'ln_x_b': jnp.zeros((DIM_IN,), jnp.float32), 'ln_l_g': jnp.ones((DIM_LAT,), jnp.float32), 'ln_l_b': jnp.zeros((DIM_LAT,), jnp.float32), 'qn_g': jnp.ones((DIM_HEAD,), jnp.float32), 'kn_g': jnp.ones((DIM_HEAD,), jnp.float32), 'Wq': s(ks[3], (INNER, DIM_LAT), DIM_LAT), 'Wkv': s(ks[4], (2 * INNER, DIM_IN), DIM_IN), 'Wlkv': s(ks[5], (2 * INNER, DIM_LAT), DIM_LAT), 'Wo': s(ks[6], (DIM_LAT, INNER), INNER), 'bo': jnp.zeros((DIM_LAT,), jnp.float32)}
    _L0_xattn_all = _L0_xattn_setup()
    _L0_xattn_in = {k: v for k, v in _L0_xattn_all.items() if k in ('ln_x_g', 'ln_x_b', 'ln_l_g', 'ln_l_b', 'qn_g', 'kn_g', 'Wq', 'Wkv', 'Wlkv', 'Wo', 'bo')}
    del _L0_xattn_all

    def _L0_ffn_setup():
        import jax, jax.numpy as jnp
        import numpy as np
        NUM_EXPERTS = 8
        TOP_K = 2
        N_EMBD = 256
        B, T = (4, 512)
        key = jax.random.key(seed)
        k_x, k_g, k_e = jax.random.split(key, 3)
        x = jax.random.normal(k_x, (B, T, N_EMBD), dtype=jnp.float32)
        scale = 1.0 / np.sqrt(N_EMBD)
        gate_w = jax.random.uniform(k_g, (NUM_EXPERTS, N_EMBD), dtype=jnp.float32, minval=-scale, maxval=scale)
        expert_w = jax.random.uniform(k_e, (NUM_EXPERTS, N_EMBD, N_EMBD), dtype=jnp.float32, minval=-scale, maxval=scale)
        return {'x': x, 'gate_w': gate_w, 'expert_w': expert_w}
    _L0_ffn_all = _L0_ffn_setup()
    _L0_ffn_in = {k: v for k, v in _L0_ffn_all.items() if k in ('gate_w', 'expert_w')}
    del _L0_ffn_all
    return {'x': x, 'ctx_768': ctx_768, 'mask_BxS2_bk0': mask_BxS2_bk0, 'L0_attn_Wq': _L0_attn_in['Wq'], 'L0_attn_Wkv': _L0_attn_in['Wkv'], 'L0_attn_Wo': _L0_attn_in['Wo'], 'L0_attn_bo': _L0_attn_in['bo'], 'L0_xattn_ln_x_g': _L0_xattn_in['ln_x_g'], 'L0_xattn_ln_x_b': _L0_xattn_in['ln_x_b'], 'L0_xattn_ln_l_g': _L0_xattn_in['ln_l_g'], 'L0_xattn_ln_l_b': _L0_xattn_in['ln_l_b'], 'L0_xattn_qn_g': _L0_xattn_in['qn_g'], 'L0_xattn_kn_g': _L0_xattn_in['kn_g'], 'L0_xattn_Wq': _L0_xattn_in['Wq'], 'L0_xattn_Wkv': _L0_xattn_in['Wkv'], 'L0_xattn_Wlkv': _L0_xattn_in['Wlkv'], 'L0_xattn_Wo': _L0_xattn_in['Wo'], 'L0_xattn_bo': _L0_xattn_in['bo'], 'L0_ffn_gate_w': _L0_ffn_in['gate_w'], 'L0_ffn_expert_w': _L0_ffn_in['expert_w']}

def reference(x, ctx_768, mask_BxS2_bk0, L0_attn_Wq, L0_attn_Wkv, L0_attn_Wo, L0_attn_bo, L0_xattn_ln_x_g, L0_xattn_ln_x_b, L0_xattn_ln_l_g, L0_xattn_ln_l_b, L0_xattn_qn_g, L0_xattn_kn_g, L0_xattn_Wq, L0_xattn_Wkv, L0_xattn_Wlkv, L0_xattn_Wo, L0_xattn_bo, L0_ffn_gate_w, L0_ffn_expert_w):
    import jax
    import jax.numpy as jnp

    def _L0_attn_ref(x, Wq, Wkv, Wo, bo):
        import jax, jax.numpy as jnp
        import numpy as np
        HEADS = 16
        KV_HEADS = 4
        DIM_HEAD = 64
        SCALE = DIM_HEAD ** (-0.5)

        def _rotate_half(x):
            x1, x2 = jnp.split(x, 2, axis=-1)
            return jnp.concatenate((-x2, x1), axis=-1)

        def _rope_freqs(n, d):
            inv_freq = 1.0 / 10000.0 ** (jnp.arange(0, d, 2, dtype=jnp.float32) / d)
            freqs = jnp.einsum('i,j->ij', jnp.arange(n, dtype=jnp.float32), inv_freq)
            return jnp.concatenate((freqs, freqs), axis=-1)
        b, n, dim = x.shape
        g = HEADS // KV_HEADS
        q = (x @ Wq).reshape(b, n, HEADS, DIM_HEAD).transpose(0, 2, 1, 3)
        kv = (x @ Wkv).reshape(b, n, 2 * KV_HEADS, DIM_HEAD)
        k = kv[:, :, :KV_HEADS].transpose(0, 2, 1, 3)
        v = kv[:, :, KV_HEADS:].transpose(0, 2, 1, 3)
        freqs = _rope_freqs(n, DIM_HEAD)
        cos, sin = (jnp.cos(freqs), jnp.sin(freqs))
        q = q * cos + _rotate_half(q) * sin
        k = k * cos + _rotate_half(k) * sin
        k = jnp.repeat(k, g, axis=1)
        v = jnp.repeat(v, g, axis=1)
        dots = jnp.einsum('bhid,bhjd->bhij', q, k) * SCALE
        attn = jax.nn.softmax(dots, axis=-1)
        out = jnp.einsum('bhij,bhjd->bhid', attn, v)
        out = out.transpose(0, 2, 1, 3).reshape(b, n, HEADS * DIM_HEAD)
        return out @ Wo + bo

    def _L0_xattn_ref(x, latents, mask, ln_x_g, ln_x_b, ln_l_g, ln_l_b, qn_g, kn_g, Wq, Wkv, Wlkv, Wo, bo):
        import jax, jax.numpy as jnp
        import numpy as np
        DIM_IN, DIM_LAT, DIM_HEAD = (192, 256, 64)
        INNER = max(DIM_LAT, DIM_IN)
        HEADS = INNER // DIM_HEAD
        SCALE = DIM_HEAD ** (-0.5)
        RMS_EPS = 1e-08
        LN_EPS = 1e-05

        def layernorm(x, g, b):
            mu = jnp.mean(x, axis=-1, keepdims=True)
            var = jnp.mean((x - mu) ** 2, axis=-1, keepdims=True)
            return (x - mu) * jax.lax.rsqrt(var + LN_EPS) * g + b

        def rmsnorm(x, gamma):
            norm = jnp.sqrt(jnp.sum(x * x, axis=-1, keepdims=True)) * x.shape[-1] ** (-0.5)
            return x / jnp.maximum(norm, RMS_EPS) * gamma
        b, n, _ = x.shape
        m = latents.shape[1]
        xn = layernorm(x, ln_x_g, ln_x_b)
        ln = layernorm(latents, ln_l_g, ln_l_b)
        q = ln @ Wq.T
        kv = jnp.concatenate([xn @ Wkv.T, ln @ Wlkv.T], axis=1)
        k, v = (kv[..., :INNER], kv[..., INNER:])
        split_heads = lambda t: t.reshape(t.shape[0], t.shape[1], HEADS, DIM_HEAD).transpose(0, 2, 1, 3)
        q, k, v = (split_heads(q), split_heads(k), split_heads(v))
        qn = rmsnorm(q, qn_g) * SCALE
        kn = rmsnorm(k, kn_g)
        attn = jnp.einsum('bhid,bhjd->bhij', qn, kn)
        full_mask = jnp.pad(mask, ((0, 0), (0, m)), constant_values=True)
        attn = jnp.where(full_mask[:, None, None, :], attn, -jnp.finfo(attn.dtype).max)
        attn = jax.nn.softmax(attn, axis=-1)
        out = jnp.einsum('bhij,bhjd->bhid', attn, v)
        out = out.transpose(0, 2, 1, 3).reshape(b, m, INNER)
        return out @ Wo.T + bo

    def _L0_ffn_ref(x, gate_w, expert_w):
        import jax, jax.numpy as jnp
        import numpy as np
        NUM_EXPERTS = 8
        TOP_K = 2
        N_EMBD = 256
        B, T = (4, 512)
        Bb, Tt, C = x.shape
        xf = x.reshape(Bb * Tt, C)
        logits = xf @ gate_w.T
        w, sel = jax.lax.top_k(logits, TOP_K)
        w = jax.nn.softmax(w.astype(jnp.float32), axis=1).astype(xf.dtype)
        n = xf.shape[0]
        w_full = jnp.zeros((n, NUM_EXPERTS), dtype=xf.dtype)
        w_full = w_full.at[jnp.arange(n)[:, None], sel].add(w)
        expert_out = jnp.einsum('nc,edc->ned', xf, expert_w)
        out = jnp.einsum('ne,ned->nd', w_full, expert_out)
        return out.reshape(Bb, Tt, C)
    x = _layernorm(x + _L0_attn_ref(x, L0_attn_Wq, L0_attn_Wkv, L0_attn_Wo, L0_attn_bo), axis=-1)
    x = _layernorm(x + _L0_xattn_ref(ctx_768, x, mask_BxS2_bk0, L0_xattn_ln_x_g, L0_xattn_ln_x_b, L0_xattn_ln_l_g, L0_xattn_ln_l_b, L0_xattn_qn_g, L0_xattn_kn_g, L0_xattn_Wq, L0_xattn_Wkv, L0_xattn_Wlkv, L0_xattn_Wo, L0_xattn_bo), axis=-1)
    x = _layernorm(x + _L0_ffn_ref(x, L0_ffn_gate_w, L0_ffn_expert_w), axis=-1)
    return x

_drawn_inputs = setup_inputs


def setup_inputs(seed=0):
    import zlib

    import numpy as np

    out = dict(_drawn_inputs(seed))
    spreads = {'L0_attn_bo': (0.0, 0.1),
     'L0_xattn_ln_x_g': (1.0, 0.2),
     'L0_xattn_ln_x_b': (0.0, 0.1),
     'L0_xattn_ln_l_g': (1.0, 0.2),
     'L0_xattn_ln_l_b': (0.0, 0.1),
     'L0_xattn_qn_g': (1.0, 0.2),
     'L0_xattn_kn_g': (1.0, 0.2),
     'L0_xattn_bo': (0.0, 0.1)}
    factors = {}
    for name, (base, spread) in spreads.items():
        noise = np.random.default_rng([zlib.crc32(name.encode()), seed]).standard_normal(out[name].shape)
        drawn = base * np.exp(spread * noise) if base else spread * noise
        out[name] = jnp.asarray(drawn.astype(out[name].dtype))
    for name, factor in factors.items():
        out[name] = (out[name] * factor).astype(out[name].dtype)
    return out
```

```python
from contextlib import ExitStack

import numpy as np
import concourse.bass as bass
from concourse import mybir

F32 = mybir.dt.float32
F32R = mybir.dt.float32r
U8 = mybir.dt.uint8
ALU = mybir.AluOpType
ACT = mybir.ActivationFunctionType
AX = mybir.AxisListType

P = 128
B, N, D = 8, 256, 256
NT = N // P
KC = D // P
DH = 64
HQ, HKV = 16, 4
G = HQ // HKV
HX = D // DH
NC_, DC = 77, 192
NCP = NC_ + 1
DC2 = DC - P
E = 8
SCALE = DH ** -0.5
LN_EPS = 1e-5
RMS_FLOOR = 1e-16
MASKED = 3e38
VW = DH + 1

W_COLS = dict(q=KC * HQ * DH, kv=KC * 2 * HKV * DH, o=HQ * DH // P * D,
              xq=KC * D, xl=KC * 2 * D, xo=KC * D, ex=KC * E * D, xc=2 * 2 * D, gate=KC * E)
CHUNKS_OF = {name: KC for name in W_COLS}
CHUNKS_OF["o"] = HQ * DH // P
W_AT, _at = {}, 0
for _name, _cols in W_COLS.items():
    W_AT[_name] = _at
    _at += _cols
W_ALL = _at
CHUNKS = [([("q", 0, KC), ("kv", 0, KC)], 0), ([("o", 0, 8), ("xq", 0, KC), ("xl", 0, KC), ("xo", 0, KC)], 1),
          ([("ex", 0, 1)], 0), ([("ex", 1, 2)], 1), ([("xc", 0, 2), ("gate", 0, KC)], 0)]
STAGE = (3072, 4096)

KVU = "K"
BANKS = ("PJ", "TP0", "TP1", "SM", "ST0", "ST1", "OO", "YY")
EX_BANKS = ("ST0", "ST1", "TP0", "TP1")


def banks_of(step):
    kind, args = step[0], step[1:]
    if kind in ("a_proj", "a_mrow", "b_proj", "b_cproj", "b_mrow", "b_wo", "b_gate"):
        return ("PJ",)
    if kind in ("a_turn", "b_turn"):
        return ("TP0",) if args == ("c",) else ("TP0", "TP1")
    if kind in ("a_max", "b_max", "b_maxc"):
        return ("SM",)
    if kind == "a_scores":
        return ("ST0", "ST1")
    if kind == "b_scores":
        return ("ST0", "ST1", "SM")
    if kind in ("a_pv", "b_pv"):
        return ("OO",)
    if kind in ("a_ot", "b_ot", "b_zt"):
        return ("TP0",)
    if kind in ("b_ct", "b_x2t"):
        return ("TP1",)
    if kind == "b_expert":
        return (EX_BANKS[args[0] % 4],)
    return ()


def stream_a():
    s = [("a_load",), ("a_split",), ("a_proj", KVU), ("a_proj", "V"), ("a_turn", KVU)]
    s += [("a_proj", 0), ("a_turn", 0)]
    s += [("a_max", 0, h) for h in range(G)] + [("a_proj", 1), ("a_mrow", 0)]
    for g in range(HKV):
        if g + 1 < HKV:
            s += [("a_turn", g + 1)]
        s += [("a_scores", g, 0)]
        nxt = [("a_max", g + 1, h) for h in range(G)] if g + 1 < HKV else []
        s += nxt[:2] + [("a_scores", g, 1)] + nxt[2:]
        s += [("a_pv", g, 0)]
        if g + 2 < HKV:
            s += [("a_proj", g + 2)]
        s += [("a_pv", g, 1)]
        if g + 1 < HKV:
            s += [("a_mrow", g + 1)]
        s += [("a_ot", g), ("a_wo", g)]
    return s + [("a_res",)]


def stream_b():
    s = [("b_load",), ("b_ln",), ("b_cln",), ("b_zt",), ("b_ct",),
         ("b_proj", "q"), ("b_proj", "v"), ("b_turn", "q"), ("b_proj", "k"), ("b_turn", "k"),
         ("b_cproj",), ("b_turn", "c")]
    s += [("b_maxc", p) for p in range(HX // 2)] + [("b_max", h) for h in range(HX)] + [("b_mrow",)]
    for p in range(HX // 2):
        s += [("b_scores", p), ("b_pv", p)]
    s += [("b_ot",), ("b_wo",), ("b_res",), ("b_x2t",), ("b_gate",), ("b_route",)]
    s += [("b_expert", n) for n in range(NT * E // 2)]
    return s + [("b_out",)]


def merge(a, b):
    out, done = [], 0
    for n, step in enumerate(a[:-1]):
        out.append(step)
        upto = len(b) * (n + 1) // (len(a) - 1)
        out += b[done:upto]
        done = upto
    return out + [a[-1]]


class Section:

    def __init__(self, steps, base):
        self.steps, self.base, self.per, self.turn = steps, dict(base), {k: 0 for k in BANKS}, 0
        self.order = {}
        for step in steps:
            for bank in banks_of(step):
                self.order[step, bank] = self.per[bank]
                self.per[bank] += 1

    def after(self, turns):
        return {k: self.base[k] + turns * self.per[k] for k in BANKS}

    def used(self, step, bank):
        return self.turn * self.per[bank] + (self.base[bank] + self.order[step, bank])


def build(nc, ins, out):
    ctx = ExitStack()
    with ctx:
        def sb(name, shape, dt=F32):
            return ctx.enter_context(nc.sbuf_tensor(name, shape, dt))

        def sem(name):
            return ctx.enter_context(nc.semaphore(name))

        bank = {k: ctx.enter_context(nc.psum_tensor(f"bank_{k}", [P, 512], F32)) for k in BANKS}
        full = {k: sem(f"full_{k}") for k in BANKS}
        free = {k: sem(f"free_{k}") for k in BANKS}

        w_hi, w_lo = sb("w_hi", [P, W_ALL], F32R), sb("w_lo", [P, W_ALL], F32R)
        arena = sb("arena", [P, sum(STAGE)])
        stage = [arena[:, 0:STAGE[0]], arena[:, STAGE[0]:sum(STAGE)]]
        arena_at = [0]

        def lay(*shape):
            n = int(np.prod(shape))
            t = arena[:, arena_at[0]:arena_at[0] + n]
            arena_at[0] += n
            names = "abc"[:len(shape)]
            if len(shape) == 1:
                return t
            return t.rearrange(f"p ({' '.join(names)}) -> p {' '.join(names)}",
                               **{m: w for m, w in zip(names[1:], shape[1:])})

        ident = sb("ident", [P, P])
        cos_t, sin_t = sb("cos_t", [P, NT, DH]), sb("sin_t", [P, NT, DH])
        before = sb("before", [P, E, E])
        bo, xbo = sb("bo", [P, D]), sb("xbo", [P, D])
        half_neg = sb("half_neg", [P, 8])
        ln_g, ln_b = sb("ln_g", [P, KC]), sb("ln_b", [P, KC])
        lc_g, lc_b = sb("lc_g", [P, KC]), sb("lc_b", [P, KC])
        g_q, g_k = sb("g_q", [P, 1]), sb("g_k", [P, 1])

        x_t = sb("x_t", [P, KC, N])
        x_n = sb("x_n", [P, NT, D])
        x_hi, x_lo = sb("x_hi", [P, KC, N], F32R), sb("x_lo", [P, KC, N], F32R)
        rot_c, rot_s = sb("rot_c", [P, NT, G, DH]), sb("rot_s", [P, NT, G, DH])
        rot = sb("rot", [P, NT * G, 2, DH])
        k1, k2 = sb("k1", [P, HKV, N], F32R), sb("k2", [P, HKV, N], F32R)
        t1 = [sb(f"t1_{i}", [P, G, N], F32R) for i in range(2)]
        t2 = [sb(f"t2_{i}", [P, G, N], F32R) for i in range(2)]
        val = sb("val", [P, NT, HKV, VW])
        mx = [sb(f"mx{i}", [P, NT, G]) for i in range(2)]
        mrows = sb("mrows", [DH, N], F32R)
        mrow, mrow_b = mrows[0:G, :], mrows[32:32 + HX, :]
        prob = [lay(NT, 2 * N) for i in range(2)]
        rden = sb("rden", [P, NT, 2])
        att = sb("att", [P, NT, G, DH])
        att_hi, att_lo = sb("att_hi", [P, 2, N], F32R), sb("att_lo", [P, 2, N], F32R)
        st_a, mv_a = sb("st_a", [P, NT, 6]), sb("mv_a", [P, NT, 2])
        ve_a, rs_a = sb("ve_a", [P, NT]), sb("rs_a", [P, NT])
        x1 = sb("x1", [P, NT, D])

        ctx_n = sb("ctx_n", [NC_, DC])
        m_u8, mc_u8 = sb("m_u8", [P, NC_], U8), sb("mc_u8", [NC_, 1], U8)
        m_neg, mc_neg = sb("m_neg", [P, NC_]), sb("mc_neg", [NC_, 1])
        st_b, mv_b = sb("st_b", [P, NT, 6]), sb("mv_b", [P, NT, 2])
        ve_b, rs_b = sb("ve_b", [P, NT]), sb("rs_b", [P, NT])
        z = y = lay(NT, D)
        zf = acc = lay(KC, N)
        z_hi, z_lo = sb("z_hi", [P, KC, N], F32R), sb("z_lo", [P, KC, N], F32R)
        cf = sb("cf", [P, 2, NCP])
        c_hi, c_lo = sb("c_hi", [P, 2, NCP], F32R), sb("c_lo", [P, 2, NCP], F32R)
        probx = lay(NT + 1, 2 * N)
        sq = probx[:, 0, :]
        ss, ri = sb("ss", [P, NT * HX]), sb("ri", [P, NT * HX])
        xn = lay(NT * HX, 2, DH)
        attx = xn.rearrange("p h two d -> p (h two d)")[:, 0:NT * HX * DH].rearrange(
            "p (t h d) -> p t h d", t=NT, h=HX)
        t1x, t2x = sb("t1x", [P, HX, N], F32R), sb("t2x", [P, HX, N], F32R)
        k1x, k2x = sb("k1x", [P, HX, N + NCP], F32R), sb("k2x", [P, HX, N + NCP], F32R)
        valx = lay(NT + 1, HX, VW)
        mx_l, mx_c, mx_b = sb("mx_l", [P, NT, HX]), sb("mx_c", [P, NT, HX]), sb("mx_b", [P, NT, HX])
        sc_c = lay(2, NT, NC_)
        rden_b = sb("rden_b", [P, NT, 2])
        attx_hi, attx_lo = z_hi, z_lo
        x2, x2_hi, x2_lo = x1, z_hi, z_lo
        lg = sb("lg", [P, NT, E])
        gt, eq = lay(NT, E * E).rearrange("p t (e f) -> p t e f", e=E), sb("eq", [P, NT, E, E])
        rank, sel0, sel1 = sb("rank", [P, NT, E]), sb("sel0", [P, NT, E]), sb("sel1", [P, NT, E])
        top = sb("top", [P, 6, NT])
        gate = sb("gate", [P, NT, E])

        w_in = [sem(f"w_in{i}") for i in range(2)]
        c_in = sem("c_in")
        w_hi_done, w_lo_done = sem("w_hi_done"), sem("w_lo_done")
        fill_done, const_done = sem("fill_done"), sem("const_done")
        xt_in, xn_in = sem("xt_in"), sem("xn_in")
        x_hi_done, x_lo_done = sem("x_hi_done"), sem("x_lo_done")
        rp_done = sem("rp_done")
        rot_done = sem("rot_done")
        t1_done = sem("t1_done")
        v_done = sem("v_done")
        mx_done = sem("mx_done")
        mr_done = sem("mr_done")
        mr_in = [sem(f"mr_in{i}") for i in range(2)]
        p_done = sem("p_done")
        o_done = sem("o_done")
        oh_done = sem("oh_done")
        wo_done = sem("wo_done")
        ya_free = sem("ya_free")
        va_done, ra_done = sem("va_done"), sem("ra_done")
        x1_done = sem("x1_done")
        dve_a = sem("dve_a")
        cx_in = sem("cx_in")
        vb_done, rb_done = sem("vb_done"), sem("rb_done")
        z_done = sem("z_done")
        zf_done = sem("zf_done")
        zh_done, zl_done = sem("zh_done"), sem("zl_done")
        sq_done = sem("sq_done")
        vx_done = sem("vx_done")
        xn_done = sem("xn_done")
        tx_done = sem("tx_done")
        mb_done = sem("mb_done")
        mrb_done = sem("mrb_done")
        mrb_in = sem("mrb_in")
        px_done, ox_done = sem("px_done"), sem("ox_done")
        ohx_done = sem("ohx_done")
        x2_done = sem("x2_done")
        x2h_done = sem("x2h_done")
        dif_done, exp_done = sem("dif_done"), sem("exp_done")
        y_done, y_out = sem("y_done"), sem("y_out")
        dve_b = sem("dve_b")

        A_LINKS, B_LINKS = 11, 49
        B_NORMS = 7

        none = {k: 0 for k in BANKS}
        first = Section(stream_a(), none)
        second = Section(merge(stream_a(), stream_b()), first.after(1))
        steady = Section(second.steps, second.after(1))
        last = Section(stream_b(), steady.after(B - 2))

        def walk(eng, steps_of):
            def run(sec, a, b):
                steps = steps_of(sec, a, b)
                for step in sec.steps:
                    if step[0] in steps:
                        steps[step[0]](*step[1:])

            run(first, 0, None)
            run(second, 1, 0)
            with eng.Fori(0, B - 2) as i:
                steady.turn = i
                run(steady, i + 2, i + 1)
            run(last, None, B - 1)

        def wait(eng, s, value):
            if not isinstance(value, int) or value > 0:
                eng.wait_ge(s, value)

        def weights(t, name, chunk, c0, c1):
            per = W_COLS[name] // CHUNKS_OF[name]
            at = W_AT[name] + chunk * per
            return t[:, at + c0:at + c1]

        def chunk(n):
            parts, st = CHUNKS[n]
            name, k0, _ = parts[0]
            at = W_AT[name] + k0 * (W_COLS[name] // CHUNKS_OF[name])
            cols = sum(W_COLS[m] // CHUNKS_OF[m] * (k1_ - k0_) for m, k0_, k1_ in parts)
            loads = sum(1 + (m == "xc") for c in CHUNKS[:n + 1] if c[1] == st for m, _, _ in c[0])
            return at, cols, st, 16 * loads

        def is_head(t, h):
            return t[:, :].rearrange("p (h n) -> p h n", h=2)[:, h, :]

        block = ctx.enter_context(nc.Block())

        @block.sync
        def _(sp):
            def load_weights(n):
                parts, st = CHUNKS[n]
                if n >= 2:
                    sp.wait_ge(w_lo_done, n - 1)
                at = 0
                for name, k0, k1_ in parts:
                    cols = W_COLS[name] // CHUNKS_OF[name] * (k1_ - k0)
                    src, dst = ins[name], stage[st][:, at:at + cols]
                    if name == "xc":
                        sp.dma_start(dst[:, 0:2 * D], src[0:P, :]).then_inc(w_in[st], 16)
                        src, dst = src[P:DC, :], dst[0:DC2, 2 * D:4 * D]
                        sp.dma_start(dst, src).then_inc(w_in[st], 16)
                    else:
                        sp.dma_start(dst.rearrange("p (k n) -> p k n", k=k1_ - k0),
                                     src.rearrange("(k p) n -> p k n", p=P)[:, k0:k1_, :]).then_inc(w_in[st], 16)
                    at += cols

            load_weights(0)
            load_weights(1)
            for dst, src in ((cos_t[:], ins["cos"].rearrange("(t p) d -> p t d", p=P)),
                             (sin_t[:], ins["sin"].rearrange("(t p) d -> p t d", p=P)),
                             (ident[:], ins["ident"]), (before[:], ins["before"].partition_broadcast(P)),
                             (bo[:], ins["bo"].partition_broadcast(P)),
                             (xbo[:], ins["xbo"].partition_broadcast(P)),
                             (ln_g[:], ins["ln_g"]), (ln_b[:], ins["ln_b"]),
                             (lc_g[:, 0:1], ins["lc_g"][0:P, :]), (lc_g[0:DC2, 1:2], ins["lc_g"][P:DC, :]),
                             (lc_b[:, 0:1], ins["lc_b"][0:P, :]), (lc_b[0:DC2, 1:2], ins["lc_b"][P:DC, :]),
                             (g_q[0:DH, :], ins["g_q"]), (g_q[DH:P, :], ins["g_q"]),
                             (g_k[0:DH, :], ins["g_k"]), (g_k[DH:P, :], ins["g_k"])):
                sp.dma_start(dst, src).then_inc(c_in, 16)
            for n in range(2, len(CHUNKS)):
                load_weights(n)

            def steps_of(sec, a, b):
                def a_load():
                    wait(sp, x_lo_done, a)
                    sp.nop(nofuse=True)
                    sp.dma_start(x_t[:], ins["x_t"][a].rearrange("(k p) n -> p k n", p=P)).then_inc(xt_in, 16)
                    wait(sp, x1_done, a)
                    sp.nop(nofuse=True)
                    sp.dma_start(x_n[:], ins["x"][a].rearrange("(t p) c -> p t c", p=P)).then_inc(xn_in, 16)

                def a_mrow(g):
                    sp.wait_ge(mr_done, a * 4 + g + 1)
                    sp.nop(nofuse=True)
                    sp.dma_start(t2[g % 2][DH:DH + 1, :, :].bitcast(F32), mrow[:, :].bitcast(F32)).then_inc(mr_in[g % 2], 16)

                def b_load():
                    wait(sp, xn_done, b * 3)
                    sp.nop(nofuse=True)
                    wait(sp, px_done, b * 2)
                    sp.nop(nofuse=True)
                    sp.dma_start(ctx_n[:], ins["ctx"][b]).then_inc(cx_in, 16)
                    sp.dma_start(m_u8[:], ins["mask"][b].partition_broadcast(P)).then_inc(cx_in, 16)
                    sp.dma_start(mc_u8[:], ins["mask"][b].rearrange("(n o) -> n o", o=1)).then_inc(cx_in, 16)

                def b_mrow():
                    sp.wait_ge(mrb_done, b + 1)
                    sp.nop(nofuse=True)
                    sp.dma_start(t2x[DH:DH + 1, :, :].bitcast(F32), mrow_b[:, :].bitcast(F32)).then_inc(mrb_in, 16)

                def b_out():
                    sp.wait_ge(y_done, b + 1)
                    sp.nop(nofuse=True)
                    sp.dma_start(out[b].rearrange("(t p) c -> p t c", p=P), y[:]).then_inc(y_out, 16)

                return dict(a_load=a_load, a_mrow=a_mrow, b_load=b_load, b_mrow=b_mrow, b_out=b_out)

            walk(sp, steps_of)
            sp.wait_ge(y_out, 16 * B)

        @block.tensor
        def _(pe):
            mm = nc.tensor.matmul

            def split_product(o, l_hi, l_lo, r_hi, r_lo, start, stop):
                mm(o, l_hi, r_hi, start=start, stop=False)
                mm(o, l_hi, r_lo, start=False, stop=False)
                return mm(o, l_lo, r_hi, start=False, stop=stop)

            def project(o, l_hi, l_lo, name, c0, c1):
                for it in range(NT):
                    rows = slice(it * P, (it + 1) * P)
                    for k in range(KC):
                        ins_ = split_product(o[:, it * D:(it + 1) * D], l_hi[:, k, rows], l_lo[:, k, rows],
                                             weights(w_hi, name, k, c0, c1), weights(w_lo, name, k, c0, c1),
                                             k == 0, k == KC - 1)
                return ins_

            pe.wait_ge(w_lo_done, len(CHUNKS))
            pe.wait_ge(c_in, 16 * 16)
            pe.wait_ge(const_done, 2)

            def steps_of(sec, a, b):
                def take(step, k):
                    wait(pe, free[k], sec.used(step, k))
                    return bank[k]

                def a_proj(u):
                    pe.wait_ge(x_lo_done, a + 1)
                    o = take(("a_proj", u), "PJ")
                    name, c0 = ("kv", {KVU: 0, "V": HKV * DH}[u]) if u in (KVU, "V") else ("q", u * G * DH)
                    project(o, x_hi, x_lo, name, c0, c0 + G * DH).then_inc(full["PJ"], 1)

                def a_turn(u):
                    n = 0 if u == KVU else u + 1
                    pe.wait_ge(rot_done, a * 5 + n + 1)
                    for half in range(2):
                        k = f"TP{half}"
                        o = take(("a_turn", u), k)
                        for h in range(2):
                            for it in range(NT):
                                src = rot[:, it * G + half * 2 + h, :, :]
                                ins_ = nc.tensor.transpose(is_head(o, h)[:, it * P:(it + 1) * P], src, ident[:])
                        ins_.then_inc(full[k], 1)

                def a_max(g, h):
                    pe.wait_ge(t1_done, a * 10 + 2 * g + 4)
                    pe.wait_ge(free["TP1"], sec.used(("a_turn", KVU), "TP1") + 1)
                    o = take(("a_max", g, h), "SM")
                    for it in range(NT):
                        ins_ = mm(o[:, it * N:(it + 1) * N], t1[g % 2][:, h, it * P:(it + 1) * P],
                                  k1[:, g, :], start=True, stop=True)
                    ins_.then_inc(full["SM"], 1)

                def a_mrow(g):
                    pe.wait_ge(mx_done, a * 16 + G * g + G)
                    o = take(("a_mrow", g), "PJ")
                    for it in range(NT):
                        ins_ = nc.tensor.transpose(o[0:G, it * P:(it + 1) * P], mx[g % 2][:, it, :], ident[:])
                    ins_.then_inc(full["PJ"], 1)

                def a_scores(g, p):
                    pe.wait_ge(free["TP1"], sec.used(("a_turn", g), "TP1") + 1)
                    pe.wait_ge(mr_in[g % 2], (a * 2 + (g // 2 + 1)) * 16)
                    for jt in range(NT):
                        k = f"ST{jt}"
                        o = take(("a_scores", g, p), k)
                        rows = slice(jt * P, (jt + 1) * P)
                        mm(o[:, :], k1[:, g, rows], t1[g % 2][:, 2 * p:2 * p + 2, :], start=True, stop=False)
                        mm(o[:, :], k2[:, g, rows], t2[g % 2][:, 2 * p:2 * p + 2, :], start=False,
                           stop=True).then_inc(full[k], 1)

                def a_pv(g, p):
                    pe.wait_ge(p_done, a * 8 + 2 * g + p + 1)
                    pe.wait_ge(v_done, a + 1)
                    o = take(("a_pv", g, p), "OO")
                    for it in range(NT):
                        for h in range(2):
                            c = (it * 2 + h) * VW
                            for jt in range(NT):
                                ins_ = mm(o[:, c:c + VW], prob[p][:, jt, h * N + it * P:h * N + (it + 1) * P],
                                          val[:, jt, g, :], start=(jt == 0), stop=(jt == NT - 1))
                    ins_.then_inc(full["OO"], 1)

                def a_ot(g):
                    pe.wait_ge(o_done, a * 8 + 2 * g + 2)
                    o = take(("a_ot", g), "TP0")
                    for p in range(2):
                        for it in range(NT):
                            ins_ = nc.tensor.transpose(is_head(o, p)[:, it * P:(it + 1) * P],
                                                       att[:, it, 2 * p:2 * p + 2, :], ident[:])
                    ins_.then_inc(full["TP0"], 1)

                def a_wo(g):
                    if g == 0:
                        wait(pe, ya_free, a)
                    pe.wait_ge(oh_done, a * 4 + g + 1)
                    pe.wait_ge(free["TP0"], sec.used(("a_ot", g), "TP0") + 1)
                    for it in range(NT):
                        rows = slice(it * P, (it + 1) * P)
                        for p in range(2):
                            o = bank["YY"][:, it * D:(it + 1) * D]
                            r_hi, r_lo = (weights(w, "o", 2 * g + p, 0, D) for w in (w_hi, w_lo))
                            l_hi, l_lo = att_hi[:, p, rows], att_lo[:, p, rows]
                            mm(o, l_hi, r_hi, start=(g == 0 and it == 0 and p == 0), stop=False, skip_group_check=True)
                            mm(o, l_hi, r_lo, start=False, stop=False, skip_group_check=True)
                            ins_ = mm(o, l_lo, r_hi, start=False, stop=(g == HKV - 1 and p == 1), skip_group_check=True)
                    ins_.then_inc(wo_done, 1)

                def b_zt():
                    pe.wait_ge(z_done, b * 2 + 1)
                    o = take(("b_zt",), "TP0")
                    for k in range(KC):
                        for it in range(NT):
                            ins_ = nc.tensor.transpose(is_head(o, k)[:, it * P:(it + 1) * P],
                                                       z[:, it, k * P:(k + 1) * P], ident[:])
                    ins_.then_inc(full["TP0"], 1)

                def b_ct():
                    pe.wait_ge(z_done, b * 2 + 2)
                    o = take(("b_ct",), "TP1")
                    nc.tensor.transpose(o[:, 0:NC_], ctx_n[:, 0:P], ident[0:NC_, 0:NC_])
                    nc.tensor.transpose(o[0:DC2, P:P + NC_], ctx_n[:, P:DC],
                                        ident[0:NC_, 0:NC_]).then_inc(full["TP1"], 1)

                def b_proj(u):
                    pe.wait_ge(zl_done, b * 2 + 1)
                    o = take(("b_proj", u), "PJ")
                    name, c0 = {"q": ("xq", 0), "k": ("xl", 0), "v": ("xl", D)}[u]
                    project(o, z_hi, z_lo, name, c0, c0 + D).then_inc(full["PJ"], 1)

                def b_cproj():
                    pe.wait_ge(zl_done, b * 2 + 2)
                    o = take(("b_cproj",), "PJ")
                    for k, rows in ((0, P), (1, DC2)):
                        ins_ = split_product(o[0:NC_, :], c_hi[0:rows, k, 0:NC_], c_lo[0:rows, k, 0:NC_],
                                             weights(w_hi, "xc", k, 0, 2 * D)[0:rows], weights(w_lo, "xc", k, 0, 2 * D)[0:rows],
                                             k == 0, k == 1)
                    ins_.then_inc(full["PJ"], 1)

                def b_turn(u):
                    pe.wait_ge(xn_done, b * 3 + {"q": 1, "k": 2, "c": 3}[u])
                    if u == "c":
                        o = take(("b_turn", u), "TP0")
                        for h in range(HX):
                            src = xn[0:NC_, h, :, :]
                            ins_ = nc.tensor.transpose(o[:, h * NCP:h * NCP + NC_], src, ident[0:NC_, 0:NC_])
                        ins_.then_inc(full["TP0"], 1)
                        return
                    for half in range(2):
                        k = f"TP{half}"
                        o = take(("b_turn", u), k)
                        for h in range(2):
                            for it in range(NT):
                                src = xn[:, it * HX + half * 2 + h, :, :]
                                ins_ = nc.tensor.transpose(is_head(o, h)[:, it * P:(it + 1) * P], src, ident[:])
                        ins_.then_inc(full[k], 1)

                def b_max(h):
                    pe.wait_ge(free["TP0"], sec.used(("b_turn", "c"), "TP0") + 1)
                    pe.wait_ge(free["TP1"], sec.used(("b_turn", "k"), "TP1") + 1)
                    o = take(("b_max", h), "SM")
                    for it in range(NT):
                        ins_ = mm(o[:, it * N:(it + 1) * N], t1x[:, h, it * P:(it + 1) * P],
                                  k1x[:, h, 0:N], start=True, stop=True)
                    ins_.then_inc(full["SM"], 1)

                def b_maxc(p):
                    pe.wait_ge(free["TP0"], sec.used(("b_turn", "c"), "TP0") + 1)
                    pe.wait_ge(free["TP1"], sec.used(("b_turn", "k"), "TP1") + 1)
                    o = take(("b_maxc", p), "SM")
                    for h in range(2):
                        for it in range(NT):
                            c = (h * NT + it) * NCP
                            ins_ = mm(o[:, c:c + NCP], t1x[:, 2 * p + h, it * P:(it + 1) * P],
                                      k1x[:, 2 * p + h, N:N + NCP], start=True, stop=True)
                    ins_.then_inc(full["SM"], 1)

                def b_mrow():
                    pe.wait_ge(mb_done, b + 1)
                    o = take(("b_mrow",), "PJ")
                    for it in range(NT):
                        ins_ = nc.tensor.transpose(o[0:HX, it * P:(it + 1) * P], mx_b[:, it, :], ident[:])
                    ins_.then_inc(full["PJ"], 1)

                def b_scores(p):
                    pe.wait_ge(mrb_in, (b + 1) * 16)
                    for jt, k in enumerate(("ST0", "ST1", "SM")):
                        o = take(("b_scores", p), k)
                        m = P if jt < NT else NC_
                        for h in range(2):
                            keys = slice(jt * P, jt * P + m)
                            dst = o[0:m, h * N:(h + 1) * N]
                            mm(dst, k1x[:, 2 * p + h, keys], t1x[:, 2 * p + h, :], start=True, stop=False)
                            ins_ = mm(dst, k2x[:, 2 * p + h, keys], t2x[:, 2 * p + h, :], start=False, stop=True)
                        ins_.then_inc(full[k], 1)

                def b_pv(p):
                    pe.wait_ge(px_done, b * 2 + p + 1)
                    pe.wait_ge(vx_done, b + 1)
                    o = take(("b_pv", p), "OO")
                    for it in range(NT):
                        for h in range(2):
                            c = (it * 2 + h) * VW
                            for jt in range(NT + 1):
                                m = P if jt < NT else NC_
                                ins_ = mm(o[:, c:c + VW], probx[0:m, jt, h * N + it * P:h * N + (it + 1) * P],
                                          valx[0:m, jt, 2 * p + h, :], start=(jt == 0), stop=(jt == NT))
                    ins_.then_inc(full["OO"], 1)

                def b_ot():
                    pe.wait_ge(ox_done, b * 2 + 2)
                    o = take(("b_ot",), "TP0")
                    for k in range(KC):
                        for it in range(NT):
                            ins_ = nc.tensor.transpose(is_head(o, k)[:, it * P:(it + 1) * P],
                                                       attx[:, it, 2 * k:2 * k + 2, :], ident[:])
                    ins_.then_inc(full["TP0"], 1)

                def b_wo():
                    pe.wait_ge(free["TP0"], sec.used(("b_ot",), "TP0") + 1)
                    o = take(("b_wo",), "PJ")
                    project(o, attx_hi, attx_lo, "xo", 0, D).then_inc(full["PJ"], 1)

                def b_x2t():
                    pe.wait_ge(x2_done, b + 1)
                    o = take(("b_x2t",), "TP1")
                    for k in range(KC):
                        for it in range(NT):
                            ins_ = nc.tensor.transpose(is_head(o, k)[:, it * P:(it + 1) * P],
                                                       x2[:, it, k * P:(k + 1) * P], ident[:])
                    ins_.then_inc(full["TP1"], 1)

                def b_gate():
                    pe.wait_ge(free["TP1"], sec.used(("b_x2t",), "TP1") + 1)
                    o = take(("b_gate",), "PJ")
                    for it in range(NT):
                        rows = slice(it * P, (it + 1) * P)
                        for k in range(KC):
                            ins_ = split_product(o[:, it * E:(it + 1) * E], x2_hi[:, k, rows], x2_lo[:, k, rows],
                                                 weights(w_hi, "gate", k, 0, E), weights(w_lo, "gate", k, 0, E),
                                                 k == 0, k == KC - 1)
                    ins_.then_inc(full["PJ"], 1)

                def b_expert(n):
                    it, e2 = n // (E // 2), n % (E // 2)
                    k_ = EX_BANKS[n % 4]
                    o = take(("b_expert", n), k_)
                    rows = slice(it * P, (it + 1) * P)
                    for k in range(KC):
                        ins_ = split_product(o[:, :], x2_hi[:, k, rows], x2_lo[:, k, rows],
                                             weights(w_hi, "ex", k, e2 * 2 * D, (e2 + 1) * 2 * D),
                                             weights(w_lo, "ex", k, e2 * 2 * D, (e2 + 1) * 2 * D),
                                             k == 0, k == KC - 1)
                    ins_.then_inc(full[k_], 1)

                return dict(a_proj=a_proj, a_turn=a_turn, a_max=a_max, a_mrow=a_mrow, a_scores=a_scores,
                            a_pv=a_pv, a_ot=a_ot, a_wo=a_wo, b_zt=b_zt, b_ct=b_ct, b_proj=b_proj,
                            b_cproj=b_cproj, b_turn=b_turn, b_max=b_max, b_maxc=b_maxc, b_mrow=b_mrow,
                            b_scores=b_scores, b_pv=b_pv, b_ot=b_ot, b_wo=b_wo, b_x2t=b_x2t,
                            b_gate=b_gate, b_expert=b_expert)

            walk(pe, steps_of)

        @block.scalar
        def _(act):
            run = nc.scalar.activation
            for n in range(len(CHUNKS)):
                at, cols, st, count = chunk(n)
                act.wait_ge(w_in[st], count)
                if n == len(CHUNKS) - 1:
                    act.wait_ge(const_done, 1)
                run(w_hi[:, at:at + cols], stage[st][:, 0:cols], ACT.Copy).then_inc(w_hi_done, 1)
            act.wait_ge(c_in, 16 * 16)

            def steps_of(sec, a, b):
                def filled(step, k):
                    act.wait_ge(full[k], sec.used(step, k) + 1)
                    return bank[k]

                def a_split():
                    act.wait_ge(xt_in, (a + 1) * 16)
                    wait(act, rp_done, a * 5)
                    wait(act, v_done, a)
                    run(x_hi[:], x_t[:], ACT.Copy).then_inc(x_hi_done, 1)

                def a_proj(u):
                    if u != "V":
                        return
                    wait(act, o_done, a * 8)
                    o = filled(("a_proj", u), "PJ")
                    run(val[:, :, :, 0:DH], o[:, :].rearrange("p (t h d) -> p t h d", t=NT, h=HKV),
                        ACT.Copy).then_inc(v_done, 1)
                    act.wait_ge(v_done, a + 1)
                    act.sem_inc(free["PJ"], 1)

                def a_turn(u):
                    if u == KVU:
                        wait(act, p_done, a * 8)
                    else:
                        wait(act, p_done, a * 8 + 2 * u - 2)
                    for half in range(2):
                        o = filled(("a_turn", u), f"TP{half}")
                        heads = slice(2 * half, 2 * half + 2)
                        if u == KVU:
                            run(k2[0:DH, heads, :], o[0:DH, :].rearrange("p (h n) -> p h n", h=2), ACT.Copy)
                            run(k1[:, heads, :], o[:, :].rearrange("p (h n) -> p h n", h=2),
                                ACT.Copy).then_inc(t1_done, 1)
                        else:
                            run(t1[u % 2][:, heads, :], o[:, :].rearrange("p (h n) -> p h n", h=2),
                                ACT.Copy).then_inc(t1_done, 1)

                def a_mrow(g):
                    o = filled(("a_mrow", g), "PJ")
                    wait(act, mr_in[(g - 1) % 2], (a * 2 + (g + 1) // 2) * 16)
                    run(mrow[:, :], o[0:G, 0:N], ACT.Copy, scale=-1.0).then_inc(mr_done, 1)
                    act.wait_ge(mr_done, a * 4 + g + 1)
                    act.sem_inc(free["PJ"], 1)

                def a_scores(g, p):
                    wait(act, o_done, a * 8 + 2 * g + p - 1)
                    for jt in range(NT):
                        o = filled(("a_scores", g, p), f"ST{jt}")
                        run(prob[p][:, jt, :], o[:, :], ACT.Exp, scale=SCALE).then_inc(free[f"ST{jt}"], 1)
                    act.wait_ge(free["ST1"], sec.used(("a_scores", g, p), "ST1") + 1)
                    act.sem_inc(p_done, 1)

                def a_ot(g):
                    o = filled(("a_ot", g), "TP0")
                    wait(act, wo_done, a * 4 + g)
                    run(att_hi[:], o[:, :].rearrange("p (h n) -> p h n", h=2),
                        ACT.Copy).then_inc(oh_done, 1)

                def b_zt():
                    o = filled(("b_zt",), "TP0")
                    wait(act, zl_done, b * 2)
                    for k in range(KC):
                        ins_ = run(zf[:, k, :], is_head(o, k), ACT.Identity, bias=ln_b[:, k:k + 1],
                                   scale=ln_g[:, k:k + 1])
                    ins_.then_inc(zf_done, 1)
                    act.wait_ge(zf_done, b * 2 + 1)
                    act.sem_inc(free["TP0"], 1)
                    wait(act, y_done, b)
                    run(z_hi[:], zf[:], ACT.Copy).then_inc(zh_done, 1)

                def b_ct():
                    o = filled(("b_ct",), "TP1")
                    run(cf[:, 0, 0:NC_], o[:, 0:NC_], ACT.Identity, bias=lc_b[:, 0:1], scale=lc_g[:, 0:1])
                    run(cf[0:DC2, 1, 0:NC_], o[0:DC2, P:P + NC_], ACT.Identity, bias=lc_b[0:DC2, 1:2],
                        scale=lc_g[0:DC2, 1:2]).then_inc(zf_done, 1)
                    act.wait_ge(zf_done, b * 2 + 2)
                    act.sem_inc(free["TP1"], 1)
                    run(c_hi[:, 0, 0:NC_], cf[:, 0, 0:NC_], ACT.Copy)
                    run(c_hi[0:DC2, 1, 0:NC_], cf[0:DC2, 1, 0:NC_], ACT.Copy).then_inc(zh_done, 1)

                def b_proj(u):
                    o = filled(("b_proj", u), "PJ")
                    if u == "v":
                        wait(act, ox_done, b * 2)
                        run(valx[:, 0:NT, :, 0:DH], o[:, :].rearrange("p (t h d) -> p t h d", t=NT, h=HX),
                            ACT.Copy).then_inc(vx_done, 1)
                        act.wait_ge(vx_done, b + 1)
                        act.sem_inc(free["PJ"], 1)
                    else:
                        wait(act, vb_done, b * B_NORMS + {"q": 2, "k": 3}[u])
                        wait(act, ox_done, b * 2)
                        run(sq[:], o[:, :], ACT.Square).then_inc(sq_done, 1)

                def b_cproj():
                    o = filled(("b_cproj",), "PJ")
                    act.wait_ge(vb_done, b * B_NORMS + 4)
                    wait(act, ox_done, b * 2)
                    run(valx[0:NC_, NT, :, 0:DH], o[0:NC_, D:2 * D].rearrange("p (h d) -> p h d", h=HX), ACT.Copy)
                    run(sq[0:NC_, 0:D], o[0:NC_, 0:D], ACT.Square).then_inc(sq_done, 1)

                def b_turn(u):
                    wait(act, px_done, b * 2)
                    for half in range(1 if u == "c" else 2):
                        o = filled(("b_turn", u), f"TP{half}")
                        heads = slice(2 * half, 2 * half + 2)
                        if u == "c":
                            src = o[:, 0:HX * NCP].rearrange("p (h n) -> p h n", h=HX)[:, :, 0:NC_]
                            heads, keys = slice(0, HX), slice(N, N + NC_)
                        else:
                            src, keys = o[:, :].rearrange("p (h n) -> p h n", h=2), slice(0, N)
                        if u == "q":
                            run(t1x[:, heads, :], src, ACT.Copy, scale=g_q[:, 0:1]).then_inc(tx_done, 1)
                        else:
                            run(k2x[0:DH, heads, keys], src[0:DH], ACT.Copy, scale=g_k[0:DH, 0:1])
                            run(k1x[:, heads, keys], src, ACT.Copy, scale=g_k[:, 0:1]).then_inc(tx_done, 1)

                def b_mrow():
                    o = filled(("b_mrow",), "PJ")
                    run(mrow_b[:, :], o[0:HX, 0:N], ACT.Copy, scale=-1.0).then_inc(mrb_done, 1)
                    act.wait_ge(mrb_done, b + 1)
                    act.sem_inc(free["PJ"], 1)

                def b_scores(p):
                    wait(act, ox_done, b * 2 + p)
                    for jt, k in enumerate(("ST0", "ST1", "SM")):
                        o = filled(("b_scores", p), k)
                        if jt < NT:
                            run(probx[:, jt, :], o[:, :], ACT.Exp, scale=SCALE).then_inc(free[k], 1)
                        else:
                            run(probx[0:NC_, jt, :], o[0:NC_, :], ACT.Exp, bias=mc_neg[:, 0:1],
                                scale=SCALE).then_inc(free[k], 1)
                    act.wait_ge(free["SM"], sec.used(("b_scores", p), "SM") + 1)
                    act.sem_inc(px_done, 1)

                def b_ot():
                    o = filled(("b_ot",), "TP0")
                    run(attx_hi[:], o[:, :].rearrange("p (h n) -> p h n", h=2), ACT.Copy).then_inc(ohx_done, 1)

                def b_x2t():
                    o = filled(("b_x2t",), "TP1")
                    run(x2_hi[:], o[:, :].rearrange("p (h n) -> p h n", h=2), ACT.Copy).then_inc(x2h_done, 1)

                def b_route():
                    act.wait_ge(dif_done, b + 1)
                    run(top[:, 3, :], top[:, 2, :], ACT.Exp).then_inc(exp_done, 1)

                return dict(a_split=a_split, a_proj=a_proj, a_turn=a_turn, a_mrow=a_mrow, a_scores=a_scores,
                            a_ot=a_ot, b_zt=b_zt, b_ct=b_ct, b_proj=b_proj, b_cproj=b_cproj, b_turn=b_turn,
                            b_mrow=b_mrow, b_scores=b_scores, b_ot=b_ot, b_x2t=b_x2t, b_route=b_route)

            walk(act, steps_of)

        @block.gpsimd
        def _(pool):
            tt = nc.gpsimd.tensor_tensor
            fixed = [(half_neg[:], -0.5)]
            fixed += [(t[DH:P].bitcast(F32), 0.0) for t in (k2, t2[0], t2[1], k2x, t2x)]
            fixed += [(k1x[:, :, N + NC_:N + NCP].bitcast(F32), 0.0), (val[:, :, :, DH:VW], 1.0)]
            fixed += [(t[DH:DH + 1].bitcast(F32), 1.0) for t in (k2, k2x)]
            for n, (t, value) in enumerate(fixed):
                nc.gpsimd.memset(t, value).then_inc(fill_done, 1)
                pool.wait_ge(fill_done, n + 1)
            pool.wait_ge(w_lo_done, 3)
            nc.gpsimd.memset(stage[0][DC2:P, 2 * D:4 * D], 0.0).then_inc(const_done, 1)
            pool.wait_ge(w_lo_done, len(CHUNKS))
            nc.gpsimd.memset(valx[:, :, :, DH:VW], 1.0).then_inc(const_done, 1)
            pool.wait_ge(const_done, 2)

            def steps_of(sec, a, b):
                def a_turn(u):
                    n = 0 if u == KVU else u + 1
                    pool.wait_ge(rp_done, a * 5 + n + 1)
                    wait(pool, t1_done, a * 10 + 2 * n)
                    for twice in range(2):
                        ins_ = tt(rot[:, :, twice, :], rot_c[:].rearrange("p t h d -> p (t h) d"),
                                  rot_s[:].rearrange("p t h d -> p (t h) d"), ALU.add)
                    ins_.then_inc(rot_done, 1)

                def power(n, rows, src, dst, cols, done_in, done_out, count):
                    pool.wait_ge(done_in, count)
                    tt(dst[0:rows, 0:cols], src[0:rows, 0:cols], half_neg[0:rows, 0:cols],
                       ALU.pow).then_inc(done_out, 1)

                def a_res():
                    power(0, P, ve_a, rs_a, NT, va_done, ra_done, a + 1)

                def b_norm(n, rows, src, dst, cols):
                    power(n, rows, src, dst, cols, vb_done, rb_done, b * B_NORMS + n + 1)

                def b_ln():
                    b_norm(0, P, ve_b, rs_b, NT)

                def b_cln():
                    b_norm(1, NC_, ve_b, rs_b, 1)

                def b_proj(u):
                    if u != "v":
                        b_norm({"q": 2, "k": 3}[u], P, ss, ri, NT * HX)

                def b_cproj():
                    b_norm(4, NC_, ss, ri, HX)

                def b_res():
                    b_norm(5, P, ve_b, rs_b, NT)

                def b_out():
                    b_norm(6, P, ve_b, rs_b, NT)

                def b_zt():
                    pool.wait_ge(zh_done, b * 2 + 1)
                    tt(z_lo[:], zf[:], z_hi[:], ALU.subtract).then_inc(zl_done, 1)

                def b_ct():
                    pool.wait_ge(zh_done, b * 2 + 2)
                    tt(c_lo[:, 0, 0:NC_], cf[:, 0, 0:NC_], c_hi[:, 0, 0:NC_], ALU.subtract)
                    tt(c_lo[0:DC2, 1, 0:NC_], cf[0:DC2, 1, 0:NC_], c_hi[0:DC2, 1, 0:NC_],
                       ALU.subtract).then_inc(zl_done, 1)

                return dict(a_turn=a_turn, a_res=a_res, b_ln=b_ln, b_cln=b_cln, b_proj=b_proj,
                            b_cproj=b_cproj, b_res=b_res, b_zt=b_zt, b_ct=b_ct, b_out=b_out)

            walk(pool, steps_of)

        @block.vector
        def _(dve):
            v = nc.vector
            for n in range(len(CHUNKS)):
                at, cols, st, _ = chunk(n)
                dve.wait_ge(w_hi_done, n + 1)
                v.tensor_tensor(w_lo[:, at:at + cols], stage[st][:, 0:cols], w_hi[:, at:at + cols],
                                ALU.subtract).then_inc(w_lo_done, 1)
            dve.wait_ge(c_in, 16 * 16)

            def steps_of(sec, a, b):
                count = {"a": 0, "b": 0}

                def link(ins_, s):
                    count[s] += 1
                    chain, at = (dve_a, a * A_LINKS) if s == "a" else (dve_b, b * B_LINKS)
                    ins_.then_inc(chain, 1)
                    dve.wait_ge(chain, at + count[s])

                def filled(step, k):
                    dve.wait_ge(full[k], sec.used(step, k) + 1)
                    return bank[k]

                def stats(s, src, rows, tiles, st, mv, ve):
                    for t in range(tiles):
                        ins_ = v.bn_stats(st[0:rows, t, :], src[t])
                    link(ins_, s)
                    dve.nop(nofuse=True)
                    for t in range(tiles):
                        ins_ = v.bn_aggr(mv[0:rows, t, :], st[0:rows, t, :])
                    link(ins_, s)
                    return v.tensor_scalar(ve[0:rows, 0:tiles], mv[0:rows, 0:tiles, 1], LN_EPS, None, ALU.add)

                def normed(dst, src, rows, tiles, mv, rs):
                    for t in range(tiles):
                        ins_ = v.tensor_scalar(dst[t], src[t], mv[0:rows, t, 0:1], rs[0:rows, t:t + 1],
                                               ALU.subtract, ALU.mult)
                    return ins_

                def tiles_of(t):
                    return [t[:, it, :] for it in range(NT)]

                def a_split():
                    dve.wait_ge(x_hi_done, a + 1)
                    v.tensor_tensor(x_lo[:], x_t[:], x_hi[:], ALU.subtract).then_inc(x_lo_done, 1)

                def a_proj(u):
                    if u == "V":
                        return
                    n = 0 if u == KVU else u + 1
                    o = filled(("a_proj", u), "PJ")
                    wait(dve, rot_done, a * 5 + n)
                    q4 = o[:, :].rearrange("p (t h d) -> p t h d", t=NT, h=G)

                    def table(t, lo, hi):
                        return t[:, :, lo:hi].unsqueeze(2).to_broadcast([P, NT, G, hi - lo])

                    hw = DH // 2
                    v.tensor_tensor(rot_c[:], q4, table(cos_t, 0, DH), ALU.mult)
                    v.tensor_tensor(rot_s[:, :, :, 0:hw], q4[:, :, :, hw:DH], table(sin_t, 0, hw), ALU.mult)
                    v.tensor_tensor(rot_s[:, :, :, hw:DH], q4[:, :, :, 0:hw], table(sin_t, hw, DH),
                                    ALU.mult).then_inc(rp_done, 1)
                    dve.wait_ge(rp_done, a * 5 + n + 1)
                    dve.sem_inc(free["PJ"], 1)

                def a_turn(u):
                    n = 0 if u == KVU else u + 1
                    for half in range(2):
                        o = filled(("a_turn", u), f"TP{half}")
                        heads = slice(2 * half, 2 * half + 2)
                        dve.wait_ge(t1_done, a * 10 + 2 * n + half + 1)
                        src = o[:, :].rearrange("p (h n) -> p h n", h=2)
                        if u == KVU:
                            ins_ = v.tensor_tensor(k1[DH:P, heads, :], src[DH:P], k1[DH:P, heads, :], ALU.subtract)
                        else:
                            ins_ = v.tensor_tensor(t2[u % 2][0:DH, heads, :], src[0:DH], t1[u % 2][0:DH, heads, :],
                                                   ALU.subtract)
                        ins_.then_inc(free[f"TP{half}"], 1)

                def a_max(g, h):
                    o = filled(("a_max", g, h), "SM")
                    if h == 0:
                        wait(dve, mr_done, a * 4 + g - 1)
                    v.tensor_reduce(mx[g % 2][:, :, h], o[:, :].rearrange("p (t n) -> p t n", t=NT),
                                    AX.X, ALU.max).then_inc(mx_done, 1)
                    dve.wait_ge(mx_done, a * 16 + G * g + h + 1)
                    dve.sem_inc(free["SM"], 1)

                def a_pv(g, p):
                    o = filled(("a_pv", g, p), "OO")
                    o4 = o[:, 0:2 * NT * VW].rearrange("p (t h d) -> p t h d", t=NT, h=2)
                    link(v.reciprocal(rden[:], o4[:, :, :, DH]), "a")
                    if p == 0:
                        wait(dve, oh_done, a * 4 + g)
                    v.tensor_tensor(att[:, :, 2 * p:2 * p + 2, :], o4[:, :, :, 0:DH],
                                    rden[:].unsqueeze(3).to_broadcast([P, NT, 2, DH]), ALU.mult).then_inc(o_done, 1)
                    dve.wait_ge(o_done, a * 8 + 2 * g + p + 1)
                    dve.sem_inc(free["OO"], 1)

                def a_ot(g):
                    o = filled(("a_ot", g), "TP0")
                    dve.wait_ge(oh_done, a * 4 + g + 1)
                    v.tensor_tensor(att_lo[:], o[:, :].rearrange("p (h n) -> p h n", h=2),
                                    att_hi[:], ALU.subtract).then_inc(free["TP0"], 1)

                def a_res():
                    dve.wait_ge(wo_done, (a + 1) * 4)
                    dve.wait_ge(xn_in, (a + 1) * 16)
                    v.tensor_tensor(x_n[:], bank["YY"][:, :].rearrange("p (t c) -> p t c", t=NT), x_n[:],
                                    ALU.add).then_inc(ya_free, 1)
                    dve.wait_ge(ya_free, a + 1)
                    link(v.tensor_tensor(x_n[:], x_n[:], bo[:].unsqueeze(1).to_broadcast([P, NT, D]), ALU.add), "a")
                    stats("a", tiles_of(x_n), P, NT, st_a, mv_a, ve_a).then_inc(va_done, 1)
                    dve.wait_ge(ra_done, a + 1)
                    if b is not None:
                        dve.wait_ge(y_done, b + 1)
                    normed(tiles_of(x1), tiles_of(x_n), P, NT, mv_a, rs_a).then_inc(x1_done, 1)
                    check("a")

                def b_ln():
                    dve.wait_ge(x1_done, b + 1)
                    stats("b", tiles_of(x1), P, NT, st_b, mv_b, ve_b).then_inc(vb_done, 1)
                    dve.wait_ge(rb_done, b * B_NORMS + 1)
                    wait(dve, y_out, b * 16)
                    normed(tiles_of(z), tiles_of(x1), P, NT, mv_b, rs_b).then_inc(z_done, 1)
                    dve.wait_ge(z_done, b * 2 + 1)

                def b_cln():
                    dve.wait_ge(cx_in, (b + 1) * 48)
                    v.tensor_scalar(m_neg[:], m_u8[:], 1.0, MASKED, ALU.subtract, ALU.mult)
                    link(v.tensor_scalar(mc_neg[:], mc_u8[:], 1.0, MASKED, ALU.subtract, ALU.mult), "b")
                    stats("b", [ctx_n[:]], NC_, 1, st_b, mv_b, ve_b).then_inc(vb_done, 1)
                    dve.wait_ge(rb_done, b * B_NORMS + 2)
                    normed([ctx_n[:]], [ctx_n[:]], NC_, 1, mv_b, rs_b).then_inc(z_done, 1)

                def head_norm(n, rows, src, tiles):
                    dve.wait_ge(sq_done, b * 3 + n + 1)
                    cols = tiles * HX
                    link(v.tensor_reduce(ss[0:rows, 0:cols], sq[0:rows, 0:cols * DH].rearrange("p (h d) -> p h d", d=DH),
                                         AX.X, ALU.add), "b")
                    v.tensor_scalar(ss[0:rows, 0:cols], ss[0:rows, 0:cols], 1.0 / DH, RMS_FLOOR,
                                    ALU.mult, ALU.max).then_inc(vb_done, 1)
                    dve.wait_ge(rb_done, b * B_NORMS + n + 3)
                    dve.wait_ge(tx_done, b * 5 + 2 * n) if n else wait(dve, ohx_done, b)
                    v.tensor_tensor(xn[0:rows, 0:cols], src.unsqueeze(2).to_broadcast([rows, cols, 2, DH]),
                                    ri[0:rows, 0:cols].unsqueeze(2).unsqueeze(2).to_broadcast([rows, cols, 2, DH]),
                                    ALU.mult).then_inc(xn_done, 1)
                    dve.wait_ge(xn_done, b * 3 + n + 1)
                    dve.sem_inc(free["PJ"], 1)

                def b_proj(u):
                    if u == "v":
                        return
                    o = filled(("b_proj", u), "PJ")
                    head_norm({"q": 0, "k": 1}[u], P, o[:, :].rearrange("p (h d) -> p h d", d=DH), NT)

                def b_cproj():
                    o = filled(("b_cproj",), "PJ")
                    head_norm(2, NC_, o[0:NC_, 0:D].rearrange("p (h d) -> p h d", d=DH), 1)

                def b_turn(u):
                    for half in range(1 if u == "c" else 2):
                        o = filled(("b_turn", u), f"TP{half}")
                        n = {"q": 0, "k": 2, "c": 4}[u] + half
                        dve.wait_ge(tx_done, b * 5 + n + 1)
                        heads = slice(2 * half, 2 * half + 2)
                        if u == "c":
                            src = o[:, 0:HX * NCP].rearrange("p (h n) -> p h n", h=HX)[:, :, 0:NC_]
                            heads, keys = slice(0, HX), slice(N, N + NC_)
                        else:
                            src, keys = o[:, :].rearrange("p (h n) -> p h n", h=2), slice(0, N)
                        if u == "q":
                            ins_ = v.scalar_tensor_tensor(t2x[0:DH, heads, :], src[0:DH], g_q[0:DH, 0:1],
                                                          t1x[0:DH, heads, :], ALU.mult, ALU.subtract)
                        else:
                            ins_ = v.scalar_tensor_tensor(k1x[DH:P, heads, keys], src[DH:P], g_k[DH:P, 0:1],
                                                          k1x[DH:P, heads, keys], ALU.mult, ALU.subtract)
                        ins_.then_inc(free[f"TP{half}"], 1)

                def b_max(h):
                    o = filled(("b_max", h), "SM")
                    v.tensor_reduce(mx_l[:, :, h], o[:, :].rearrange("p (t n) -> p t n", t=NT),
                                    AX.X, ALU.max).then_inc(free["SM"], 1)

                def b_maxc(p):
                    o = filled(("b_maxc", p), "SM")
                    link(v.tensor_tensor(sc_c[:], o[:, 0:2 * NT * NCP].rearrange("p (h t n) -> p h t n", h=2, t=NT)[:, :, :, 0:NC_],
                                         m_neg[:].unsqueeze(1).unsqueeze(1).to_broadcast([P, 2, NT, NC_]), ALU.add), "b")
                    dve.sem_inc(free["SM"], 1)
                    link(v.tensor_reduce(mx_c[:].rearrange("p t h -> p h t")[:, 2 * p:2 * p + 2, :], sc_c[:],
                                         AX.X, ALU.max), "b")

                def b_mrow():
                    dve.wait_ge(free["SM"], sec.used(("b_max", HX - 1), "SM") + 1)
                    wait(dve, mrb_done, b)
                    v.tensor_tensor(mx_b[:], mx_l[:], mx_c[:], ALU.max).then_inc(mb_done, 1)

                def b_pv(p):
                    o = filled(("b_pv", p), "OO")
                    o4 = o[:, 0:2 * NT * VW].rearrange("p (t h d) -> p t h d", t=NT, h=2)
                    link(v.reciprocal(rden_b[:], o4[:, :, :, DH]), "b")
                    if p == 0:
                        wait(dve, ohx_done, b)
                    v.tensor_tensor(attx[:, :, 2 * p:2 * p + 2, :], o4[:, :, :, 0:DH],
                                    rden_b[:].unsqueeze(3).to_broadcast([P, NT, 2, DH]), ALU.mult).then_inc(ox_done, 1)
                    dve.wait_ge(ox_done, b * 2 + p + 1)
                    dve.sem_inc(free["OO"], 1)

                def b_ot():
                    o = filled(("b_ot",), "TP0")
                    dve.wait_ge(ohx_done, b + 1)
                    v.tensor_tensor(attx_lo[:], o[:, :].rearrange("p (h n) -> p h n", h=2), attx_hi[:],
                                    ALU.subtract).then_inc(free["TP0"], 1)

                def b_res():
                    o = filled(("b_wo",), "PJ")
                    link(v.tensor_tensor(acc[:], o[:, :].rearrange("p (t c) -> p t c", t=NT), x1[:], ALU.add), "b")
                    dve.sem_inc(free["PJ"], 1)
                    link(v.tensor_tensor(acc[:], acc[:], xbo[:].unsqueeze(1).to_broadcast([P, NT, D]), ALU.add), "b")
                    stats("b", tiles_of(acc), P, NT, st_b, mv_b, ve_b).then_inc(vb_done, 1)
                    dve.wait_ge(rb_done, b * B_NORMS + 6)
                    normed(tiles_of(x2), tiles_of(acc), P, NT, mv_b, rs_b).then_inc(x2_done, 1)
                    dve.wait_ge(x2_done, b + 1)

                def b_x2t():
                    o = filled(("b_x2t",), "TP1")
                    dve.wait_ge(x2h_done, b + 1)
                    v.tensor_tensor(x2_lo[:], o[:, :].rearrange("p (h n) -> p h n", h=2), x2_hi[:],
                                    ALU.subtract).then_inc(free["TP1"], 1)

                def b_route():
                    o = filled(("b_gate",), "PJ")
                    link(v.tensor_copy(lg[:], o[:, 0:NT * E].rearrange("p (t e) -> p t e", t=NT)), "b")
                    dve.sem_inc(free["PJ"], 1)
                    own = lg[:].unsqueeze(3).to_broadcast([P, NT, E, E])
                    other = lg[:].unsqueeze(2).to_broadcast([P, NT, E, E])
                    v.tensor_tensor(gt[:], other, own, ALU.is_gt)
                    link(v.tensor_tensor(eq[:], other, own, ALU.is_equal), "b")
                    link(v.tensor_tensor(eq[:], eq[:], before[:].unsqueeze(1).to_broadcast([P, NT, E, E]), ALU.mult), "b")
                    link(v.tensor_tensor(gt[:], gt[:], eq[:], ALU.add), "b")
                    link(v.tensor_reduce(rank[:], gt[:], AX.X, ALU.add), "b")
                    v.tensor_scalar(sel0[:], rank[:], 0.0, None, ALU.is_equal)
                    link(v.tensor_scalar(sel1[:], rank[:], 1.0, None, ALU.is_equal), "b")
                    v.tensor_reduce(top[:, 0, :], lg[:], AX.X, ALU.max)
                    link(v.tensor_tensor(gate[:], lg[:], sel1[:], ALU.mult), "b")
                    link(v.tensor_reduce(top[:, 1, :], gate[:], AX.X, ALU.add), "b")
                    v.tensor_tensor(top[:, 2, :], top[:, 1, :], top[:, 0, :], ALU.subtract).then_inc(dif_done, 1)
                    dve.wait_ge(exp_done, b + 1)
                    link(v.tensor_scalar(top[:, 4, :], top[:, 3, :], 1.0, None, ALU.add), "b")
                    link(v.reciprocal(top[:, 4, :], top[:, 4, :]), "b")
                    link(v.tensor_tensor(top[:, 5, :], top[:, 4, :], top[:, 3, :], ALU.mult), "b")
                    v.tensor_tensor(sel0[:], sel0[:], top[:, 4, :].unsqueeze(2).to_broadcast([P, NT, E]), ALU.mult)
                    link(v.tensor_tensor(sel1[:], sel1[:], top[:, 5, :].unsqueeze(2).to_broadcast([P, NT, E]), ALU.mult), "b")
                    link(v.tensor_tensor(gate[:], sel0[:], sel1[:], ALU.add), "b")

                def b_expert(n):
                    it, e2 = n // (E // 2), n % (E // 2)
                    k = EX_BANKS[n % 4]
                    o = filled(("b_expert", n), k)
                    for j in range(2):
                        e = 2 * e2 + j
                        prev = x2 if e == 0 else acc
                        link(v.scalar_tensor_tensor(acc[:, it, :], o[:, j * D:(j + 1) * D], gate[:, it, e:e + 1],
                                                    prev[:, it, :], ALU.mult, ALU.add), "b")
                    dve.sem_inc(free[k], 1)

                def b_out():
                    stats("b", tiles_of(acc), P, NT, st_b, mv_b, ve_b).then_inc(vb_done, 1)
                    dve.wait_ge(rb_done, b * B_NORMS + 7)
                    normed(tiles_of(y), tiles_of(acc), P, NT, mv_b, rs_b).then_inc(y_done, 1)
                    check("b")

                def check(s):
                    want = A_LINKS if s == "a" else B_LINKS
                    assert count[s] == want, (s, count[s])

                return dict(a_split=a_split, a_proj=a_proj, a_turn=a_turn, a_max=a_max, a_pv=a_pv, a_ot=a_ot,
                            a_res=a_res, b_ln=b_ln, b_cln=b_cln, b_proj=b_proj, b_cproj=b_cproj, b_turn=b_turn,
                            b_max=b_max, b_maxc=b_maxc, b_mrow=b_mrow, b_pv=b_pv, b_ot=b_ot, b_res=b_res,
                            b_x2t=b_x2t, b_route=b_route, b_expert=b_expert, b_out=b_out)

            walk(dve, steps_of)


def tables():
    inv = (np.float32(1.0) / np.float32(10000.0) ** (np.arange(0, DH, 2, dtype=np.float32) / np.float32(DH))).astype(np.float32)
    ang = np.arange(N, dtype=np.float32)[:, None] * inv[None, :]
    cos, sin = np.cos(ang).astype(np.float32), np.sin(ang).astype(np.float32)
    return {"cos": np.concatenate([cos, cos], 1), "sin": np.concatenate([-sin, sin], 1),
            "ident": np.eye(P, dtype=np.float32), "before": np.tril(np.ones((E, E), np.float32), -1)}


def kernel(**inputs):
    import concourse.bacc as bacc
    from concourse.bass_utils import run_bass_kernel_spmd

    i = {k: np.asarray(v) for k, v in inputs.items()}
    x = i["x"]
    arrays = {
        "x": x, "x_t": x.transpose(0, 2, 1), "ctx": i["ctx_768"], "mask": i["mask_BxS2_bk0"],
        "q": i["L0_attn_Wq"], "kv": i["L0_attn_Wkv"], "o": i["L0_attn_Wo"],
        "xq": i["L0_xattn_Wq"].T, "xl": i["L0_xattn_Wlkv"].T, "xo": i["L0_xattn_Wo"].T, "xc": i["L0_xattn_Wkv"].T,
        "ex": i["L0_ffn_expert_w"].transpose(2, 0, 1).reshape(D, E * D), "gate": i["L0_ffn_gate_w"].T,
        "bo": i["L0_attn_bo"], "xbo": i["L0_xattn_bo"],
        "ln_g": i["L0_xattn_ln_l_g"].reshape(KC, P).T, "ln_b": i["L0_xattn_ln_l_b"].reshape(KC, P).T,
        "lc_g": i["L0_xattn_ln_x_g"].reshape(DC, 1), "lc_b": i["L0_xattn_ln_x_b"].reshape(DC, 1),
        "g_q": i["L0_xattn_qn_g"].reshape(DH, 1), "g_k": i["L0_xattn_kn_g"].reshape(DH, 1),
        **tables(),
    }
    nc = bacc.Bacc("TRN2", target_bir_lowering=False, num_devices=1)
    feeds, ins = {}, {}
    for name, a in arrays.items():
        a = np.ascontiguousarray(a)
        feeds[f"{name}_dram"] = a
        ins[name] = nc.dram_tensor(f"{name}_dram", a.shape, mybir.dt.from_np(a.dtype), kind="ExternalInput").ap()
    out = nc.dram_tensor("out_dram", (B, N, D), F32, kind="ExternalOutput").ap()
    build(nc, ins, out)
    r = run_bass_kernel_spmd(nc, [feeds], core_ids=[0])
    return r.results[0]["out_dram"]
```

```python
from contextlib import ExitStack

import numpy as np
import concourse.bass as bass
from concourse import mybir

F32 = mybir.dt.float32
F32R = mybir.dt.float32r
U8 = mybir.dt.uint8
ALU = mybir.AluOpType
ACT = mybir.ActivationFunctionType
AX = mybir.AxisListType

P = 128
B, N, D = 8, 256, 256
NT = N // P
KC = D // P
DH = 64
HQ, HKV = 16, 4
G = HQ // HKV
HX = D // DH
NC_, DC = 77, 192
NCP = NC_ + 1
DC2 = DC - P
E = 8
SCALE = DH ** -0.5
LN_EPS = 1e-5
RMS_FLOOR = 1e-16
MASKED = 3e38
VW = DH + 1

W_COLS = dict(kv=KC * 2 * HKV * DH, q=KC * HQ * DH, o=HQ * DH // P * D, xq=KC * D, xo=KC * D, xl=KC * 2 * D,
              ex=KC * E * D, xc=2 * 2 * D, gate=KC * E)
CHUNKS_OF = {name: KC for name in W_COLS}
CHUNKS_OF["o"] = HQ * DH // P
W_AT, _at = {}, 0
for _name, _cols in W_COLS.items():
    W_AT[_name] = _at
    _at += _cols
W_ALL = _at
CHUNKS = [([("kv", 0, KC)], 0), ([("q", 0, KC)], 1), ([("o", 0, 8)], 0),
          ([("xq", 0, KC), ("xo", 0, KC), ("xl", 0, KC)], 1), ([("ex", 0, 1)], 0), ([("ex", 1, 2)], 1),
          ([("xc", 0, 2), ("gate", 0, KC)], 0)]
STAGE = (2048, 2048)
ARENA = 6336

KVU = "K"
RING = tuple(f"R{i}" for i in range(7))
BANKS = RING + ("YY",)


def banks_of(step):
    kind, args = step[0], step[1:]
    if kind in ("a_turn", "b_turn"):
        return 1 if args == ("c",) else 2
    if kind in ("a_scores", "b_scores"):
        return {"a_scores": NT, "b_scores": NT + 1}[kind]
    return int(kind in ("a_proj", "a_max", "a_mrow", "a_pv", "a_ot", "b_zt", "b_ct", "b_proj", "b_cproj",
                        "b_max", "b_maxc", "b_mrow", "b_pv", "b_ot", "b_wo", "c_x2t", "c_gate", "c_expert"))


def reader_of(step):
    kind, args = step[0], step[1:]
    if kind in ("a_turn", "b_turn"):
        return (kind[0] + "_lo", *args)
    if kind == "b_proj" and args != ("v",):
        return ("b_xn", *args)
    return {"b_cproj": ("b_xn", "c"), "a_ot": ("a_otlo", *args), "b_ot": ("b_otlo",), "b_wo": ("b_res",),
            "c_x2t": ("c_x2lo",), "c_gate": ("c_route",)}.get(kind, step)


def listed(text):
    return [tuple(int(w) if w.isdigit() else w for w in step.split(":")) for step in text.split()]


ORDER = listed("""
    a_next b_ln c_x2t b_cln a_proj:K c_x2lo a_rot:K a_proj:0 b_z a_proj:V b_cn a_turn:K a_rot:0 c_gate b_zt
    c_route a_turn:0 a_lo:K b_ct a_lo:0 b_proj:q a_load c_weights a_max:0:0 a_max:0:1 a_max:0:2 b_ss:q
    c_expert:0 a_proj:1 b_proj:k a_max:0:3 b_cproj a_mrow:0 a_rot:1 c_expert:1 b_ss:k a_turn:1 a_lo:1
    a_scores:0:0 a_max:1:0 b_ss:c b_xn:q a_max:1:1 b_proj:v c_expert:2 a_max:1:2 a_scores:0:1 c_expert:3
    b_turn:q b_lo:q a_proj:2 c_expert:4 a_max:1:3 a_pv:0:0 a_rot:2 a_pv:0:1 b_xn:k c_expert:5 a_mrow:1
    a_ot:0 b_turn:k a_otlo:0 b_xn:c c_expert:6 b_lo:k a_wo:0 a_turn:2 c_expert:7 a_max:2:0 a_scores:1:0
    a_max:2:1 b_turn:c c_out b_lo:c a_max:2:2 a_scores:1:1 b_maxc:0 b_max:0 a_pv:1:0 a_max:2:3 b_maxc:1
    a_proj:3 a_pv:1:1 a_mrow:2 b_max:1 a_ot:1 b_max:2 a_otlo:1 c_y a_rot:3 a_wo:1 a_lo:2 b_max:3 a_turn:3
    b_mrow a_max:3:0 a_scores:2:0 a_lo:3 a_scores:2:1 a_max:3:1 b_scores:0 a_max:3:2 b_pv:0 b_scores:1
    a_pv:2:0 a_max:3:3 b_pv:1 a_pv:2:1 a_mrow:3 b_ot a_ot:2 a_scores:3:0 b_otlo a_otlo:2 b_wo a_pv:3:0
    a_scores:3:1 a_wo:2 b_res a_pv:3:1 b_next b_x2 a_ot:3 a_otlo:3 a_wo:3 a_res a_split a_norm
""")

FILL = listed("""
    a_load a_next a_proj:K a_rot:K a_proj:0 a_rot:0 a_turn:K a_lo:K a_proj:V a_turn:0 a_lo:0 a_max:0:0
    a_max:0:1 a_max:0:2 a_max:0:3 a_proj:1 a_rot:1 a_mrow:0 a_turn:1 a_lo:1 a_scores:0:0 a_max:1:0
    a_scores:0:1 a_max:1:1 a_max:1:2 a_max:1:3 a_pv:0:0 a_proj:2 a_rot:2 a_mrow:1 a_pv:0:1 a_ot:0 a_otlo:0
    a_scores:1:0 a_turn:2 a_wo:0 a_lo:2 a_max:2:0 a_max:2:1 a_scores:1:1 a_max:2:2 a_max:2:3 a_pv:1:0
    a_proj:3 a_pv:1:1 a_rot:3 a_ot:1 a_otlo:1 a_mrow:2 a_wo:1 a_turn:3 a_lo:3 a_scores:2:0 a_max:3:0
    a_max:3:1 a_scores:2:1 a_max:3:2 a_pv:2:0 a_max:3:3 a_pv:2:1 a_mrow:3 a_ot:2 a_otlo:2 a_scores:3:0
    a_scores:3:1 a_pv:3:0 a_wo:2 a_pv:3:1 a_ot:3 a_otlo:3 a_wo:3 a_res a_split a_norm
""")


def only(steps, streams):
    return [step for step in steps if step[0][0] in streams]


def setup(a):
    out, n = [], 2
    for step in a:
        out.append(step)
        if step[0] in ("a_lo", "a_max") and step[-1] != 0 and n < len(CHUNKS):
            out += [("w_split", n)] + [("w_load", n + 2)] * (n + 2 < len(CHUNKS))
            n += 1
        if step == ("a_otlo", 0):
            out += [("w_need", 3)]
    return out + [("w_need", len(CHUNKS))]


class Section:

    def __init__(self, steps, base):
        self.steps, self.base, self.per, self.turn = steps, dict(base), {k: 0 for k in BANKS}, 0
        self.order, at = {}, {step: n for n, step in enumerate(steps)}
        freed_at = {k: n - len(RING) for n, k in enumerate(RING)}
        for step in steps:
            for n in range(banks_of(step)):
                bank = min(RING, key=freed_at.get)
                assert freed_at[bank] < at[step], step
                freed_at[bank] = at[reader_of(step)]
                self.order[step, n] = bank, self.per[bank]
                self.per[bank] += 1

    def after(self, turns):
        return {k: self.base[k] + turns * self.per[k] for k in BANKS}

    def bank(self, step, n=0):
        return self.order[step, n][0]

    def used(self, step, n=0):
        bank, order = self.order[step, n]
        return self.turn * self.per[bank] + (self.base[bank] + order)


def build(nc, ins, out):
    ctx = ExitStack()
    with ctx:
        def sb(name, shape, dt=F32):
            return ctx.enter_context(nc.sbuf_tensor(name, shape, dt))

        def sem(name):
            return ctx.enter_context(nc.semaphore(name))

        bank = {k: ctx.enter_context(nc.psum_tensor(f"bank_{k}", [P, 512], F32)) for k in BANKS}
        full = {k: sem(f"full_{k}") for k in BANKS}
        free = {k: sem(f"free_{k}") for k in BANKS}

        w_hi, w_lo = sb("w_hi", [P, W_ALL], F32R), sb("w_lo", [P, W_ALL], F32R)
        arena = sb("arena", [P, ARENA])
        stage = [arena[:, 0:STAGE[0]], arena[:, STAGE[0]:sum(STAGE)]]
        arena_at = [0]

        def lay(*shape):
            n = int(np.prod(shape))
            t = arena[:, arena_at[0]:arena_at[0] + n]
            arena_at[0] += n
            names = "abc"[:len(shape)]
            if len(shape) == 1:
                return t
            return t.rearrange(f"p ({' '.join(names)}) -> p {' '.join(names)}",
                               **{m: w for m, w in zip(names[1:], shape[1:])})

        prob = [arena[:, ARENA - n * NT * 2 * N:ARENA - (n - 1) * NT * 2 * N].rearrange(
            "p (t n) -> p t n", t=NT) for n in (1, 2)]

        ident = sb("ident", [P, P])
        cos_t, sin_t = sb("cos_t", [P, NT, DH]), sb("sin_t", [P, NT, DH])
        before = sb("before", [P, E, E])
        bo, xbo = sb("bo", [P, D]), sb("xbo", [P, D])
        half_neg = sb("half_neg", [P, 8])
        ln_g, ln_b = sb("ln_g", [P, KC]), sb("ln_b", [P, KC])
        lc_g, lc_b = sb("lc_g", [P, KC]), sb("lc_b", [P, KC])
        g_q, g_k = sb("g_q", [P, 1]), sb("g_k", [P, 1])

        x_t = sb("x_t", [P, KC, N])
        x_n = sb("x_n", [P, NT, D])
        x_hi, x_lo = sb("x_hi", [P, KC, N], F32R), sb("x_lo", [P, KC, N], F32R)
        rot_c, rot_s = sb("rot_c", [P, NT, G, DH]), sb("rot_s", [P, NT, G, DH])
        rot = sb("rot", [P, NT * G, 2, DH])
        k1, k2 = sb("k1", [P, HKV, N], F32R), sb("k2", [P, HKV, N], F32R)
        t1 = [sb(f"t1_{i}", [P, G, N], F32R) for i in range(2)]
        t2 = [sb(f"t2_{i}", [P, G, N], F32R) for i in range(2)]
        val = sb("val", [P, NT, HKV, VW])
        mx = [sb(f"mx{i}", [P, NT, G]) for i in range(2)]
        mrows = sb("mrows", [DH, N], F32R)
        mrow, mrow_b = mrows[0:G, :], mrows[32:32 + HX, :]
        rden = [sb(f"rden{p}", [P, NT, 2]) for p in range(2)]
        att = sb("att", [P, NT, G, DH])
        att_hi, att_lo = sb("att_hi", [P, 2, N], F32R), sb("att_lo", [P, 2, N], F32R)
        st_a, mv_a = sb("st_a", [P, NT, 6]), sb("mv_a", [P, NT, 2])
        ve_a, rs_a = sb("ve_a", [P, NT]), sb("rs_a", [P, NT])
        x1 = sb("x1", [P, NT, D])

        ctx_n = sb("ctx_n", [NC_, DC])
        m_u8, mc_u8 = sb("m_u8", [P, NC_], U8), sb("mc_u8", [NC_, 1], U8)
        m_neg, mc_neg = sb("m_neg", [P, NC_]), sb("mc_neg", [NC_, 1])
        st_b, mv_b = sb("st_b", [P, NT, 6]), sb("mv_b", [P, NT, 2])
        ve_b, rs_b = sb("ve_b", [P, NT]), sb("rs_b", [P, NT])
        st_c, mv_c = sb("st_c", [P, 1, 6]), sb("mv_c", [P, 1, 2])
        ve_c, rs_c = sb("ve_c", [P, 1]), sb("rs_c", [P, 1])
        z_hi, z_lo = sb("z_hi", [P, KC, N], F32R), sb("z_lo", [P, KC, N], F32R)
        cf = sb("cf", [P, 2, NCP])
        c_hi, c_lo = sb("c_hi", [P, 2, NCP], F32R), sb("c_lo", [P, 2, NCP], F32R)
        probx = lay(NT + 1, 2 * N)
        z = probx[:, 0, :].rearrange("p (t c) -> p t c", t=NT)
        zf = probx[:, 1, :].rearrange("p (k n) -> p k n", k=KC)
        sq = [probx[:, n, :] for n in range(3)]
        ss = [sb(f"ss{n}", [P, NT * HX]) for n in range(3)]
        ri = [sb(f"ri{n}", [P, NT * HX]) for n in range(3)]
        xn = lay(NT * HX, 2, DH)
        attx = xn.rearrange("p h two d -> p (h two d)")[:, 0:NT * HX * DH].rearrange(
            "p (t h d) -> p t h d", t=NT, h=HX)
        t1x, t2x = sb("t1x", [P, HX, N], F32R), sb("t2x", [P, HX, N], F32R)
        k1x, k2x = sb("k1x", [P, HX, N + NCP], F32R), sb("k2x", [P, HX, N + NCP], F32R)
        valx = lay(NT + 1, HX, VW)
        mx_l, mx_c, mx_b = sb("mx_l", [P, NT, HX]), sb("mx_c", [P, NT, HX]), sb("mx_b", [P, NT, HX])
        sc_c = lay(2, NT, NC_)
        rden_b = [sb(f"rden_b{p}", [P, NT, 2]) for p in range(HX // 2)]
        attx_hi, attx_lo = z_hi, z_lo

        x2 = acc = y = lay(NT, D)
        x2_hi, x2_lo = sb("x2_hi", [P, KC, N], F32R), sb("x2_lo", [P, KC, N], F32R)
        st_y, mv_y = sb("st_y", [P, NT, 6]), sb("mv_y", [P, NT, 2])
        ve_y, rs_y = sb("ve_y", [P, NT]), sb("rs_y", [P, NT])
        lg = sb("lg", [P, NT, E])
        gt, eq = lay(NT, E * E).rearrange("p t (e f) -> p t e f", e=E), sb("eq", [P, NT, E, E])
        rank, sel0, sel1 = sb("rank", [P, NT, E]), sb("sel0", [P, NT, E]), sb("sel1", [P, NT, E])
        top = sb("top", [P, 6, NT])
        gate = sb("gate", [P, NT, E])

        w_in = [sem(f"w_in{i}") for i in range(2)]
        c_in = sem("c_in")
        w_hi_done, w_lo_done = sem("w_hi_done"), sem("w_lo_done")
        fill_done, const_done = sem("fill_done"), sem("const_done")
        xt_in, xn_in = sem("xt_in"), sem("xn_in")
        x_hi_done, x_lo_done = sem("x_hi_done"), sem("x_lo_done")
        rot_done = sem("rot_done")
        t1_done = sem("t1_done")
        mr_in = [sem(f"mr_in{i}") for i in range(2)]
        oh_done = sem("oh_done")
        wo_done = sem("wo_done")
        ya_free = sem("ya_free")
        va_done, ra_done = sem("va_done"), sem("ra_done")
        x1_done = sem("x1_done")
        dve_a = sem("dve_a")
        cx_in = sem("cx_in")
        vb_done, rb_done = sem("vb_done"), sem("rb_done")
        z_done = sem("z_done")
        zh_done, zl_done = sem("zh_done"), sem("zl_done")
        sq_done = sem("sq_done")
        xn_done = sem("xn_done")
        tx_done = sem("tx_done")
        mb_done = sem("mb_done")
        mrb_in = sem("mrb_in")
        ohx_done = sem("ohx_done")
        x2_done = sem("x2_done")
        x2h_done = sem("x2h_done")
        dif_done, exp_done = sem("dif_done"), sem("exp_done")
        y_done, y_out = sem("y_done"), sem("y_out")
        dve_b, dve_c = sem("dve_b"), sem("dve_c")
        vc_done, rc_done = sem("vc_done"), sem("rc_done")

        A_LINKS, B_LINKS, C_LINKS = 11, 15, 14
        B_NORMS = 6

        first = Section(setup(only(FILL, "a")), {k: 0 for k in BANKS})
        second = Section(only(ORDER, "ab"), first.after(1))
        third = Section(ORDER, second.after(1))
        steady = Section(ORDER, third.after(1))
        drain = Section([s for s in only(ORDER, "bc") if s != ("b_next",)], steady.after(B - 3))
        last = Section(only(ORDER, "c"), drain.after(1))

        def walk(eng, steps_of):
            def run(sec, a, b, c):
                steps = steps_of(sec, a, b, c)
                for step in sec.steps:
                    if step[0] in steps:
                        steps[step[0]](*step[1:])

            run(first, 0, None, None)
            run(second, 1, 0, None)
            run(third, 2, 1, 0)
            with eng.Fori(0, B - 3) as i:
                steady.turn = i
                run(steady, i + 3, i + 2, i + 1)
            run(drain, None, B - 1, B - 2)
            run(last, None, None, B - 1)

        def wait(eng, s, value):
            if not isinstance(value, int) or value > 0:
                eng.wait_ge(s, value)

        def weights(t, name, chunk, c0, c1):
            per = W_COLS[name] // CHUNKS_OF[name]
            at = W_AT[name] + chunk * per
            return t[:, at + c0:at + c1]

        def chunk(n):
            parts, st = CHUNKS[n]
            name, k0, _ = parts[0]
            at = W_AT[name] + k0 * (W_COLS[name] // CHUNKS_OF[name])
            cols = sum(W_COLS[m] // CHUNKS_OF[m] * (k1_ - k0_) for m, k0_, k1_ in parts)
            loads = sum(1 + (m == "xc") for c in CHUNKS[:n + 1] if c[1] == st for m, _, _ in c[0])
            return at, cols, st, 16 * loads

        def latest(sec, fills, then):
            last = {}
            for step, n in fills:
                k, order = sec.order[step, n]
                if k not in last or order > sec.order[last[k]][1]:
                    last[k] = step, n
            for step, n in then:
                last.pop(sec.bank(step, n), None)
            return last.items()

        def freed(eng, sec, *fills, then=()):
            for k, fill in latest(sec, fills, then):
                eng.wait_ge(free[k], sec.used(*fill) + 1)

        def was_filled(eng, sec, *fills, then=()):
            for k, fill in latest(sec, fills, then):
                eng.wait_ge(full[k], sec.used(*fill) + 1)

        def is_head(t, h):
            return t[:, :].rearrange("p (h n) -> p h n", h=2)[:, h, :]

        block = ctx.enter_context(nc.Block())

        fixed = [(half_neg[:], -0.5)]
        fixed += [(t[DH:P].bitcast(F32), 0.0) for t in (k2, t2[0], t2[1], k2x, t2x)]
        fixed += [(k1x[:, :, N + NC_:N + NCP].bitcast(F32), 0.0), (val[:, :, :, DH:VW], 1.0)]
        fixed += [(t[DH:DH + 1].bitcast(F32), 1.0) for t in (k2, k2x)]
        FILLS = len(fixed)

        @block.sync
        def _(sp):
            def load_weights(n):
                parts, st = CHUNKS[n]
                if n >= 2:
                    sp.wait_ge(w_lo_done, n - 1)
                if n == len(CHUNKS) - 1:
                    sp.wait_ge(const_done, 1)
                at = 0
                for name, k0, k1_ in parts:
                    cols = W_COLS[name] // CHUNKS_OF[name] * (k1_ - k0)
                    src, dst = ins[name], stage[st][:, at:at + cols]
                    if name == "xc":
                        sp.dma_start(dst[:, 0:2 * D], src[0:P, :]).then_inc(w_in[st], 16)
                        src, dst = src[P:DC, :], dst[0:DC2, 2 * D:4 * D]
                        sp.dma_start(dst, src).then_inc(w_in[st], 16)
                    else:
                        sp.dma_start(dst.rearrange("p (k n) -> p k n", k=k1_ - k0),
                                     src.rearrange("(k p) n -> p k n", p=P)[:, k0:k1_, :]).then_inc(w_in[st], 16)
                    at += cols

            sp.dma_start(x_t[:], ins["x_t"][0].rearrange("(k p) n -> p k n", p=P)).then_inc(xt_in, 16)
            load_weights(0)
            load_weights(1)
            for dst, src in ((cos_t[:], ins["cos"].rearrange("(t p) d -> p t d", p=P)),
                             (sin_t[:], ins["sin"].rearrange("(t p) d -> p t d", p=P)),
                             (ident[:], ins["ident"]), (before[:], ins["before"].partition_broadcast(P)),
                             (bo[:], ins["bo"].partition_broadcast(P)),
                             (xbo[:], ins["xbo"].partition_broadcast(P)),
                             (ln_g[:], ins["ln_g"]), (ln_b[:], ins["ln_b"]),
                             (lc_g[:, 0:1], ins["lc_g"][0:P, :]), (lc_g[0:DC2, 1:2], ins["lc_g"][P:DC, :]),
                             (lc_b[:, 0:1], ins["lc_b"][0:P, :]), (lc_b[0:DC2, 1:2], ins["lc_b"][P:DC, :]),
                             (g_q[0:DH, :], ins["g_q"]), (g_q[DH:P, :], ins["g_q"]),
                             (g_k[0:DH, :], ins["g_k"]), (g_k[DH:P, :], ins["g_k"])):
                sp.dma_start(dst, src).then_inc(c_in, 16)
            for n in (2, 3):
                load_weights(n)

            def load_context(b):
                sp.dma_start(ctx_n[:], ins["ctx"][b]).then_inc(cx_in, 16)
                sp.dma_start(m_u8[:], ins["mask"][b].partition_broadcast(P)).then_inc(cx_in, 16)
                sp.dma_start(mc_u8[:], ins["mask"][b].rearrange("(n o) -> n o", o=1)).then_inc(cx_in, 16)

            load_context(0)

            def steps_of(sec, a, b, c):
                def a_load():
                    wait(sp, x1_done, a)
                    sp.nop(nofuse=True)
                    sp.dma_start(x_n[:], ins["x"][a].rearrange("(t p) c -> p t c", p=P)).then_inc(xn_in, 16)

                def a_next():
                    sp.wait_ge(x_lo_done, a + 1)
                    sp.nop(nofuse=True)
                    sp.dma_start(x_t[:], ins["x_t"][a + 1].rearrange("(k p) n -> p k n", p=P)).then_inc(xt_in, 16)

                def a_mrow(g):
                    freed(sp, sec, (("a_mrow", g), 0))
                    sp.nop(nofuse=True)
                    sp.dma_start(t2[g % 2][DH:DH + 1, :, :].bitcast(F32), mrow[:, :].bitcast(F32)).then_inc(mr_in[g % 2], 16)

                def b_next():
                    sp.wait_ge(xn_done, (b + 1) * 3)
                    sp.nop(nofuse=True)
                    load_context(b + 1)

                def b_mrow():
                    freed(sp, sec, (("b_mrow",), 0))
                    sp.nop(nofuse=True)
                    sp.dma_start(t2x[DH:DH + 1, :, :].bitcast(F32), mrow_b[:, :].bitcast(F32)).then_inc(mrb_in, 16)

                def c_y():
                    sp.wait_ge(y_done, c + 1)
                    sp.nop(nofuse=True)
                    sp.dma_start(out[c].rearrange("(t p) c -> p t c", p=P), y[:]).then_inc(y_out, 16)

                return dict(w_load=load_weights, a_load=a_load, a_next=a_next, a_mrow=a_mrow, b_next=b_next, b_mrow=b_mrow, c_y=c_y)

            walk(sp, steps_of)
            sp.wait_ge(y_out, 16 * B)

        @block.tensor
        def _(pe):
            mm = nc.tensor.matmul

            def split_product(o, l_hi, l_lo, r_hi, r_lo, start, stop):
                mm(o, l_hi, r_hi, start=start, stop=False)
                mm(o, l_hi, r_lo, start=False, stop=False)
                return mm(o, l_lo, r_hi, start=False, stop=stop)

            def project(o, l_hi, l_lo, name, c0, c1):
                for it in range(NT):
                    rows = slice(it * P, (it + 1) * P)
                    for k in range(KC):
                        ins_ = split_product(o[:, it * D:(it + 1) * D], l_hi[:, k, rows], l_lo[:, k, rows],
                                             weights(w_hi, name, k, c0, c1), weights(w_lo, name, k, c0, c1),
                                             k == 0, k == KC - 1)
                return ins_

            pe.wait_ge(w_lo_done, 2)
            pe.wait_ge(c_in, 16 * 16)
            pe.wait_ge(fill_done, FILLS)

            def steps_of(sec, a, b, c):
                def take(step, n=0):
                    k = sec.bank(step, n)
                    wait(pe, free[k], sec.used(step, n))
                    return bank[k], full[k]

                def w_need(n):
                    pe.wait_ge(w_lo_done, n)
                    if n == len(CHUNKS):
                        pe.wait_ge(const_done, 2)

                def a_proj(u):
                    pe.wait_ge(x_lo_done, a + 1)
                    o, done = take(("a_proj", u))
                    name, c0 = ("kv", {KVU: 0, "V": HKV * DH}[u]) if u in (KVU, "V") else ("q", u * G * DH)
                    project(o, x_hi, x_lo, name, c0, c0 + G * DH).then_inc(done, 1)

                def a_turn(u):
                    n = 0 if u == KVU else u + 1
                    pe.wait_ge(rot_done, a * 5 + n + 1)
                    for half in range(2):
                        o, done = take(("a_turn", u), half)
                        for h in range(2):
                            for it in range(NT):
                                src = rot[:, it * G + half * 2 + h, :, :]
                                ins_ = nc.tensor.transpose(is_head(o, h)[:, it * P:(it + 1) * P], src, ident[:])
                        ins_.then_inc(done, 1)

                def a_max(g, h):
                    if h == 0:
                        pe.wait_ge(t1_done, a * 10 + 2 * g + 4)
                        freed(pe, sec, (("a_turn", KVU), 0), (("a_turn", KVU), 1), then=[(("a_max", g, h), 0)])
                    o, done = take(("a_max", g, h))
                    for it in range(NT):
                        ins_ = mm(o[:, it * N:(it + 1) * N], t1[g % 2][:, h, it * P:(it + 1) * P],
                                  k1[:, g, :], start=True, stop=True)
                    ins_.then_inc(done, 1)

                def a_mrow(g):
                    freed(pe, sec, *((("a_max", g, h), 0) for h in range(G)), then=[(("a_mrow", g), 0)])
                    o, done = take(("a_mrow", g))
                    for it in range(NT):
                        ins_ = nc.tensor.transpose(o[0:G, it * P:(it + 1) * P], mx[g % 2][:, it, :], ident[:])
                    ins_.then_inc(done, 1)

                def a_scores(g, p):
                    if p == 0:
                        freed(pe, sec, (("a_turn", g), 0), (("a_turn", g), 1), then=[(("a_scores", g, 0), 0)])
                        pe.wait_ge(mr_in[g % 2], (a * 2 + (g // 2 + 1)) * 16)
                    for jt in range(NT):
                        o, done = take(("a_scores", g, p), jt)
                        rows = slice(jt * P, (jt + 1) * P)
                        mm(o[:, :], k1[:, g, rows], t1[g % 2][:, 2 * p:2 * p + 2, :], start=True, stop=False)
                        mm(o[:, :], k2[:, g, rows], t2[g % 2][:, 2 * p:2 * p + 2, :], start=False,
                           stop=True).then_inc(done, 1)

                def a_pv(g, p):
                    freed(pe, sec, *((("a_scores", g, p), jt) for jt in range(NT)),
                          *[(("a_proj", "V"), 0)][g:], then=[(("a_pv", g, p), 0)])
                    o, done = take(("a_pv", g, p))
                    for it in range(NT):
                        for h in range(2):
                            c = (it * 2 + h) * VW
                            for jt in range(NT):
                                ins_ = mm(o[:, c:c + VW], prob[p][:, jt, h * N + it * P:h * N + (it + 1) * P],
                                          val[:, jt, g, :], start=(jt == 0), stop=(jt == NT - 1))
                    ins_.then_inc(done, 1)

                def a_ot(g):
                    freed(pe, sec, *((("a_pv", g, p), 0) for p in range(2)), then=[(("a_ot", g), 0)])
                    o, done = take(("a_ot", g))
                    for p in range(2):
                        for it in range(NT):
                            ins_ = nc.tensor.transpose(is_head(o, p)[:, it * P:(it + 1) * P],
                                                       att[:, it, 2 * p:2 * p + 2, :], ident[:])
                    ins_.then_inc(done, 1)

                def a_wo(g):
                    if g == 0:
                        wait(pe, ya_free, a)
                    pe.wait_ge(oh_done, a * 4 + g + 1)
                    freed(pe, sec, (("a_ot", g), 0))
                    for it in range(NT):
                        rows = slice(it * P, (it + 1) * P)
                        for p in range(2):
                            o = bank["YY"][:, it * D:(it + 1) * D]
                            r_hi, r_lo = (weights(w, "o", 2 * g + p, 0, D) for w in (w_hi, w_lo))
                            l_hi, l_lo = att_hi[:, p, rows], att_lo[:, p, rows]
                            mm(o, l_hi, r_hi, start=(g == 0 and it == 0 and p == 0), stop=False, skip_group_check=True)
                            mm(o, l_hi, r_lo, start=False, stop=False, skip_group_check=True)
                            ins_ = mm(o, l_lo, r_hi, start=False, stop=(g == HKV - 1 and p == 1), skip_group_check=True)
                    ins_.then_inc(wo_done, 1)

                def b_zt():
                    pe.wait_ge(z_done, b * 2 + 1)
                    o, done = take(("b_zt",))
                    for k in range(KC):
                        for it in range(NT):
                            ins_ = nc.tensor.transpose(is_head(o, k)[:, it * P:(it + 1) * P],
                                                       z[:, it, k * P:(k + 1) * P], ident[:])
                    ins_.then_inc(done, 1)

                def b_ct():
                    pe.wait_ge(z_done, b * 2 + 2)
                    o, done = take(("b_ct",))
                    nc.tensor.transpose(o[:, 0:NC_], ctx_n[:, 0:P], ident[0:NC_, 0:NC_])
                    nc.tensor.transpose(o[0:DC2, P:P + NC_], ctx_n[:, P:DC],
                                        ident[0:NC_, 0:NC_]).then_inc(done, 1)

                def b_proj(u):
                    pe.wait_ge(zl_done, b * 2 + 1)
                    o, done = take(("b_proj", u))
                    name, c0 = {"q": ("xq", 0), "k": ("xl", 0), "v": ("xl", D)}[u]
                    project(o, z_hi, z_lo, name, c0, c0 + D).then_inc(done, 1)

                def b_cproj():
                    pe.wait_ge(zl_done, b * 2 + 2)
                    o, done = take(("b_cproj",))
                    for k, rows in ((0, P), (1, DC2)):
                        ins_ = split_product(o[0:NC_, :], c_hi[0:rows, k, 0:NC_], c_lo[0:rows, k, 0:NC_],
                                             weights(w_hi, "xc", k, 0, 2 * D)[0:rows], weights(w_lo, "xc", k, 0, 2 * D)[0:rows],
                                             k == 0, k == 1)
                    ins_.then_inc(done, 1)

                def b_turn(u):
                    pe.wait_ge(xn_done, b * 3 + {"q": 1, "k": 2, "c": 3}[u])
                    if u == "c":
                        o, done = take(("b_turn", u))
                        for h in range(HX):
                            src = xn[0:NC_, h, :, :]
                            ins_ = nc.tensor.transpose(o[:, h * NCP:h * NCP + NC_], src, ident[0:NC_, 0:NC_])
                        ins_.then_inc(done, 1)
                        return
                    for half in range(2):
                        o, done = take(("b_turn", u), half)
                        for h in range(2):
                            for it in range(NT):
                                src = xn[:, it * HX + half * 2 + h, :, :]
                                ins_ = nc.tensor.transpose(is_head(o, h)[:, it * P:(it + 1) * P], src, ident[:])
                        ins_.then_inc(done, 1)

                def b_max(h):
                    o, done = take(("b_max", h))
                    for it in range(NT):
                        ins_ = mm(o[:, it * N:(it + 1) * N], t1x[:, h, it * P:(it + 1) * P],
                                  k1x[:, h, 0:N], start=True, stop=True)
                    ins_.then_inc(done, 1)

                def b_maxc(p):
                    if p == 0:
                        turns = (("b_turn", "q"), ("b_turn", "k"), ("b_turn", "c"))
                        freed(pe, sec, *((step, n) for step in turns for n in range(banks_of(step))),
                              then=[(("b_maxc", p), 0)])
                    o, done = take(("b_maxc", p))
                    for h in range(2):
                        for it in range(NT):
                            c = (h * NT + it) * NCP
                            ins_ = mm(o[:, c:c + NCP], t1x[:, 2 * p + h, it * P:(it + 1) * P],
                                      k1x[:, 2 * p + h, N:N + NCP], start=True, stop=True)
                    ins_.then_inc(done, 1)

                def b_mrow():
                    pe.wait_ge(mb_done, b + 1)
                    o, done = take(("b_mrow",))
                    for it in range(NT):
                        ins_ = nc.tensor.transpose(o[0:HX, it * P:(it + 1) * P], mx_b[:, it, :], ident[:])
                    ins_.then_inc(done, 1)

                def b_scores(p):
                    if p == 0:
                        pe.wait_ge(mrb_in, (b + 1) * 16)
                    for jt in range(NT + 1):
                        o, done = take(("b_scores", p), jt)
                        m = P if jt < NT else NC_
                        for h in range(2):
                            keys = slice(jt * P, jt * P + m)
                            dst = o[0:m, h * N:(h + 1) * N]
                            mm(dst, k1x[:, 2 * p + h, keys], t1x[:, 2 * p + h, :], start=True, stop=False)
                            ins_ = mm(dst, k2x[:, 2 * p + h, keys], t2x[:, 2 * p + h, :], start=False, stop=True)
                        ins_.then_inc(done, 1)

                def b_pv(p):
                    freed(pe, sec, *((("b_scores", p), jt) for jt in range(NT + 1)),
                          *[(("b_proj", "v"), 0)][p:], then=[(("b_pv", p), 0)])
                    o, done = take(("b_pv", p))
                    for it in range(NT):
                        for h in range(2):
                            c = (it * 2 + h) * VW
                            for jt in range(NT + 1):
                                m = P if jt < NT else NC_
                                ins_ = mm(o[:, c:c + VW], probx[0:m, jt, h * N + it * P:h * N + (it + 1) * P],
                                          valx[0:m, jt, 2 * p + h, :], start=(jt == 0), stop=(jt == NT))
                    ins_.then_inc(done, 1)

                def b_ot():
                    freed(pe, sec, *((("b_pv", p), 0) for p in range(HX // 2)), then=[(("b_ot",), 0)])
                    o, done = take(("b_ot",))
                    for k in range(KC):
                        for it in range(NT):
                            ins_ = nc.tensor.transpose(is_head(o, k)[:, it * P:(it + 1) * P],
                                                       attx[:, it, 2 * k:2 * k + 2, :], ident[:])
                    ins_.then_inc(done, 1)

                def b_wo():
                    freed(pe, sec, (("b_ot",), 0), then=[(("b_wo",), 0)])
                    o, done = take(("b_wo",))
                    project(o, attx_hi, attx_lo, "xo", 0, D).then_inc(done, 1)

                def c_x2t():
                    pe.wait_ge(x2_done, c + 1)
                    o, done = take(("c_x2t",))
                    for k in range(KC):
                        for it in range(NT):
                            ins_ = nc.tensor.transpose(is_head(o, k)[:, it * P:(it + 1) * P],
                                                       x2[:, it, k * P:(k + 1) * P], ident[:])
                    ins_.then_inc(done, 1)

                def c_gate():
                    freed(pe, sec, (("c_x2t",), 0), then=[(("c_gate",), 0)])
                    o, done = take(("c_gate",))
                    for it in range(NT):
                        rows = slice(it * P, (it + 1) * P)
                        for k in range(KC):
                            ins_ = split_product(o[:, it * E:(it + 1) * E], x2_hi[:, k, rows], x2_lo[:, k, rows],
                                                 weights(w_hi, "gate", k, 0, E), weights(w_lo, "gate", k, 0, E),
                                                 k == 0, k == KC - 1)
                    ins_.then_inc(done, 1)

                def c_expert(e):
                    o, done = take(("c_expert", e))
                    project(o, x2_hi, x2_lo, "ex", e * D, (e + 1) * D).then_inc(done, 1)

                return dict(w_need=w_need, a_proj=a_proj, a_turn=a_turn, a_max=a_max, a_mrow=a_mrow, a_scores=a_scores,
                            a_pv=a_pv, a_ot=a_ot, a_wo=a_wo, b_zt=b_zt, b_ct=b_ct, b_proj=b_proj,
                            b_cproj=b_cproj, b_turn=b_turn, b_max=b_max, b_maxc=b_maxc, b_mrow=b_mrow,
                            b_scores=b_scores, b_pv=b_pv, b_ot=b_ot, b_wo=b_wo, c_x2t=c_x2t,
                            c_gate=c_gate, c_expert=c_expert)

            walk(pe, steps_of)

        @block.scalar
        def _(act):
            run = nc.scalar.activation
            def w_split(n):
                at, cols, st, count = chunk(n)
                act.wait_ge(w_in[st], count)
                run(w_hi[:, at:at + cols], stage[st][:, 0:cols], ACT.Copy).then_inc(w_hi_done, 1)

            def w_need(n):
                act.wait_ge(w_lo_done, n)

            def x_split(a):
                act.wait_ge(xt_in, (a + 1) * 16)
                run(x_hi[:], x_t[:], ACT.Copy).then_inc(x_hi_done, 1)

            x_split(0)
            w_split(0)
            w_split(1)
            act.wait_ge(c_in, 16 * 16)

            def steps_of(sec, a, b, c):
                def filled(step, n=0):
                    k = sec.bank(step, n)
                    act.wait_ge(full[k], sec.used(step, n) + 1)
                    return bank[k], free[k]

                def a_split():
                    was_filled(act, sec, *((("a_proj", u), 0) for u in (KVU, "V", HKV - 1)))
                    act.nop(nofuse=True)
                    x_split(a + 1)

                def a_proj(u):
                    if u != "V":
                        return
                    wait(act, wo_done, a * 4)
                    o, done = filled(("a_proj", u))
                    run(val[:, :, :, 0:DH], o[:, :].rearrange("p (t h d) -> p t h d", t=NT, h=HKV),
                        ACT.Copy).then_inc(done, 1)

                def a_turn(u):
                    if u == KVU or u < 2:
                        wait(act, wo_done, a * 4)
                    else:
                        was_filled(act, sec, (("a_scores", u - 2, 1), 1), then=[(("a_turn", u), 0)])
                    for half in range(2):
                        o, _ = filled(("a_turn", u), half)
                        heads = slice(2 * half, 2 * half + 2)
                        if u == KVU:
                            run(k2[0:DH, heads, :], o[0:DH, :].rearrange("p (h n) -> p h n", h=2), ACT.Copy)
                            run(k1[:, heads, :], o[:, :].rearrange("p (h n) -> p h n", h=2),
                                ACT.Copy).then_inc(t1_done, 1)
                        else:
                            run(t1[u % 2][:, heads, :], o[:, :].rearrange("p (h n) -> p h n", h=2),
                                ACT.Copy).then_inc(t1_done, 1)

                def a_mrow(g):
                    o, done = filled(("a_mrow", g))
                    wait(act, mr_in[(g - 1) % 2], (a * 2 + (g + 1) // 2) * 16)
                    run(mrow[:, :], o[0:G, 0:N], ACT.Copy, scale=-1.0).then_inc(done, 1)

                def a_scores(g, p):
                    if g == 0:
                        wait(act, wo_done, a * 4)
                    else:
                        was_filled(act, sec, (("a_pv", g - 1, p), 0), then=[(("a_scores", g, p), 0)])
                    for jt in range(NT):
                        o, done = filled(("a_scores", g, p), jt)
                        run(prob[p][:, jt, :], o[:, :], ACT.Exp, scale=SCALE).then_inc(done, 1)

                def a_ot(g):
                    o, _ = filled(("a_ot", g))
                    wait(act, wo_done, a * 4 + g)
                    run(att_hi[:], o[:, :].rearrange("p (h n) -> p h n", h=2),
                        ACT.Copy).then_inc(oh_done, 1)

                def b_zt():
                    o, done = filled(("b_zt",))
                    wait(act, x2_done, b)
                    for k in range(KC):
                        ins_ = run(zf[:, k, :], is_head(o, k), ACT.Identity, bias=ln_b[:, k:k + 1],
                                   scale=ln_g[:, k:k + 1])
                    ins_.then_inc(done, 1)
                    freed(act, sec, (("b_zt",), 0))
                    run(z_hi[:], zf[:], ACT.Copy).then_inc(zh_done, 1)

                def b_ct():
                    o, done = filled(("b_ct",))
                    run(cf[:, 0, 0:NC_], o[:, 0:NC_], ACT.Identity, bias=lc_b[:, 0:1], scale=lc_g[:, 0:1])
                    run(cf[0:DC2, 1, 0:NC_], o[0:DC2, P:P + NC_], ACT.Identity, bias=lc_b[0:DC2, 1:2],
                        scale=lc_g[0:DC2, 1:2]).then_inc(done, 1)
                    freed(act, sec, (("b_ct",), 0))
                    run(c_hi[:, 0, 0:NC_], cf[:, 0, 0:NC_], ACT.Copy)
                    run(c_hi[0:DC2, 1, 0:NC_], cf[0:DC2, 1, 0:NC_], ACT.Copy).then_inc(zh_done, 1)

                def b_proj(u):
                    o, done = filled(("b_proj", u))
                    if u == "v":
                        run(valx[:, 0:NT, :, 0:DH], o[:, :].rearrange("p (t h d) -> p t h d", t=NT, h=HX),
                            ACT.Copy).then_inc(done, 1)
                    else:
                        run(sq[{"q": 0, "k": 1}[u]][:], o[:, :], ACT.Square).then_inc(sq_done, 1)

                def b_cproj():
                    o, _ = filled(("b_cproj",))
                    run(valx[0:NC_, NT, :, 0:DH], o[0:NC_, D:2 * D].rearrange("p (h d) -> p h d", h=HX), ACT.Copy)
                    run(sq[2][0:NC_, 0:D], o[0:NC_, 0:D], ACT.Square).then_inc(sq_done, 1)

                def b_turn(u):
                    for half in range(banks_of(("b_turn", u))):
                        o, _ = filled(("b_turn", u), half)
                        heads = slice(2 * half, 2 * half + 2)
                        if u == "c":
                            src = o[:, 0:HX * NCP].rearrange("p (h n) -> p h n", h=HX)[:, :, 0:NC_]
                            heads, keys = slice(0, HX), slice(N, N + NC_)
                        else:
                            src, keys = o[:, :].rearrange("p (h n) -> p h n", h=2), slice(0, N)
                        if u == "q":
                            run(t1x[:, heads, :], src, ACT.Copy, scale=g_q[:, 0:1]).then_inc(tx_done, 1)
                        else:
                            run(k2x[0:DH, heads, keys], src[0:DH], ACT.Copy, scale=g_k[0:DH, 0:1])
                            run(k1x[:, heads, keys], src, ACT.Copy, scale=g_k[:, 0:1]).then_inc(tx_done, 1)

                def b_mrow():
                    o, done = filled(("b_mrow",))
                    run(mrow_b[:, :], o[0:HX, 0:N], ACT.Copy, scale=-1.0).then_inc(done, 1)

                def b_scores(p):
                    if p:
                        was_filled(act, sec, (("b_pv", p - 1), 0), then=[(("b_scores", p), 0)])
                    for jt in range(NT + 1):
                        o, done = filled(("b_scores", p), jt)
                        if jt < NT:
                            run(probx[:, jt, :], o[:, :], ACT.Exp, scale=SCALE).then_inc(done, 1)
                        else:
                            run(probx[0:NC_, jt, :], o[0:NC_, :], ACT.Exp, bias=mc_neg[:, 0:1],
                                scale=SCALE).then_inc(done, 1)

                def b_ot():
                    o, _ = filled(("b_ot",))
                    run(attx_hi[:], o[:, :].rearrange("p (h n) -> p h n", h=2), ACT.Copy).then_inc(ohx_done, 1)

                def c_x2t():
                    o, _ = filled(("c_x2t",))
                    wait(act, y_done, c)
                    run(x2_hi[:], o[:, :].rearrange("p (h n) -> p h n", h=2), ACT.Copy).then_inc(x2h_done, 1)

                def c_route():
                    act.wait_ge(dif_done, c + 1)
                    run(top[:, 3, :], top[:, 2, :], ACT.Exp).then_inc(exp_done, 1)

                return dict(w_split=w_split, w_need=w_need, a_split=a_split, a_proj=a_proj, a_turn=a_turn,
                            a_mrow=a_mrow, a_scores=a_scores, a_ot=a_ot, b_zt=b_zt, b_ct=b_ct, b_proj=b_proj,
                            b_cproj=b_cproj, b_turn=b_turn, b_mrow=b_mrow, b_scores=b_scores, b_ot=b_ot,
                            c_x2t=c_x2t, c_route=c_route)

            walk(act, steps_of)

        @block.gpsimd
        def _(pool):
            tt = nc.gpsimd.tensor_tensor
            for n, (t, value) in enumerate(fixed):
                nc.gpsimd.memset(t, value).then_inc(fill_done, 1)
                pool.wait_ge(fill_done, n + 1)

            def w_load(n):
                if n == len(CHUNKS) - 1:
                    pool.wait_ge(w_lo_done, n - 1)
                    nc.gpsimd.memset(stage[0][:, 2 * D:4 * D], 0.0).then_inc(const_done, 1)

            def w_need(n):
                if n == len(CHUNKS):
                    pool.wait_ge(w_lo_done, n)
                    nc.gpsimd.memset(valx[:, :, :, DH:VW], 1.0).then_inc(const_done, 1)
                    pool.wait_ge(const_done, 2)

            def steps_of(sec, a, b, c):
                def a_rot(u):
                    freed(pool, sec, (("a_proj", u), 0))
                    if u == KVU:
                        wait(pool, wo_done, a * 4)
                    else:
                        was_filled(pool, sec, (("a_turn", KVU if u == 0 else u - 1), 1))
                    for twice in range(2):
                        ins_ = tt(rot[:, :, twice, :], rot_c[:].rearrange("p t h d -> p (t h) d"),
                                  rot_s[:].rearrange("p t h d -> p (t h) d"), ALU.add)
                    ins_.then_inc(rot_done, 1)

                def power(n, rows, src, dst, cols, done_in, done_out, count):
                    pool.wait_ge(done_in, count)
                    tt(dst[0:rows, 0:cols], src[0:rows, 0:cols], half_neg[0:rows, 0:cols],
                       ALU.pow).then_inc(done_out, 1)

                def a_res():
                    power(0, P, ve_a, rs_a, NT, va_done, ra_done, a + 1)

                def b_norm(n, rows, src, dst, cols):
                    power(n, rows, src, dst, cols, vb_done, rb_done, b * B_NORMS + n + 1)

                def b_ln():
                    b_norm(0, P, ve_b, rs_b, NT)

                def b_cln():
                    b_norm(1, NC_, ve_c, rs_c, 1)

                def b_ss(u):
                    n = "qkc".index(u)
                    b_norm(2 + n, NC_ if u == "c" else P, ss[n], ri[n], HX if u == "c" else NT * HX)

                def b_res():
                    b_norm(5, P, ve_b, rs_b, NT)

                def c_out():
                    power(0, P, ve_y, rs_y, NT, vc_done, rc_done, c + 1)

                def b_zt():
                    pool.wait_ge(zh_done, b * 2 + 1)
                    tt(z_lo[:], zf[:], z_hi[:], ALU.subtract).then_inc(zl_done, 1)

                def b_ct():
                    pool.wait_ge(zh_done, b * 2 + 2)
                    tt(c_lo[:, 0, 0:NC_], cf[:, 0, 0:NC_], c_hi[:, 0, 0:NC_], ALU.subtract)
                    tt(c_lo[0:DC2, 1, 0:NC_], cf[0:DC2, 1, 0:NC_], c_hi[0:DC2, 1, 0:NC_],
                       ALU.subtract).then_inc(zl_done, 1)

                return dict(w_load=w_load, w_need=w_need, a_rot=a_rot, a_res=a_res, b_ln=b_ln, b_cln=b_cln,
                            b_ss=b_ss, b_res=b_res, b_zt=b_zt, b_ct=b_ct, c_out=c_out)

            walk(pool, steps_of)

        @block.vector
        def _(dve):
            v = nc.vector
            def w_split(n):
                at, cols, st, _ = chunk(n)
                dve.wait_ge(w_hi_done, n + 1)
                v.tensor_tensor(w_lo[:, at:at + cols], stage[st][:, 0:cols], w_hi[:, at:at + cols],
                                ALU.subtract).then_inc(w_lo_done, 1)

            def x_split(a):
                dve.wait_ge(x_hi_done, a + 1)
                v.tensor_tensor(x_lo[:], x_t[:], x_hi[:], ALU.subtract).then_inc(x_lo_done, 1)

            x_split(0)
            w_split(0)
            w_split(1)
            dve.wait_ge(c_in, 16 * 16)

            def steps_of(sec, a, b, c):
                count = {"a": 0, "b": 0, "c": 0}

                def link(ins_, s):
                    count[s] += 1
                    chain, at, per = {"a": (dve_a, a, A_LINKS), "b": (dve_b, b, B_LINKS), "c": (dve_c, c, C_LINKS)}[s]
                    ins_.then_inc(chain, 1)
                    dve.wait_ge(chain, at * per + count[s])

                def filled(step, n=0):
                    k = sec.bank(step, n)
                    dve.wait_ge(full[k], sec.used(step, n) + 1)
                    return bank[k], free[k]

                def stats(s, src, rows, tiles, st, mv, ve):
                    for t in range(tiles):
                        ins_ = v.bn_stats(st[0:rows, t, :], src[t])
                    link(ins_, s)
                    dve.nop(nofuse=True)
                    for t in range(tiles):
                        ins_ = v.bn_aggr(mv[0:rows, t, :], st[0:rows, t, :])
                    link(ins_, s)
                    return v.tensor_scalar(ve[0:rows, 0:tiles], mv[0:rows, 0:tiles, 1], LN_EPS, None, ALU.add)

                def normed(dst, src, rows, tiles, mv, rs):
                    for t in range(tiles):
                        ins_ = v.tensor_scalar(dst[t], src[t], mv[0:rows, t, 0:1], rs[0:rows, t:t + 1],
                                               ALU.subtract, ALU.mult)
                    return ins_

                def tiles_of(t):
                    return [t[:, it, :] for it in range(NT)]

                def a_split():
                    x_split(a + 1)

                def a_proj(u):
                    if u == "V":
                        return
                    n = 0 if u == KVU else u + 1
                    o, done = filled(("a_proj", u))
                    wait(dve, rot_done, a * 5 + n)
                    q4 = o[:, :].rearrange("p (t h d) -> p t h d", t=NT, h=G)

                    def table(t, lo, hi):
                        return t[:, :, lo:hi].unsqueeze(2).to_broadcast([P, NT, G, hi - lo])

                    hw = DH // 2
                    v.tensor_tensor(rot_c[:], q4, table(cos_t, 0, DH), ALU.mult)
                    v.tensor_tensor(rot_s[:, :, :, 0:hw], q4[:, :, :, hw:DH], table(sin_t, 0, hw), ALU.mult)
                    v.tensor_tensor(rot_s[:, :, :, hw:DH], q4[:, :, :, 0:hw], table(sin_t, hw, DH),
                                    ALU.mult).then_inc(done, 1)

                def a_lo(u):
                    n = 0 if u == KVU else u + 1
                    for half in range(2):
                        o, done = filled(("a_turn", u), half)
                        heads = slice(2 * half, 2 * half + 2)
                        dve.wait_ge(t1_done, a * 10 + 2 * n + half + 1)
                        src = o[:, :].rearrange("p (h n) -> p h n", h=2)
                        if u == KVU:
                            ins_ = v.tensor_tensor(k1[DH:P, heads, :], src[DH:P], k1[DH:P, heads, :], ALU.subtract)
                        else:
                            ins_ = v.tensor_tensor(t2[u % 2][0:DH, heads, :], src[0:DH], t1[u % 2][0:DH, heads, :],
                                                   ALU.subtract)
                        ins_.then_inc(done, 1)

                def a_max(g, h):
                    o, done = filled(("a_max", g, h))
                    if h == 0 and g >= 2:
                        was_filled(dve, sec, (("a_mrow", g - 2), 0), then=[(("a_max", g, h), 0)])
                    elif h == 0:
                        wait(dve, wo_done, a * 4)
                    v.tensor_reduce(mx[g % 2][:, :, h], o[:, :].rearrange("p (t n) -> p t n", t=NT),
                                    AX.X, ALU.max).then_inc(done, 1)

                def over_sum(dst, step, rd, s):
                    o, done = filled(step)
                    o4 = o[:, 0:2 * NT * VW].rearrange("p (t h d) -> p t h d", t=NT, h=2)
                    link(v.reciprocal(rd[:], o4[:, :, :, DH]), s)
                    v.tensor_tensor(dst, o4[:, :, :, 0:DH], rd[:].unsqueeze(3).to_broadcast([P, NT, 2, DH]),
                                    ALU.mult).then_inc(done, 1)

                def a_pv(g, p):
                    if p == 0:
                        wait(dve, oh_done, a * 4 + g)
                    over_sum(att[:, :, 2 * p:2 * p + 2, :], ("a_pv", g, p), rden[p], "a")

                def a_otlo(g):
                    o, done = filled(("a_ot", g))
                    dve.wait_ge(oh_done, a * 4 + g + 1)
                    v.tensor_tensor(att_lo[:], o[:, :].rearrange("p (h n) -> p h n", h=2),
                                    att_hi[:], ALU.subtract).then_inc(done, 1)

                def a_res():
                    dve.wait_ge(wo_done, (a + 1) * 4)
                    dve.wait_ge(xn_in, (a + 1) * 16)
                    v.tensor_tensor(x_n[:], bank["YY"][:, :].rearrange("p (t c) -> p t c", t=NT), x_n[:],
                                    ALU.add).then_inc(ya_free, 1)
                    dve.wait_ge(ya_free, a + 1)
                    link(v.tensor_tensor(x_n[:], x_n[:], bo[:].unsqueeze(1).to_broadcast([P, NT, D]), ALU.add), "a")
                    stats("a", tiles_of(x_n), P, NT, st_a, mv_a, ve_a).then_inc(va_done, 1)

                def a_norm():
                    dve.wait_ge(ra_done, a + 1)
                    if b is not None:
                        dve.wait_ge(x2_done, b + 1)
                    normed(tiles_of(x1), tiles_of(x_n), P, NT, mv_a, rs_a).then_inc(x1_done, 1)
                    check("a")

                def b_ln():
                    dve.wait_ge(x1_done, b + 1)
                    stats("b", tiles_of(x1), P, NT, st_b, mv_b, ve_b).then_inc(vb_done, 1)

                def b_z():
                    dve.wait_ge(rb_done, b * B_NORMS + 1)
                    wait(dve, x2_done, b)
                    normed(tiles_of(z), tiles_of(x1), P, NT, mv_b, rs_b).then_inc(z_done, 1)

                def b_cln():
                    dve.wait_ge(cx_in, (b + 1) * 48)
                    v.tensor_scalar(m_neg[:], m_u8[:], 1.0, MASKED, ALU.subtract, ALU.mult)
                    link(v.tensor_scalar(mc_neg[:], mc_u8[:], 1.0, MASKED, ALU.subtract, ALU.mult), "b")
                    stats("b", [ctx_n[:]], NC_, 1, st_c, mv_c, ve_c).then_inc(vb_done, 1)

                def b_cn():
                    dve.wait_ge(rb_done, b * B_NORMS + 2)
                    normed([ctx_n[:]], [ctx_n[:]], NC_, 1, mv_c, rs_c).then_inc(z_done, 1)

                def b_ss(u):
                    n = "qkc".index(u)
                    rows, cols = (NC_, HX) if u == "c" else (P, NT * HX)
                    dve.wait_ge(sq_done, b * 3 + n + 1)
                    link(v.tensor_reduce(ss[n][0:rows, 0:cols], sq[n][0:rows, 0:cols * DH].rearrange("p (h d) -> p h d", d=DH),
                                         AX.X, ALU.add), "b")
                    v.tensor_scalar(ss[n][0:rows, 0:cols], ss[n][0:rows, 0:cols], 1.0 / DH, RMS_FLOOR,
                                    ALU.mult, ALU.max).then_inc(vb_done, 1)

                def b_xn(u):
                    n = "qkc".index(u)
                    rows, cols = (NC_, HX) if u == "c" else (P, NT * HX)
                    step = ("b_cproj",) if u == "c" else ("b_proj", u)
                    o, done = bank[sec.bank(step)], free[sec.bank(step)]
                    src = o[0:rows, 0:cols * DH].rearrange("p (h d) -> p h d", d=DH)
                    was_filled(dve, sec, (step, 0))
                    dve.wait_ge(rb_done, b * B_NORMS + n + 3)
                    dve.nop(nofuse=True)
                    if n:
                        was_filled(dve, sec, (("b_turn", "qkc"[n - 1]), 1))
                    else:
                        wait(dve, ohx_done, b)
                    v.tensor_tensor(xn[0:rows, 0:cols], src.unsqueeze(2).to_broadcast([rows, cols, 2, DH]),
                                    ri[n][0:rows, 0:cols].unsqueeze(2).unsqueeze(2).to_broadcast([rows, cols, 2, DH]),
                                    ALU.mult).then_inc(xn_done, 1)
                    dve.wait_ge(xn_done, b * 3 + n + 1)
                    dve.sem_inc(done, 1)

                def b_lo(u):
                    for half in range(banks_of(("b_turn", u))):
                        o, done = filled(("b_turn", u), half)
                        n = {"q": 0, "k": 2, "c": 4}[u] + half
                        dve.wait_ge(tx_done, b * 5 + n + 1)
                        heads = slice(2 * half, 2 * half + 2)
                        if u == "c":
                            src = o[:, 0:HX * NCP].rearrange("p (h n) -> p h n", h=HX)[:, :, 0:NC_]
                            heads, keys = slice(0, HX), slice(N, N + NC_)
                        else:
                            src, keys = o[:, :].rearrange("p (h n) -> p h n", h=2), slice(0, N)
                        if u == "q":
                            ins_ = v.scalar_tensor_tensor(t2x[0:DH, heads, :], src[0:DH], g_q[0:DH, 0:1],
                                                          t1x[0:DH, heads, :], ALU.mult, ALU.subtract)
                        else:
                            ins_ = v.scalar_tensor_tensor(k1x[DH:P, heads, keys], src[DH:P], g_k[DH:P, 0:1],
                                                          k1x[DH:P, heads, keys], ALU.mult, ALU.subtract)
                        ins_.then_inc(done, 1)

                def b_max(h):
                    o, done = filled(("b_max", h))
                    v.tensor_reduce(mx_l[:, :, h], o[:, :].rearrange("p (t n) -> p t n", t=NT),
                                    AX.X, ALU.max).then_inc(done, 1)

                def b_maxc(p):
                    o, done = filled(("b_maxc", p))
                    v.tensor_tensor(sc_c[:], o[:, 0:2 * NT * NCP].rearrange("p (h t n) -> p h t n", h=2, t=NT)[:, :, :, 0:NC_],
                                    m_neg[:].unsqueeze(1).unsqueeze(1).to_broadcast([P, 2, NT, NC_]), ALU.add).then_inc(done, 1)
                    freed(dve, sec, (("b_maxc", p), 0))
                    link(v.tensor_reduce(mx_c[:].rearrange("p t h -> p h t")[:, 2 * p:2 * p + 2, :], sc_c[:],
                                         AX.X, ALU.max), "b")

                def b_mrow():
                    freed(dve, sec, *((("b_max", h), 0) for h in range(HX)))
                    v.tensor_tensor(mx_b[:], mx_l[:], mx_c[:], ALU.max).then_inc(mb_done, 1)

                def b_pv(p):
                    if p == 0:
                        was_filled(dve, sec, (("b_turn", "c"), 0), then=[(("b_pv", 0), 0)])
                    over_sum(attx[:, :, 2 * p:2 * p + 2, :], ("b_pv", p), rden_b[p], "b")

                def b_otlo():
                    o, done = filled(("b_ot",))
                    dve.wait_ge(ohx_done, b + 1)
                    v.tensor_tensor(attx_lo[:], o[:, :].rearrange("p (h n) -> p h n", h=2), attx_hi[:],
                                    ALU.subtract).then_inc(done, 1)

                def b_res():
                    o, done = filled(("b_wo",))
                    v.tensor_tensor(x1[:], o[:, :].rearrange("p (t c) -> p t c", t=NT), x1[:], ALU.add).then_inc(done, 1)
                    freed(dve, sec, (("b_wo",), 0))
                    link(v.tensor_tensor(x1[:], x1[:], xbo[:].unsqueeze(1).to_broadcast([P, NT, D]), ALU.add), "b")
                    stats("b", tiles_of(x1), P, NT, st_b, mv_b, ve_b).then_inc(vb_done, 1)

                def b_x2():
                    dve.wait_ge(rb_done, b * B_NORMS + 6)
                    wait(dve, y_out, b * 16)
                    normed(tiles_of(x2), tiles_of(x1), P, NT, mv_b, rs_b).then_inc(x2_done, 1)
                    check("b")

                def c_x2lo():
                    o, done = filled(("c_x2t",))
                    dve.wait_ge(x2h_done, c + 1)
                    v.tensor_tensor(x2_lo[:], o[:, :].rearrange("p (h n) -> p h n", h=2), x2_hi[:],
                                    ALU.subtract).then_inc(done, 1)

                def c_route():
                    o, done = filled(("c_gate",))
                    v.tensor_copy(lg[:], o[:, 0:NT * E].rearrange("p (t e) -> p t e", t=NT)).then_inc(done, 1)
                    freed(dve, sec, (("c_gate",), 0))
                    own = lg[:].unsqueeze(3).to_broadcast([P, NT, E, E])
                    other = lg[:].unsqueeze(2).to_broadcast([P, NT, E, E])
                    v.tensor_tensor(gt[:], other, own, ALU.is_gt)
                    link(v.tensor_tensor(eq[:], other, own, ALU.is_equal), "c")
                    link(v.tensor_tensor(eq[:], eq[:], before[:].unsqueeze(1).to_broadcast([P, NT, E, E]), ALU.mult), "c")
                    link(v.tensor_tensor(gt[:], gt[:], eq[:], ALU.add), "c")
                    link(v.tensor_reduce(rank[:], gt[:], AX.X, ALU.add), "c")
                    v.tensor_scalar(sel0[:], rank[:], 0.0, None, ALU.is_equal)
                    link(v.tensor_scalar(sel1[:], rank[:], 1.0, None, ALU.is_equal), "c")
                    v.tensor_reduce(top[:, 0, :], lg[:], AX.X, ALU.max)
                    link(v.tensor_tensor(gate[:], lg[:], sel1[:], ALU.mult), "c")
                    link(v.tensor_reduce(top[:, 1, :], gate[:], AX.X, ALU.add), "c")
                    v.tensor_tensor(top[:, 2, :], top[:, 1, :], top[:, 0, :], ALU.subtract).then_inc(dif_done, 1)

                def c_weights():
                    dve.wait_ge(exp_done, c + 1)
                    link(v.tensor_scalar(top[:, 4, :], top[:, 3, :], 1.0, None, ALU.add), "c")
                    link(v.reciprocal(top[:, 4, :], top[:, 4, :]), "c")
                    link(v.tensor_tensor(top[:, 5, :], top[:, 4, :], top[:, 3, :], ALU.mult), "c")
                    v.tensor_tensor(sel0[:], sel0[:], top[:, 4, :].unsqueeze(2).to_broadcast([P, NT, E]), ALU.mult)
                    link(v.tensor_tensor(sel1[:], sel1[:], top[:, 5, :].unsqueeze(2).to_broadcast([P, NT, E]), ALU.mult), "c")
                    link(v.tensor_tensor(gate[:], sel0[:], sel1[:], ALU.add), "c")

                def c_expert(e):
                    o, done = filled(("c_expert", e))
                    if e:
                        freed(dve, sec, (("c_expert", e - 1), 0))
                    for it in range(NT):
                        ins_ = v.scalar_tensor_tensor(acc[:, it, :], o[:, it * D:(it + 1) * D], gate[:, it, e:e + 1],
                                                      acc[:, it, :], ALU.mult, ALU.add)
                    ins_.then_inc(done, 1)

                def c_out():
                    freed(dve, sec, (("c_expert", E - 1), 0))
                    stats("c", tiles_of(acc), P, NT, st_y, mv_y, ve_y).then_inc(vc_done, 1)

                def c_y():
                    dve.wait_ge(rc_done, c + 1)
                    normed(tiles_of(y), tiles_of(acc), P, NT, mv_y, rs_y).then_inc(y_done, 1)
                    check("c")

                def check(s):
                    want = {"a": A_LINKS, "b": B_LINKS, "c": C_LINKS}[s]
                    assert count[s] == want, (s, count[s])

                return dict(w_split=w_split, a_split=a_split, a_proj=a_proj, a_lo=a_lo, a_max=a_max, a_pv=a_pv,
                            a_otlo=a_otlo, a_res=a_res, a_norm=a_norm, b_ln=b_ln, b_z=b_z, b_cln=b_cln, b_cn=b_cn,
                            b_ss=b_ss, b_xn=b_xn, b_lo=b_lo, b_max=b_max, b_maxc=b_maxc, b_mrow=b_mrow,
                            b_pv=b_pv, b_otlo=b_otlo, b_res=b_res, b_x2=b_x2, c_x2lo=c_x2lo, c_route=c_route,
                            c_weights=c_weights, c_expert=c_expert, c_out=c_out, c_y=c_y)

            walk(dve, steps_of)


def tables():
    inv = (np.float32(1.0) / np.float32(10000.0) ** (np.arange(0, DH, 2, dtype=np.float32) / np.float32(DH))).astype(np.float32)
    ang = np.arange(N, dtype=np.float32)[:, None] * inv[None, :]
    cos, sin = np.cos(ang).astype(np.float32), np.sin(ang).astype(np.float32)
    return {"cos": np.concatenate([cos, cos], 1), "sin": np.concatenate([-sin, sin], 1),
            "ident": np.eye(P, dtype=np.float32), "before": np.tril(np.ones((E, E), np.float32), -1)}


def kernel(**inputs):
    import concourse.bacc as bacc
    from concourse.bass_utils import run_bass_kernel_spmd

    i = {k: np.asarray(v) for k, v in inputs.items()}
    x = i["x"]
    arrays = {
        "x": x, "x_t": np.concatenate([x.transpose(0, 2, 1), np.zeros((1, D, N), x.dtype)]), "ctx": i["ctx_768"], "mask": i["mask_BxS2_bk0"],
        "q": i["L0_attn_Wq"], "kv": i["L0_attn_Wkv"], "o": i["L0_attn_Wo"],
        "xq": i["L0_xattn_Wq"].T, "xl": i["L0_xattn_Wlkv"].T, "xo": i["L0_xattn_Wo"].T, "xc": i["L0_xattn_Wkv"].T,
        "ex": i["L0_ffn_expert_w"].transpose(2, 0, 1).reshape(D, E * D), "gate": i["L0_ffn_gate_w"].T,
        "bo": i["L0_attn_bo"], "xbo": i["L0_xattn_bo"],
        "ln_g": i["L0_xattn_ln_l_g"].reshape(KC, P).T, "ln_b": i["L0_xattn_ln_l_b"].reshape(KC, P).T,
        "lc_g": i["L0_xattn_ln_x_g"].reshape(DC, 1), "lc_b": i["L0_xattn_ln_x_b"].reshape(DC, 1),
        "g_q": i["L0_xattn_qn_g"].reshape(DH, 1), "g_k": i["L0_xattn_kn_g"].reshape(DH, 1),
        **tables(),
    }
    nc = bacc.Bacc("TRN2", target_bir_lowering=False, num_devices=1)
    feeds, ins = {}, {}
    for name, a in arrays.items():
        a = np.ascontiguousarray(a)
        feeds[f"{name}_dram"] = a
        ins[name] = nc.dram_tensor(f"{name}_dram", a.shape, mybir.dt.from_np(a.dtype), kind="ExternalInput").ap()
    out = nc.dram_tensor("out_dram", (B, N, D), F32, kind="ExternalOutput").ap()
    build(nc, ins, out)
    r = run_bass_kernel_spmd(nc, [feeds], core_ids=[0])
    return r.results[0]["out_dram"]
```

```python
from contextlib import ExitStack

import numpy as np
import concourse.bass as bass
from concourse import mybir

F32 = mybir.dt.float32
F32R = mybir.dt.float32r
U8 = mybir.dt.uint8
ALU = mybir.AluOpType
ACT = mybir.ActivationFunctionType
AX = mybir.AxisListType

P = 128
B, N, D = 8, 256, 256
NT = N // P
KC = D // P
DH = 64
HQ, HKV = 16, 4
G = HQ // HKV
HX = D // DH
NC_, DC = 77, 192
NCP = NC_ + 1
DC2 = DC - P
E = 8
SCALE = DH ** -0.5
LN_EPS = 1e-5
RMS_FLOOR = 1e-16
MASKED = 3e38
VW = DH + 1

W_COLS = dict(kv=KC * 2 * HKV * DH, q=KC * HQ * DH, o=HQ * DH // P * D, xq=KC * D, xo=KC * D, xl=KC * 2 * D,
              ex=KC * E * D, xc=2 * 2 * D, gate=KC * E)
CHUNKS_OF = {name: KC for name in W_COLS}
CHUNKS_OF["o"] = HQ * DH // P
W_AT, _at = {}, 0
for _name, _cols in W_COLS.items():
    W_AT[_name] = _at
    _at += _cols
W_ALL = _at
CHUNKS = [([("kv", 0, KC)], 0), ([("q", 0, KC)], 1), ([("o", 0, 8)], 0),
          ([("xq", 0, KC), ("xo", 0, KC), ("xl", 0, KC)], 1), ([("ex", 0, 1)], 0), ([("ex", 1, 2)], 1),
          ([("xc", 0, 2), ("gate", 0, KC)], 0)]
STAGE = (2048, 2048)
DVE_CHUNKS = 3
ARENA = sum(STAGE) + 2 * NT * 2 * N

KVU = "K"
RING = tuple(f"R{i}" for i in range(7))
BANKS = RING + ("YY",)


def banks_of(step):
    kind, args = step[0], step[1:]
    if kind in ("a_scores", "b_scores"):
        return {"a_scores": NT, "b_scores": NT + 1}[kind]
    return int(kind in ("a_proj", "a_turn", "a_max", "a_mrow", "a_pv", "a_ot", "b_zt", "b_ct", "b_proj",
                        "b_cproj", "b_turn", "b_max", "b_maxc", "b_mrow", "b_pv", "b_ot", "b_wo", "c_x2t", "c_gate", "c_expert"))


def reader_of(step):
    kind, args = step[0], step[1:]
    if kind in ("a_turn", "b_turn"):
        return (kind[0] + "_lo", *args)
    if kind == "b_proj" and args != ("v",):
        return ("b_xn", *args)
    return {"b_cproj": ("b_xn", "c"), "a_ot": ("a_otlo", *args), "b_ot": ("b_otlo",), "b_wo": ("b_res",),
            "c_x2t": ("c_x2lo",), "c_gate": ("c_route",)}.get(kind, step)


def listed(text):
    return [tuple(int(w) if w.isdigit() else w for w in step.split(":")) for step in text.split()]


ORDER = listed("""
    a_proj:K c_x2t a_rot:K b_ln a_proj:V c_x2lo a_proj:0 a_rot:0 a_turn:K c_gate b_cln b_z a_lo:K a_proj:1
    a_turn:0 b_zt b_cn c_route a_max:0:0 b_ct a_max:0:1 c_weights a_rot:1 c_expert:0 a_max:0:2 c_expert:1
    a_max:0:3 a_proj:2 b_proj:q b_proj:k a_mrow:0 a_rot:2 a_turn:1 b_ss:q a_lo:0 c_expert:2 b_cproj b_proj:v
    b_ss:k b_xn:q a_scores:0:0 a_lo:1 b_bias a_scores:0:1 a_max:1:0 b_turn:q a_load b_ss:c a_max:1:1
    a_max:1:2 a_max:1:3 a_pv:0:0 b_xn:k c_expert:3 a_mrow:1 b_lo:q a_turn:2 a_pv:0:1 a_lo:2 b_turn:k
    a_proj:3 a_scores:1:0 a_max:2:0 a_rot:3 b_xn:c c_expert:4 a_scores:1:1 a_max:2:1 a_ot:0 b_next a_max:2:2
    b_turn:c a_otlo:0 b_lo:k a_next a_turn:3 a_max:2:3 b_lo:c a_pv:1:0 c_expert:5 a_pv:1:1 a_mrow:2 b_maxc:0
    b_max:0 b_max:1 a_wo:0 a_ot:1 a_max:3:0 a_otlo:1 c_expert:6 b_max:2 b_max:3 b_maxc:1 a_scores:2:0 a_wo:1
    a_scores:2:1 a_bias b_mrow a_max:3:1 a_max:3:2 c_expert:7 a_max:3:3 a_lo:3 a_pv:2:0 a_mrow:3 a_pv:2:1
    b_scores:0 a_ot:2 a_scores:3:0 b_pv:0 c_out b_scores:1 a_split a_otlo:2 a_pv:3:0 a_scores:3:1 b_pv:1
    a_pv:3:1 b_ot c_y a_wo:2 b_otlo a_ot:3 b_wo a_otlo:3 b_res a_wo:3 a_res b_x2 a_norm
""")

FILL = listed("""
    w_split:1 a_proj:K w_need:2 a_rot:K w_split:2 a_proj:0 a_rot:0 a_turn:K a_proj:1 a_turn:0 w_load:4
    a_lo:K a_max:0:0 a_max:0:1 a_load a_rot:1 a_lo:0 w_split:3 a_max:0:2 a_turn:1 a_max:0:3 a_proj:2
    a_mrow:0 w_load:5 a_max:1:0 a_rot:2 a_max:1:1 a_proj:V a_max:1:2 a_max:1:3 w_split:4 a_proj:3
    a_scores:0:0 a_lo:1 a_mrow:1 a_scores:0:1 a_turn:2 a_pv:0:0 a_pv:0:1 a_max:2:0 a_scores:1:0 a_rot:3
    a_scores:1:1 w_load:6 a_ot:0 a_max:2:1 a_max:2:2 a_turn:3 a_max:2:3 a_lo:2 a_otlo:0 a_pv:1:0 a_mrow:2
    a_pv:1:1 a_max:3:0 w_need:3 a_max:3:1 a_wo:0 w_split:5 a_max:3:2 a_ot:1 a_max:3:3 a_scores:2:0 a_otlo:1
    a_scores:2:1 a_mrow:3 a_lo:3 a_pv:2:0 a_pv:2:1 a_wo:1 a_next a_scores:3:0 a_scores:3:1 a_ot:2 a_otlo:2
    a_bias a_split a_pv:3:0 a_pv:3:1 w_split:6 a_wo:2 a_ot:3 a_otlo:3 a_wo:3 w_need:7 a_res a_norm
""")


def only(steps, streams):
    return [step for step in steps if step[0][0] in streams]


class Section:

    def __init__(self, steps, base):
        self.steps, self.base, self.per, self.turn = steps, dict(base), {k: 0 for k in BANKS}, 0
        self.order, at = {}, {step: n for n, step in enumerate(steps)}
        freed_at = {k: n - len(RING) for n, k in enumerate(RING)}
        for step in steps:
            for n in range(banks_of(step)):
                bank = min(RING, key=freed_at.get)
                assert freed_at[bank] < at[step], step
                freed_at[bank] = at[reader_of(step)]
                self.order[step, n] = bank, self.per[bank]
                self.per[bank] += 1

    def after(self, turns):
        return {k: self.base[k] + turns * self.per[k] for k in BANKS}

    def bank(self, step, n=0):
        return self.order[step, n][0]

    def used(self, step, n=0):
        bank, order = self.order[step, n]
        return self.turn * self.per[bank] + (self.base[bank] + order)


def build(nc, ins, out):
    ctx = ExitStack()
    with ctx:
        def sb(name, shape, dt=F32):
            return ctx.enter_context(nc.sbuf_tensor(name, shape, dt))

        def sem(name):
            return ctx.enter_context(nc.semaphore(name))

        bank = {k: ctx.enter_context(nc.psum_tensor(f"bank_{k}", [P, 512], F32)) for k in BANKS}
        full = {k: sem(f"full_{k}") for k in BANKS}
        free = {k: sem(f"free_{k}") for k in BANKS}

        w_hi, w_lo = sb("w_hi", [P, W_ALL], F32R), sb("w_lo", [P, W_ALL], F32R)
        arena = sb("arena", [P, ARENA])
        stage = [arena[:, 0:STAGE[0]], arena[:, STAGE[0]:sum(STAGE)]]
        arena_at = [0]

        def lay(*shape):
            n = int(np.prod(shape))
            t = arena[:, arena_at[0]:arena_at[0] + n]
            arena_at[0] += n
            names = "abc"[:len(shape)]
            if len(shape) == 1:
                return t
            return t.rearrange(f"p ({' '.join(names)}) -> p {' '.join(names)}",
                               **{m: w for m, w in zip(names[1:], shape[1:])})

        prob = [arena[:, ARENA - n * NT * 2 * N:ARENA - (n - 1) * NT * 2 * N].rearrange(
            "p (t n) -> p t n", t=NT) for n in (1, 2)]

        ident = sb("ident", [P, P])
        cos_t, sin_t = sb("cos_t", [P, NT, DH]), sb("sin_t", [P, NT, DH])
        before = sb("before", [P, E, E])
        bo, xbo = sb("bo", [P, D]), sb("xbo", [P, D])
        half_neg = sb("half_neg", [P, 8])
        ln_g, ln_b = sb("ln_g", [P, KC]), sb("ln_b", [P, KC])
        lc_g, lc_b = sb("lc_g", [P, KC]), sb("lc_b", [P, KC])
        g_q, g_k = sb("g_q", [P, 1]), sb("g_k", [P, 1])

        x_t = sb("x_t", [P, KC, N])
        x_n = sb("x_n", [P, NT, D])
        x_hi, x_lo = sb("x_hi", [P, KC, N], F32R), sb("x_lo", [P, KC, N], F32R)
        rot_c, rot_s = sb("rot_c", [P, NT, G, DH]), sb("rot_s", [P, NT, G, DH])
        rot = [sb(f"rot{i}", [P, NT * G, DH]) for i in range(2)]
        k1, k2 = sb("k1", [P, HKV, N], F32R), sb("k2", [P, HKV, N], F32R)
        t1 = [sb(f"t1_{i}", [P, G, N], F32R) for i in range(2)]
        t2 = [sb(f"t2_{i}", [P, G, N], F32R) for i in range(2)]
        val = sb("val", [P, NT, HKV, VW])
        mx = [sb(f"mx{i}", [P, NT, G]) for i in range(2)]
        mrows = sb("mrows", [DH, P], F32R)
        mrow, mrow_b = mrows[0:NT * G, :], mrows[32:32 + NT * HX, :]
        rden = [sb(f"rden{p}", [P, NT, 2]) for p in range(2)]
        att = sb("att", [P, NT, G, DH])
        att_hi, att_lo = sb("att_hi", [P, 2, N], F32R), sb("att_lo", [P, 2, N], F32R)
        st_a, mv_a = sb("st_a", [P, NT, 6]), sb("mv_a", [P, NT, 2])
        ve_a, rs_a = sb("ve_a", [P, NT]), sb("rs_a", [P, NT])
        x1 = sb("x1", [P, NT, D])

        xr = sb("xr", [P, NT, D])
        ctx_n = sb("ctx_n", [NC_, DC])
        m_u8, mc_u8 = sb("m_u8", [P, NC_], U8), sb("mc_u8", [NC_, 1], U8)
        m_neg, mc_neg = sb("m_neg", [P, NC_]), sb("mc_neg", [NC_, 1])
        st_b, mv_b = sb("st_b", [P, NT, 6]), sb("mv_b", [P, NT, 2])
        ve_b, rs_b = sb("ve_b", [P, NT]), sb("rs_b", [P, NT])
        st_c, mv_c = sb("st_c", [P, 1, 6]), sb("mv_c", [P, 1, 2])
        ve_c, rs_c = sb("ve_c", [P, 1]), sb("rs_c", [P, 1])
        z_hi, z_lo = sb("z_hi", [P, KC, N], F32R), sb("z_lo", [P, KC, N], F32R)
        cf = sb("cf", [P, 2, NCP])
        c_hi, c_lo = sb("c_hi", [P, 2, NCP], F32R), sb("c_lo", [P, 2, NCP], F32R)
        probx = lay(NT + 1, 2 * N)
        z = probx[:, 0, :].rearrange("p (t c) -> p t c", t=NT)
        zf = probx[:, 1, :].rearrange("p (k n) -> p k n", k=KC)
        sq = [probx[:, n, :] for n in range(3)]
        ss = [sb(f"ss{n}", [P, NT * HX]) for n in range(3)]
        ri = [sb(f"ri{n}", [P, NT * HX]) for n in range(3)]
        xn = lay(NT * HX, DH)
        attx = xn.rearrange("p (t h) d -> p t h d", t=NT)
        t1x, t2x = sb("t1x", [P, HX, N], F32R), sb("t2x", [P, HX, N], F32R)
        k1x, k2x = sb("k1x", [P, HX, N + NCP], F32R), sb("k2x", [P, HX, N + NCP], F32R)
        valx = lay(NT + 1, HX, VW)
        mx_l, mx_c, mx_b = sb("mx_l", [P, NT, HX]), sb("mx_c", [P, NT, HX]), sb("mx_b", [P, NT, HX])
        sc_c = lay(2, NT, NC_)
        rden_b = [sb(f"rden_b{p}", [P, NT, 2]) for p in range(HX // 2)]
        attx_hi, attx_lo = z_hi, z_lo

        x2 = acc = y = lay(NT, D)
        x2_hi, x2_lo = sb("x2_hi", [P, KC, N], F32R), sb("x2_lo", [P, KC, N], F32R)
        st_y, mv_y = sb("st_y", [P, NT, 6]), sb("mv_y", [P, NT, 2])
        ve_y, rs_y = sb("ve_y", [P, NT]), sb("rs_y", [P, NT])
        lg = sb("lg", [P, NT, E])
        gt, eq = (lay(NT, E * E).rearrange("p t (e f) -> p t e f", e=E) for _ in range(2))
        rank, sel0, sel1 = sb("rank", [P, NT, E]), sb("sel0", [P, NT, E]), sb("sel1", [P, NT, E])
        top = sb("top", [P, 6, NT])
        gate = sb("gate", [P, NT, E])
        gw = sb("gw", [P, KC, 2 * E], F32R)

        w_in = [sem(f"w_in{i}") for i in range(2)]
        c_in, g_in = sem("c_in"), sem("g_in")
        w_hi_done, w_lo_done = sem("w_hi_done"), sem("w_lo_done")
        fill_done, const_done = sem("fill_done"), sem("const_done")
        gw_done = sem("gw_done")
        xt_in, xn_in = sem("xt_in"), sem("xn_in")
        x_hi_done, x_lo_done = sem("x_hi_done"), sem("x_lo_done")
        rot_done = sem("rot_done")
        hi_done = sem("hi_done")
        mr_in = [sem(f"mr_in{i}") for i in range(2)]
        oh_done = sem("oh_done")
        bo_done, xbo_done = sem("bo_done"), sem("xbo_done")
        wo_done = sem("wo_done")
        ya_free = sem("ya_free")
        va_done, ra_done = sem("va_done"), sem("ra_done")
        x1_done = sem("x1_done")
        dve_a = sem("dve_a")
        cx_in = sem("cx_in")
        vb_done, rb_done = sem("vb_done"), sem("rb_done")
        z_done = sem("z_done")
        zh_done, zl_done = sem("zh_done"), sem("zl_done")
        sq_done = sem("sq_done")
        xn_done = sem("xn_done")
        tx_done = sem("tx_done")
        mb_done = sem("mb_done")
        mrb_in = sem("mrb_in")
        ohx_done = sem("ohx_done")
        x2_done = sem("x2_done")
        x2h_done = sem("x2h_done")
        dif_done, exp_done = sem("dif_done"), sem("exp_done")
        y_done, y_out = sem("y_done"), sem("y_out")
        dve_b, dve_c = sem("dve_b"), sem("dve_c")
        vc_done, rc_done = sem("vc_done"), sem("rc_done")

        A_LINKS, B_LINKS, C_LINKS = 10, 14, 14
        B_NORMS = 6

        first = Section(FILL, {k: 0 for k in BANKS})
        second = Section(only(ORDER, "ab"), first.after(1))
        third = Section(ORDER, second.after(1))
        steady = Section(ORDER, third.after(1))
        drain = Section([s for s in only(ORDER, "bc") if s != ("b_next",)], steady.after(B - 3))
        last = Section(only(ORDER, "c"), drain.after(1))

        def walk(eng, steps_of):
            def run(sec, a, b, c):
                steps = steps_of(sec, a, b, c)
                for step in sec.steps:
                    if step[0] in steps:
                        steps[step[0]](*step[1:])

            run(first, 0, None, None)
            run(second, 1, 0, None)
            run(third, 2, 1, 0)
            with eng.Fori(0, B - 3) as i:
                steady.turn = i
                run(steady, i + 3, i + 2, i + 1)
            run(drain, None, B - 1, B - 2)
            run(last, None, None, B - 1)

        def wait(eng, s, value):
            if not isinstance(value, int) or value > 0:
                eng.wait_ge(s, value)

        def weights(t, name, chunk, c0, c1):
            per = W_COLS[name] // CHUNKS_OF[name]
            at = W_AT[name] + chunk * per
            return t[:, at + c0:at + c1]

        def chunk(n):
            parts, st = CHUNKS[n]
            name, k0, _ = parts[0]
            at = W_AT[name] + k0 * (W_COLS[name] // CHUNKS_OF[name])
            cols = sum(W_COLS[m] // CHUNKS_OF[m] * (k1_ - k0_) for m, k0_, k1_ in parts)
            loads = sum(1 + (m == "xc") for c in CHUNKS[:n + 1] if c[1] == st for m, _, _ in c[0])
            return at, cols, st, 16 * loads

        def latest(sec, fills, then):
            last = {}
            for step, n in fills:
                k, order = sec.order[step, n]
                if k not in last or order > sec.order[last[k]][1]:
                    last[k] = step, n
            for step, n in then:
                last.pop(sec.bank(step, n), None)
            return last.items()

        def freed(eng, sec, *fills, then=()):
            for k, fill in latest(sec, fills, then):
                eng.wait_ge(free[k], sec.used(*fill) + 1)

        def was_filled(eng, sec, *fills, then=()):
            for k, fill in latest(sec, fills, then):
                eng.wait_ge(full[k], sec.used(*fill) + 1)

        def by_head(t, n=N):
            pairs = t[:, 0:2 * n].rearrange("p (h n) -> p h n", h=2)
            return [(pairs[0:DH], slice(0, 4, 2)), (pairs[DH:P], slice(1, 4, 2))]

        def is_head(t, h):
            return t[:, :].rearrange("p (h n) -> p h n", h=2)[:, h, :]

        block = ctx.enter_context(nc.Block())

        fixed = [(half_neg[:], -0.5)]
        fixed += [(t[DH:P].bitcast(F32), 0.0) for t in (k2, t2[0], t2[1], k2x, t2x)]
        fixed += [(k1x[:, :, N + NC_:N + NCP].bitcast(F32), 0.0), (val[:, :, :, DH:VW], 1.0)]
        fixed += [(t[DH:DH + 1].bitcast(F32), 1.0) for t in (k2, k2x)]
        FILLS = len(fixed)

        @block.sync
        def _(sp):
            def load_weights(n):
                parts, st = CHUNKS[n]
                if n >= 2:
                    sp.wait_ge(w_lo_done, n - 1)
                if n == len(CHUNKS) - 1:
                    sp.wait_ge(const_done, 1)
                at = 0
                for name, k0, k1_ in parts:
                    cols = W_COLS[name] // CHUNKS_OF[name] * (k1_ - k0)
                    src, dst = ins[name], stage[st][:, at:at + cols]
                    if name == "xc":
                        sp.dma_start(dst[:, 0:2 * D], src[0:P, :]).then_inc(w_in[st], 16)
                        src, dst = src[P:DC, :], dst[0:DC2, 2 * D:4 * D]
                        sp.dma_start(dst, src).then_inc(w_in[st], 16)
                    else:
                        sp.dma_start(dst.rearrange("p (k n) -> p k n", k=k1_ - k0),
                                     src.rearrange("(k p) n -> p k n", p=P)[:, k0:k1_, :]).then_inc(w_in[st], 16)
                    at += cols

            sp.dma_start(x_t[:], ins["x_t"][0].rearrange("(k p) n -> p k n", p=P)).then_inc(xt_in, 16)
            load_weights(0)
            for dst, src in ((cos_t[:], ins["cos"].rearrange("(t p) d -> p t d", p=P)),
                             (sin_t[:], ins["sin"].rearrange("(t p) d -> p t d", p=P)), (ident[:], ins["ident"])):
                sp.dma_start(dst, src).then_inc(c_in, 16)
            load_weights(1)
            for dst, src in ((before[:], ins["before"].partition_broadcast(P)),
                             (bo[:], ins["bo"].partition_broadcast(P)),
                             (xbo[:], ins["xbo"].partition_broadcast(P)),
                             (ln_g[:], ins["ln_g"]), (ln_b[:], ins["ln_b"]),
                             (lc_g[:, 0:1], ins["lc_g"][0:P, :]), (lc_g[0:DC2, 1:2], ins["lc_g"][P:DC, :]),
                             (lc_b[:, 0:1], ins["lc_b"][0:P, :]), (lc_b[0:DC2, 1:2], ins["lc_b"][P:DC, :]),
                             (g_q[0:DH, :], ins["g_q"]), (g_q[DH:P, :], ins["g_q"]),
                             (g_k[0:DH, :], ins["g_k"]), (g_k[DH:P, :], ins["g_k"])):
                sp.dma_start(dst, src).then_inc(g_in, 16)
            for n in (2, 3):
                load_weights(n)

            def load_context(b):
                sp.dma_start(ctx_n[:], ins["ctx"][b]).then_inc(cx_in, 16)
                sp.dma_start(m_u8[:], ins["mask"][b].partition_broadcast(P)).then_inc(cx_in, 16)
                sp.dma_start(mc_u8[:], ins["mask"][b].rearrange("(n o) -> n o", o=1)).then_inc(cx_in, 16)

            load_context(0)

            def steps_of(sec, a, b, c):
                def a_load():
                    wait(sp, x1_done, a)
                    sp.nop(nofuse=True)
                    sp.dma_start(x_n[:], ins["x"][a].rearrange("(t p) c -> p t c", p=P)).then_inc(xn_in, 16)

                def a_next():
                    sp.wait_ge(x_lo_done, a + 1)
                    sp.nop(nofuse=True)
                    sp.dma_start(x_t[:], ins["x_t"][a + 1].rearrange("(k p) n -> p k n", p=P)).then_inc(xt_in, 16)

                def a_mrow(g):
                    freed(sp, sec, (("a_mrow", g), 0))
                    sp.nop(nofuse=True)
                    row = t2[g % 2][DH:DH + 1, :, :].bitcast(F32).rearrange("o h (t n) -> o t h n", t=NT)
                    for it in range(NT):
                        sp.dma_start(row[:, it, :, :], mrow[it * G:(it + 1) * G, :].bitcast(F32)).then_inc(mr_in[g % 2], 16)

                def b_next():
                    sp.wait_ge(xn_done, (b + 1) * 3)
                    sp.nop(nofuse=True)
                    load_context(b + 1)

                def b_mrow():
                    freed(sp, sec, (("b_mrow",), 0))
                    sp.nop(nofuse=True)
                    row = t2x[DH:DH + 1, :, :].bitcast(F32).rearrange("o h (t n) -> o t h n", t=NT)
                    for it in range(NT):
                        sp.dma_start(row[:, it, :, :], mrow_b[it * HX:(it + 1) * HX, :].bitcast(F32)).then_inc(mrb_in, 16)

                def c_y():
                    sp.wait_ge(y_done, c + 1)
                    sp.nop(nofuse=True)
                    sp.dma_start(out[c].rearrange("(t p) c -> p t c", p=P), y[:]).then_inc(y_out, 16)

                return dict(w_load=load_weights, a_load=a_load, a_next=a_next, a_mrow=a_mrow, b_next=b_next, b_mrow=b_mrow, c_y=c_y)

            walk(sp, steps_of)
            sp.wait_ge(y_out, 16 * B)

        @block.tensor
        def _(pe):
            mm = nc.tensor.matmul

            def split_product(o, l_hi, l_lo, r_hi, r_lo, start, stop):
                mm(o, l_hi, r_hi, start=start, stop=False)
                mm(o, l_hi, r_lo, start=False, stop=False)
                return mm(o, l_lo, r_hi, start=False, stop=stop)

            def project(o, l_hi, l_lo, name, c0, c1):
                for it in range(NT):
                    rows = slice(it * P, (it + 1) * P)
                    for k in range(KC):
                        ins_ = split_product(o[:, it * D:(it + 1) * D], l_hi[:, k, rows], l_lo[:, k, rows],
                                             weights(w_hi, name, k, c0, c1), weights(w_lo, name, k, c0, c1),
                                             k == 0, k == KC - 1)
                return ins_

            pe.wait_ge(w_lo_done, 1)
            pe.wait_ge(c_in, 3 * 16)

            def steps_of(sec, a, b, c):
                def take(step, n=0):
                    k = sec.bank(step, n)
                    wait(pe, free[k], sec.used(step, n))
                    return bank[k], full[k]

                def w_need(n):
                    pe.wait_ge(w_lo_done, n)
                    if n == 2:
                        pe.wait_ge(fill_done, FILLS)
                    if n == len(CHUNKS):
                        pe.wait_ge(const_done, 2)
                        pe.wait_ge(gw_done, 2 * KC)

                def a_proj(u):
                    pe.wait_ge(x_lo_done, a + 1)
                    o, done = take(("a_proj", u))
                    name, c0 = ("kv", {KVU: 0, "V": HKV * DH}[u]) if u in (KVU, "V") else ("q", u * G * DH)
                    project(o, x_hi, x_lo, name, c0, c0 + G * DH).then_inc(done, 1)

                def a_turn(u):
                    n = 0 if u == KVU else u + 1
                    pe.wait_ge(rot_done, a * 5 + n + 1)
                    o, done = take(("a_turn", u))
                    for pair in range(2):
                        for it in range(NT):
                            src = rot[n % 2][:, it * G + 2 * pair:it * G + 2 * pair + 2, :]
                            ins_ = nc.tensor.transpose(is_head(o, pair)[:, it * P:(it + 1) * P], src, ident[:])
                    ins_.then_inc(done, 1)

                def a_max(g, h):
                    if h == 0:
                        pe.wait_ge(hi_done, a * 5 + g + 2)
                        freed(pe, sec, (("a_turn", KVU), 0), then=[(("a_max", g, h), 0)])
                    o, done = take(("a_max", g, h))
                    for it in range(NT):
                        ins_ = mm(o[:, it * N:(it + 1) * N], t1[g % 2][:, h, it * P:(it + 1) * P],
                                  k1[:, g, :], start=True, stop=True)
                    ins_.then_inc(done, 1)

                def a_mrow(g):
                    freed(pe, sec, *((("a_max", g, h), 0) for h in range(G)), then=[(("a_mrow", g), 0)])
                    o, done = take(("a_mrow", g))
                    nc.tensor.transpose(o[0:NT * G, 0:P], mx[g % 2][:], ident[:]).then_inc(done, 1)

                def a_scores(g, p):
                    if p == 0:
                        freed(pe, sec, (("a_turn", g), 0), then=[(("a_scores", g, 0), 0)])
                        pe.wait_ge(mr_in[g % 2], (a * 2 + (g // 2 + 1)) * 16 * NT)
                    for jt in range(NT):
                        o, done = take(("a_scores", g, p), jt)
                        rows = slice(jt * P, (jt + 1) * P)
                        mm(o[:, :], k1[:, g, rows], t1[g % 2][:, 2 * p:2 * p + 2, :], start=True, stop=False)
                        mm(o[:, :], k2[:, g, rows], t2[g % 2][:, 2 * p:2 * p + 2, :], start=False,
                           stop=True).then_inc(done, 1)

                def a_pv(g, p):
                    freed(pe, sec, *((("a_scores", g, p), jt) for jt in range(NT)),
                          *[(("a_proj", "V"), 0)][g:], then=[(("a_pv", g, p), 0)])
                    o, done = take(("a_pv", g, p))
                    for it in range(NT):
                        for h in range(2):
                            c = (it * 2 + h) * VW
                            for jt in range(NT):
                                ins_ = mm(o[:, c:c + VW], prob[p][:, jt, h * N + it * P:h * N + (it + 1) * P],
                                          val[:, jt, g, :], start=(jt == 0), stop=(jt == NT - 1))
                    ins_.then_inc(done, 1)

                def a_ot(g):
                    freed(pe, sec, *((("a_pv", g, p), 0) for p in range(2)), then=[(("a_ot", g), 0)])
                    o, done = take(("a_ot", g))
                    for p in range(2):
                        for it in range(NT):
                            ins_ = nc.tensor.transpose(is_head(o, p)[:, it * P:(it + 1) * P],
                                                       att[:, it, 2 * p:2 * p + 2, :], ident[:])
                    ins_.then_inc(done, 1)

                def a_wo(g):
                    if g == 0:
                        wait(pe, ya_free, a)
                    pe.wait_ge(oh_done, a * 4 + g + 1)
                    freed(pe, sec, (("a_ot", g), 0))
                    for it in range(NT):
                        rows = slice(it * P, (it + 1) * P)
                        for p in range(2):
                            o = bank["YY"][:, it * D:(it + 1) * D]
                            r_hi, r_lo = (weights(w, "o", 2 * g + p, 0, D) for w in (w_hi, w_lo))
                            l_hi, l_lo = att_hi[:, p, rows], att_lo[:, p, rows]
                            mm(o, l_hi, r_hi, start=(g == 0 and it == 0 and p == 0), stop=False, skip_group_check=True)
                            mm(o, l_hi, r_lo, start=False, stop=False, skip_group_check=True)
                            ins_ = mm(o, l_lo, r_hi, start=False, stop=(g == HKV - 1 and p == 1), skip_group_check=True)
                    ins_.then_inc(wo_done, 1)

                def b_zt():
                    pe.wait_ge(z_done, b * 2 + 1)
                    o, done = take(("b_zt",))
                    for k in range(KC):
                        for it in range(NT):
                            ins_ = nc.tensor.transpose(is_head(o, k)[:, it * P:(it + 1) * P],
                                                       z[:, it, k * P:(k + 1) * P], ident[:])
                    ins_.then_inc(done, 1)

                def b_ct():
                    pe.wait_ge(z_done, b * 2 + 2)
                    o, done = take(("b_ct",))
                    nc.tensor.transpose(o[:, 0:NC_], ctx_n[:, 0:P], ident[0:NC_, 0:NC_])
                    nc.tensor.transpose(o[0:DC2, P:P + NC_], ctx_n[:, P:DC],
                                        ident[0:NC_, 0:NC_]).then_inc(done, 1)

                def b_proj(u):
                    pe.wait_ge(zl_done, b * 2 + 1)
                    o, done = take(("b_proj", u))
                    name, c0 = {"q": ("xq", 0), "k": ("xl", 0), "v": ("xl", D)}[u]
                    project(o, z_hi, z_lo, name, c0, c0 + D).then_inc(done, 1)

                def b_cproj():
                    pe.wait_ge(zl_done, b * 2 + 2)
                    o, done = take(("b_cproj",))
                    for k, rows in ((0, P), (1, DC2)):
                        ins_ = split_product(o[0:NC_, :], c_hi[0:rows, k, 0:NC_], c_lo[0:rows, k, 0:NC_],
                                             weights(w_hi, "xc", k, 0, 2 * D)[0:rows], weights(w_lo, "xc", k, 0, 2 * D)[0:rows],
                                             k == 0, k == 1)
                    ins_.then_inc(done, 1)

                def b_turn(u):
                    pe.wait_ge(xn_done, b * 3 + {"q": 1, "k": 2, "c": 3}[u])
                    if u == "c":
                        o, done = take(("b_turn", u))
                        for pair in range(HX // 2):
                            src = xn[0:NC_, 2 * pair:2 * pair + 2, :]
                            ins_ = nc.tensor.transpose(o[:, pair * NCP:pair * NCP + NC_], src, ident[0:NC_, 0:NC_])
                        ins_.then_inc(done, 1)
                        return
                    o, done = take(("b_turn", u))
                    for pair in range(HX // 2):
                        for it in range(NT):
                            src = xn[:, it * HX + 2 * pair:it * HX + 2 * pair + 2, :]
                            ins_ = nc.tensor.transpose(is_head(o, pair)[:, it * P:(it + 1) * P], src, ident[:])
                    ins_.then_inc(done, 1)

                def b_max(h):
                    o, done = take(("b_max", h))
                    for it in range(NT):
                        ins_ = mm(o[:, it * N:(it + 1) * N], t1x[:, h, it * P:(it + 1) * P],
                                  k1x[:, h, 0:N], start=True, stop=True)
                    ins_.then_inc(done, 1)

                def b_maxc(p):
                    if p == 0:
                        turns = (("b_turn", "q"), ("b_turn", "k"), ("b_turn", "c"))
                        freed(pe, sec, *((step, n) for step in turns for n in range(banks_of(step))),
                              then=[(("b_maxc", p), 0)])
                    o, done = take(("b_maxc", p))
                    for h in range(2):
                        for it in range(NT):
                            c = (h * NT + it) * NCP
                            ins_ = mm(o[:, c:c + NCP], t1x[:, 2 * p + h, it * P:(it + 1) * P],
                                      k1x[:, 2 * p + h, N:N + NCP], start=True, stop=True)
                    ins_.then_inc(done, 1)

                def b_mrow():
                    pe.wait_ge(mb_done, b + 1)
                    o, done = take(("b_mrow",))
                    nc.tensor.transpose(o[0:NT * HX, 0:P], mx_b[:], ident[:]).then_inc(done, 1)

                def b_scores(p):
                    if p == 0:
                        pe.wait_ge(mrb_in, (b + 1) * 16 * NT)
                    for jt in range(NT + 1):
                        o, done = take(("b_scores", p), jt)
                        m = P if jt < NT else NC_
                        for h in range(2):
                            keys = slice(jt * P, jt * P + m)
                            dst = o[0:m, h * N:(h + 1) * N]
                            mm(dst, k1x[:, 2 * p + h, keys], t1x[:, 2 * p + h, :], start=True, stop=False)
                            ins_ = mm(dst, k2x[:, 2 * p + h, keys], t2x[:, 2 * p + h, :], start=False, stop=True)
                        ins_.then_inc(done, 1)

                def b_pv(p):
                    freed(pe, sec, *((("b_scores", p), jt) for jt in range(NT + 1)),
                          *[(("b_proj", "v"), 0)][p:], then=[(("b_pv", p), 0)])
                    o, done = take(("b_pv", p))
                    for it in range(NT):
                        for h in range(2):
                            c = (it * 2 + h) * VW
                            for jt in range(NT + 1):
                                m = P if jt < NT else NC_
                                ins_ = mm(o[:, c:c + VW], probx[0:m, jt, h * N + it * P:h * N + (it + 1) * P],
                                          valx[0:m, jt, 2 * p + h, :], start=(jt == 0), stop=(jt == NT))
                    ins_.then_inc(done, 1)

                def b_ot():
                    freed(pe, sec, *((("b_pv", p), 0) for p in range(HX // 2)), then=[(("b_ot",), 0)])
                    o, done = take(("b_ot",))
                    for k in range(KC):
                        for it in range(NT):
                            ins_ = nc.tensor.transpose(is_head(o, k)[:, it * P:(it + 1) * P],
                                                       attx[:, it, 2 * k:2 * k + 2, :], ident[:])
                    ins_.then_inc(done, 1)

                def b_wo():
                    freed(pe, sec, (("b_ot",), 0), then=[(("b_wo",), 0)])
                    o, done = take(("b_wo",))
                    project(o, attx_hi, attx_lo, "xo", 0, D).then_inc(done, 1)

                def c_x2t():
                    pe.wait_ge(x2_done, c + 1)
                    o, done = take(("c_x2t",))
                    for k in range(KC):
                        for it in range(NT):
                            ins_ = nc.tensor.transpose(is_head(o, k)[:, it * P:(it + 1) * P],
                                                       x2[:, it, k * P:(k + 1) * P], ident[:])
                    ins_.then_inc(done, 1)

                def c_gate():
                    freed(pe, sec, (("c_x2t",), 0), then=[(("c_gate",), 0)])
                    o, done = take(("c_gate",))
                    for it in range(NT):
                        rows = slice(it * P, (it + 1) * P)
                        dst = o[:, it * 2 * E:(it + 1) * 2 * E]
                        for k in range(KC):
                            mm(dst, x2_hi[:, k, rows], gw[:, k, :], start=(k == 0), stop=False)
                            ins_ = mm(dst, x2_lo[:, k, rows], gw[:, k, :], start=False, stop=(k == KC - 1))
                    ins_.then_inc(done, 1)

                def c_expert(e):
                    o, done = take(("c_expert", e))
                    project(o, x2_hi, x2_lo, "ex", e * D, (e + 1) * D).then_inc(done, 1)

                return dict(w_need=w_need, a_proj=a_proj, a_turn=a_turn, a_max=a_max, a_mrow=a_mrow, a_scores=a_scores,
                            a_pv=a_pv, a_ot=a_ot, a_wo=a_wo, b_zt=b_zt, b_ct=b_ct, b_proj=b_proj,
                            b_cproj=b_cproj, b_turn=b_turn, b_max=b_max, b_maxc=b_maxc, b_mrow=b_mrow,
                            b_scores=b_scores, b_pv=b_pv, b_ot=b_ot, b_wo=b_wo, c_x2t=c_x2t,
                            c_gate=c_gate, c_expert=c_expert)

            walk(pe, steps_of)

        @block.scalar
        def _(act):
            run = nc.scalar.activation
            def w_split(n):
                at, cols, st, count = chunk(n)
                act.wait_ge(w_in[st], count)
                run(w_hi[:, at:at + cols], stage[st][:, 0:cols], ACT.Copy).then_inc(w_hi_done, 1)

            def w_need(n):
                act.wait_ge(w_lo_done, n)
                act.wait_ge(g_in, 13 * 16)
                if n == len(CHUNKS):
                    for half, w in enumerate((w_hi, w_lo)):
                        for k in range(KC):
                            run(gw[:, k, half * E:(half + 1) * E], weights(w, "gate", k, 0, E),
                                ACT.Copy).then_inc(gw_done, 1)

            def x_split(a):
                act.wait_ge(xt_in, (a + 1) * 16)
                run(x_hi[:], x_t[:], ACT.Copy).then_inc(x_hi_done, 1)

            x_split(0)
            w_split(0)

            def steps_of(sec, a, b, c):
                def filled(step, n=0):
                    k = sec.bank(step, n)
                    act.wait_ge(full[k], sec.used(step, n) + 1)
                    return bank[k], free[k]

                def a_split():
                    was_filled(act, sec, *((("a_proj", u), 0) for u in (KVU, "V", HKV - 1)))
                    act.nop(nofuse=True)
                    x_split(a + 1)

                def a_proj(u):
                    if u != "V":
                        return
                    wait(act, wo_done, a * 4)
                    o, done = filled(("a_proj", u))
                    run(val[:, :, :, 0:DH], o[:, :].rearrange("p (t h d) -> p t h d", t=NT, h=HKV),
                        ACT.Copy).then_inc(done, 1)

                def a_turn(u):
                    if u == KVU or u < 2:
                        wait(act, wo_done, a * 4)
                    else:
                        was_filled(act, sec, (("a_scores", u - 2, 1), 1), then=[(("a_turn", u), 0)])
                    o, _ = filled(("a_turn", u))
                    first, second = (k1[0:DH], k2[0:DH]) if u == KVU else (t1[u % 2][0:DH], t1[u % 2][DH:P])
                    for dst in (first, second):
                        for src, heads in by_head(o):
                            ins_ = run(dst[:, heads, :], src, ACT.Copy)
                    ins_.then_inc(hi_done, 1)

                def a_mrow(g):
                    o, done = filled(("a_mrow", g))
                    wait(act, mr_in[(g - 1) % 2], (a * 2 + (g + 1) // 2) * 16 * NT)
                    run(mrow[:, :], o[0:NT * G, 0:P], ACT.Copy, scale=-1.0).then_inc(done, 1)

                def a_scores(g, p):
                    if g == 0:
                        wait(act, wo_done, a * 4)
                    else:
                        was_filled(act, sec, (("a_pv", g - 1, p), 0), then=[(("a_scores", g, p), 0)])
                    for jt in range(NT):
                        o, done = filled(("a_scores", g, p), jt)
                        run(prob[p][:, jt, :], o[:, :], ACT.Exp, scale=SCALE).then_inc(done, 1)

                def a_ot(g):
                    o, _ = filled(("a_ot", g))
                    wait(act, wo_done, a * 4 + g)
                    run(att_hi[:], o[:, :].rearrange("p (h n) -> p h n", h=2),
                        ACT.Copy).then_inc(oh_done, 1)

                def b_zt():
                    o, done = filled(("b_zt",))
                    wait(act, x2_done, b)
                    for k in range(KC):
                        ins_ = run(zf[:, k, :], is_head(o, k), ACT.Identity, bias=ln_b[:, k:k + 1],
                                   scale=ln_g[:, k:k + 1])
                    ins_.then_inc(done, 1)
                    freed(act, sec, (("b_zt",), 0))
                    run(z_hi[:], zf[:], ACT.Copy).then_inc(zh_done, 1)

                def b_ct():
                    o, done = filled(("b_ct",))
                    run(cf[:, 0, 0:NC_], o[:, 0:NC_], ACT.Identity, bias=lc_b[:, 0:1], scale=lc_g[:, 0:1])
                    run(cf[0:DC2, 1, 0:NC_], o[0:DC2, P:P + NC_], ACT.Identity, bias=lc_b[0:DC2, 1:2],
                        scale=lc_g[0:DC2, 1:2]).then_inc(done, 1)
                    freed(act, sec, (("b_ct",), 0))
                    run(c_hi[:, 0, 0:NC_], cf[:, 0, 0:NC_], ACT.Copy)
                    run(c_hi[0:DC2, 1, 0:NC_], cf[0:DC2, 1, 0:NC_], ACT.Copy).then_inc(zh_done, 1)

                def b_proj(u):
                    o, done = filled(("b_proj", u))
                    if u == "v":
                        run(valx[:, 0:NT, :, 0:DH], o[:, :].rearrange("p (t h d) -> p t h d", t=NT, h=HX),
                            ACT.Copy).then_inc(done, 1)
                    else:
                        run(sq[{"q": 0, "k": 1}[u]][:], o[:, :], ACT.Square).then_inc(sq_done, 1)

                def b_cproj():
                    o, _ = filled(("b_cproj",))
                    run(valx[0:NC_, NT, :, 0:DH], o[0:NC_, D:2 * D].rearrange("p (h d) -> p h d", h=HX), ACT.Copy)
                    run(sq[2][0:NC_, 0:D], o[0:NC_, 0:D], ACT.Square).then_inc(sq_done, 1)

                def b_turn(u):
                    o, _ = filled(("b_turn", u))
                    n, keys = (NCP, slice(N, N + NC_)) if u == "c" else (N, slice(0, N))
                    first, second = (t1x[0:DH], t1x[DH:P]) if u == "q" else (k1x[0:DH], k2x[0:DH])
                    width = NC_ if u == "c" else N
                    for dst in (first, second):
                        for half, (src, heads) in enumerate(by_head(o, n)):
                            own = (g_q, g_k)[u != "q"][half * DH:(half + 1) * DH]
                            ins_ = run(dst[:, heads, keys], src[:, :, 0:width], ACT.Copy, scale=own[:, 0:1])
                    ins_.then_inc(tx_done, 1)

                def b_mrow():
                    o, done = filled(("b_mrow",))
                    run(mrow_b[:, :], o[0:NT * HX, 0:P], ACT.Copy, scale=-1.0).then_inc(done, 1)

                def b_scores(p):
                    if p:
                        was_filled(act, sec, (("b_pv", p - 1), 0), then=[(("b_scores", p), 0)])
                    for jt in range(NT + 1):
                        o, done = filled(("b_scores", p), jt)
                        if jt < NT:
                            run(probx[:, jt, :], o[:, :], ACT.Exp, scale=SCALE).then_inc(done, 1)
                        else:
                            run(probx[0:NC_, jt, :], o[0:NC_, :], ACT.Exp, bias=mc_neg[:, 0:1],
                                scale=SCALE).then_inc(done, 1)

                def b_ot():
                    o, _ = filled(("b_ot",))
                    run(attx_hi[:], o[:, :].rearrange("p (h n) -> p h n", h=2), ACT.Copy).then_inc(ohx_done, 1)

                def c_x2t():
                    o, _ = filled(("c_x2t",))
                    wait(act, y_done, c)
                    run(x2_hi[:], o[:, :].rearrange("p (h n) -> p h n", h=2), ACT.Copy).then_inc(x2h_done, 1)

                def c_route():
                    act.wait_ge(dif_done, c + 1)
                    run(top[:, 3, :], top[:, 2, :], ACT.Exp).then_inc(exp_done, 1)

                return dict(w_split=w_split, w_need=w_need, a_split=a_split, a_proj=a_proj, a_turn=a_turn,
                            a_mrow=a_mrow, a_scores=a_scores, a_ot=a_ot, b_zt=b_zt, b_ct=b_ct, b_proj=b_proj,
                            b_cproj=b_cproj, b_turn=b_turn, b_mrow=b_mrow, b_scores=b_scores, b_ot=b_ot,
                            c_x2t=c_x2t, c_route=c_route)

            walk(act, steps_of)

        @block.gpsimd
        def _(pool):
            tt = nc.gpsimd.tensor_tensor
            def x_split(a):
                pool.wait_ge(x_hi_done, a + 1)
                tt(x_lo[:], x_t[:], x_hi[:], ALU.subtract).then_inc(x_lo_done, 1)

            x_split(0)
            pool.wait_ge(x_lo_done, 1)
            for n, (t, value) in enumerate(fixed):
                nc.gpsimd.memset(t, value).then_inc(fill_done, 1)
                pool.wait_ge(fill_done, n + 1)

            def w_split(n):
                if n >= DVE_CHUNKS:
                    at, cols, st, _ = chunk(n)
                    pool.wait_ge(w_lo_done, n)
                    pool.wait_ge(w_hi_done, n + 1)
                    tt(w_lo[:, at:at + cols], stage[st][:, 0:cols], w_hi[:, at:at + cols],
                       ALU.subtract).then_inc(w_lo_done, 1)

            def w_load(n):
                if n == len(CHUNKS) - 1:
                    pool.wait_ge(w_lo_done, n - 1)
                    nc.gpsimd.memset(stage[0][:, 2 * D:4 * D], 0.0).then_inc(const_done, 1)

            def w_need(n):
                if n == len(CHUNKS):
                    pool.wait_ge(w_lo_done, n)
                    nc.gpsimd.memset(valx[:, :, :, DH:VW], 1.0).then_inc(const_done, 1)
                    pool.wait_ge(const_done, 2)

            def steps_of(sec, a, b, c):
                def a_rot(u):
                    freed(pool, sec, (("a_proj", u), 0))
                    n = 0 if u == KVU else u + 1
                    if n < 2:
                        wait(pool, wo_done, a * 4)
                    else:
                        was_filled(pool, sec, (("a_turn", KVU if n == 2 else u - 2), 0))
                    tt(rot[n % 2][:], rot_c[:].rearrange("p t h d -> p (t h) d"), rot_s[:].rearrange("p t h d -> p (t h) d"),
                       ALU.add).then_inc(rot_done, 1)

                def a_split():
                    x_split(a + 1)

                def biased(dst, t, bias):
                    return tt(dst[:], t[:], bias[:].unsqueeze(1).to_broadcast([P, NT, D]), ALU.add)

                def a_bias():
                    if sec is first:
                        pool.wait_ge(g_in, 13 * 16)
                    pool.wait_ge(xn_in, (a + 1) * 16)
                    biased(x_n, x_n, bo).then_inc(bo_done, 1)

                def b_bias():
                    pool.wait_ge(z_done, b * 2 + 1)
                    wait(pool, x2_done, b)
                    biased(xr, x1, xbo).then_inc(xbo_done, 1)

                def power(n, rows, src, dst, cols, done_in, done_out, count):
                    pool.wait_ge(done_in, count)
                    tt(dst[0:rows, 0:cols], src[0:rows, 0:cols], half_neg[0:rows, 0:cols],
                       ALU.pow).then_inc(done_out, 1)

                def a_res():
                    power(0, P, ve_a, rs_a, NT, va_done, ra_done, a + 1)

                def b_norm(n, rows, src, dst, cols):
                    power(n, rows, src, dst, cols, vb_done, rb_done, b * B_NORMS + n + 1)

                def b_ln():
                    b_norm(0, P, ve_b, rs_b, NT)

                def b_cln():
                    b_norm(1, NC_, ve_c, rs_c, 1)

                def b_ss(u):
                    n = "qkc".index(u)
                    b_norm(2 + n, NC_ if u == "c" else P, ss[n], ri[n], HX if u == "c" else NT * HX)

                def b_res():
                    b_norm(5, P, ve_b, rs_b, NT)

                def c_out():
                    power(0, P, ve_y, rs_y, NT, vc_done, rc_done, c + 1)

                def b_zt():
                    pool.wait_ge(zh_done, b * 2 + 1)
                    tt(z_lo[:], zf[:], z_hi[:], ALU.subtract).then_inc(zl_done, 1)

                def b_ct():
                    pool.wait_ge(zh_done, b * 2 + 2)
                    tt(c_lo[:, 0, 0:NC_], cf[:, 0, 0:NC_], c_hi[:, 0, 0:NC_], ALU.subtract)
                    tt(c_lo[0:DC2, 1, 0:NC_], cf[0:DC2, 1, 0:NC_], c_hi[0:DC2, 1, 0:NC_],
                       ALU.subtract).then_inc(zl_done, 1)

                return dict(w_load=w_load, w_split=w_split, w_need=w_need, a_split=a_split, a_bias=a_bias, b_bias=b_bias,
                            a_rot=a_rot, a_res=a_res, b_ln=b_ln, b_cln=b_cln,
                            b_ss=b_ss, b_res=b_res, b_zt=b_zt, b_ct=b_ct, c_out=c_out)

            walk(pool, steps_of)

        @block.vector
        def _(dve):
            v = nc.vector
            def w_split(n):
                if n >= DVE_CHUNKS:
                    return
                at, cols, st, _ = chunk(n)
                dve.wait_ge(w_hi_done, n + 1)
                v.tensor_tensor(w_lo[:, at:at + cols], stage[st][:, 0:cols], w_hi[:, at:at + cols],
                                ALU.subtract).then_inc(w_lo_done, 1)

            def w_need(n):
                dve.wait_ge(g_in, 13 * 16)

            w_split(0)
            dve.wait_ge(c_in, 3 * 16)

            def steps_of(sec, a, b, c):
                count = {"a": 0, "b": 0, "c": 0}

                def link(ins_, s):
                    count[s] += 1
                    chain, at, per = {"a": (dve_a, a, A_LINKS), "b": (dve_b, b, B_LINKS), "c": (dve_c, c, C_LINKS)}[s]
                    ins_.then_inc(chain, 1)
                    dve.wait_ge(chain, at * per + count[s])

                def filled(step, n=0):
                    k = sec.bank(step, n)
                    dve.wait_ge(full[k], sec.used(step, n) + 1)
                    return bank[k], free[k]

                def stats(s, src, rows, tiles, st, mv, ve):
                    for t in range(tiles):
                        ins_ = v.bn_stats(st[0:rows, t, :], src[t])
                    link(ins_, s)
                    dve.nop(nofuse=True)
                    for t in range(tiles):
                        ins_ = v.bn_aggr(mv[0:rows, t, :], st[0:rows, t, :])
                    link(ins_, s)
                    return v.tensor_scalar(ve[0:rows, 0:tiles], mv[0:rows, 0:tiles, 1], LN_EPS, None, ALU.add)

                def normed(dst, src, rows, tiles, mv, rs):
                    for t in range(tiles):
                        ins_ = v.tensor_scalar(dst[t], src[t], mv[0:rows, t, 0:1], rs[0:rows, t:t + 1],
                                               ALU.subtract, ALU.mult)
                    return ins_

                def tiles_of(t):
                    return [t[:, it, :] for it in range(NT)]

                def a_proj(u):
                    if u == "V":
                        return
                    n = 0 if u == KVU else u + 1
                    o, done = filled(("a_proj", u))
                    wait(dve, rot_done, a * 5 + n)
                    q4 = o[:, :].rearrange("p (t h d) -> p t h d", t=NT, h=G)

                    def table(t, lo, hi):
                        return t[:, :, lo:hi].unsqueeze(2).to_broadcast([P, NT, G, hi - lo])

                    hw = DH // 2
                    v.tensor_tensor(rot_c[:], q4, table(cos_t, 0, DH), ALU.mult)
                    v.tensor_tensor(rot_s[:, :, :, 0:hw], q4[:, :, :, hw:DH], table(sin_t, 0, hw), ALU.mult)
                    v.tensor_tensor(rot_s[:, :, :, hw:DH], q4[:, :, :, 0:hw], table(sin_t, hw, DH),
                                    ALU.mult).then_inc(done, 1)

                def a_lo(u):
                    n = 0 if u == KVU else u + 1
                    o, done = filled(("a_turn", u))
                    dve.wait_ge(hi_done, a * 5 + n + 1)
                    hi, lo = (k1[0:DH], k1[DH:P]) if u == KVU else (t1[u % 2][0:DH], t2[u % 2][0:DH])
                    for src, heads in by_head(o):
                        ins_ = v.tensor_tensor(lo[:, heads, :], src, hi[:, heads, :], ALU.subtract)
                    ins_.then_inc(done, 1)

                def a_max(g, h):
                    o, done = filled(("a_max", g, h))
                    if h == 0 and g >= 2:
                        was_filled(dve, sec, (("a_mrow", g - 2), 0), then=[(("a_max", g, h), 0)])
                    elif h == 0:
                        wait(dve, wo_done, a * 4)
                    v.tensor_reduce(mx[g % 2][:, :, h], o[:, :].rearrange("p (t n) -> p t n", t=NT),
                                    AX.X, ALU.max).then_inc(done, 1)

                def over_sum(dst, step, rd, s):
                    o, done = filled(step)
                    o4 = o[:, 0:2 * NT * VW].rearrange("p (t h d) -> p t h d", t=NT, h=2)
                    link(v.reciprocal(rd[:], o4[:, :, :, DH]), s)
                    v.tensor_tensor(dst, o4[:, :, :, 0:DH], rd[:].unsqueeze(3).to_broadcast([P, NT, 2, DH]),
                                    ALU.mult).then_inc(done, 1)

                def a_pv(g, p):
                    if p == 0:
                        wait(dve, oh_done, a * 4 + g)
                    over_sum(att[:, :, 2 * p:2 * p + 2, :], ("a_pv", g, p), rden[p], "a")

                def a_otlo(g):
                    o, done = filled(("a_ot", g))
                    dve.wait_ge(oh_done, a * 4 + g + 1)
                    v.tensor_tensor(att_lo[:], o[:, :].rearrange("p (h n) -> p h n", h=2),
                                    att_hi[:], ALU.subtract).then_inc(done, 1)

                def a_res():
                    dve.wait_ge(wo_done, (a + 1) * 4)
                    dve.wait_ge(bo_done, a + 1)
                    v.tensor_tensor(x_n[:], bank["YY"][:, :].rearrange("p (t c) -> p t c", t=NT), x_n[:],
                                    ALU.add).then_inc(ya_free, 1)
                    dve.wait_ge(ya_free, a + 1)
                    stats("a", tiles_of(x_n), P, NT, st_a, mv_a, ve_a).then_inc(va_done, 1)

                def a_norm():
                    dve.wait_ge(ra_done, a + 1)
                    if b is not None:
                        dve.wait_ge(xbo_done, b + 1)
                    normed(tiles_of(x1), tiles_of(x_n), P, NT, mv_a, rs_a).then_inc(x1_done, 1)
                    check("a")

                def b_ln():
                    dve.wait_ge(x1_done, b + 1)
                    stats("b", tiles_of(x1), P, NT, st_b, mv_b, ve_b).then_inc(vb_done, 1)

                def b_z():
                    dve.wait_ge(rb_done, b * B_NORMS + 1)
                    wait(dve, x2_done, b)
                    normed(tiles_of(z), tiles_of(x1), P, NT, mv_b, rs_b).then_inc(z_done, 1)

                def b_cln():
                    dve.wait_ge(cx_in, (b + 1) * 48)
                    v.tensor_scalar(m_neg[:], m_u8[:], 1.0, MASKED, ALU.subtract, ALU.mult)
                    link(v.tensor_scalar(mc_neg[:], mc_u8[:], 1.0, MASKED, ALU.subtract, ALU.mult), "b")
                    stats("b", [ctx_n[:]], NC_, 1, st_c, mv_c, ve_c).then_inc(vb_done, 1)

                def b_cn():
                    dve.wait_ge(rb_done, b * B_NORMS + 2)
                    normed([ctx_n[:]], [ctx_n[:]], NC_, 1, mv_c, rs_c).then_inc(z_done, 1)

                def b_ss(u):
                    n = "qkc".index(u)
                    rows, cols = (NC_, HX) if u == "c" else (P, NT * HX)
                    dve.wait_ge(sq_done, b * 3 + n + 1)
                    link(v.tensor_reduce(ss[n][0:rows, 0:cols], sq[n][0:rows, 0:cols * DH].rearrange("p (h d) -> p h d", d=DH),
                                         AX.X, ALU.add), "b")
                    v.tensor_scalar(ss[n][0:rows, 0:cols], ss[n][0:rows, 0:cols], 1.0 / DH, RMS_FLOOR,
                                    ALU.mult, ALU.max).then_inc(vb_done, 1)

                def b_xn(u):
                    n = "qkc".index(u)
                    rows, cols = (NC_, HX) if u == "c" else (P, NT * HX)
                    step = ("b_cproj",) if u == "c" else ("b_proj", u)
                    o, done = bank[sec.bank(step)], free[sec.bank(step)]
                    src = o[0:rows, 0:cols * DH].rearrange("p (h d) -> p h d", d=DH)
                    was_filled(dve, sec, (step, 0))
                    dve.wait_ge(rb_done, b * B_NORMS + n + 3)
                    dve.nop(nofuse=True)
                    if n:
                        was_filled(dve, sec, (("b_turn", "qkc"[n - 1]), 0))
                    else:
                        wait(dve, ohx_done, b)
                    v.tensor_tensor(xn[0:rows, 0:cols], src, ri[n][0:rows, 0:cols].unsqueeze(2).to_broadcast([rows, cols, DH]),
                                    ALU.mult).then_inc(xn_done, 1)
                    dve.wait_ge(xn_done, b * 3 + n + 1)
                    dve.sem_inc(done, 1)

                def b_lo(u):
                    o, done = filled(("b_turn", u))
                    dve.wait_ge(tx_done, b * 3 + "qkc".index(u) + 1)
                    n, keys = (NCP, slice(N, N + NC_)) if u == "c" else (N, slice(0, N))
                    hi, lo = (t1x[0:DH], t2x[0:DH]) if u == "q" else (k1x[0:DH], k1x[DH:P])
                    gain = (g_q if u == "q" else g_k)[0:DH, 0:1]
                    for src, heads in by_head(o, n):
                        ins_ = v.scalar_tensor_tensor(lo[:, heads, keys], src[:, :, 0:keys.stop - keys.start], gain,
                                                      hi[:, heads, keys], ALU.mult, ALU.subtract)
                    ins_.then_inc(done, 1)

                def b_max(h):
                    o, done = filled(("b_max", h))
                    v.tensor_reduce(mx_l[:, :, h], o[:, :].rearrange("p (t n) -> p t n", t=NT),
                                    AX.X, ALU.max).then_inc(done, 1)

                def b_maxc(p):
                    o, done = filled(("b_maxc", p))
                    v.tensor_tensor(sc_c[:], o[:, 0:2 * NT * NCP].rearrange("p (h t n) -> p h t n", h=2, t=NT)[:, :, :, 0:NC_],
                                    m_neg[:].unsqueeze(1).unsqueeze(1).to_broadcast([P, 2, NT, NC_]), ALU.add).then_inc(done, 1)
                    freed(dve, sec, (("b_maxc", p), 0))
                    link(v.tensor_reduce(mx_c[:].rearrange("p t h -> p h t")[:, 2 * p:2 * p + 2, :], sc_c[:],
                                         AX.X, ALU.max), "b")

                def b_mrow():
                    freed(dve, sec, *((("b_max", h), 0) for h in range(HX)))
                    v.tensor_tensor(mx_b[:], mx_l[:], mx_c[:], ALU.max).then_inc(mb_done, 1)

                def b_pv(p):
                    if p == 0:
                        was_filled(dve, sec, (("b_turn", "c"), 0), then=[(("b_pv", 0), 0)])
                    over_sum(attx[:, :, 2 * p:2 * p + 2, :], ("b_pv", p), rden_b[p], "b")

                def b_otlo():
                    o, done = filled(("b_ot",))
                    dve.wait_ge(ohx_done, b + 1)
                    v.tensor_tensor(attx_lo[:], o[:, :].rearrange("p (h n) -> p h n", h=2), attx_hi[:],
                                    ALU.subtract).then_inc(done, 1)

                def b_res():
                    o, done = filled(("b_wo",))
                    dve.wait_ge(xbo_done, b + 1)
                    v.tensor_tensor(xr[:], o[:, :].rearrange("p (t c) -> p t c", t=NT), xr[:], ALU.add).then_inc(done, 1)
                    freed(dve, sec, (("b_wo",), 0))
                    stats("b", tiles_of(xr), P, NT, st_b, mv_b, ve_b).then_inc(vb_done, 1)

                def b_x2():
                    dve.wait_ge(rb_done, b * B_NORMS + 6)
                    wait(dve, y_out, b * 16)
                    normed(tiles_of(x2), tiles_of(xr), P, NT, mv_b, rs_b).then_inc(x2_done, 1)
                    check("b")

                def c_x2lo():
                    o, done = filled(("c_x2t",))
                    dve.wait_ge(x2h_done, c + 1)
                    v.tensor_tensor(x2_lo[:], o[:, :].rearrange("p (h n) -> p h n", h=2), x2_hi[:],
                                    ALU.subtract).then_inc(done, 1)

                def c_route():
                    o, done = filled(("c_gate",))
                    v.tensor_reduce(lg[:], o[:, 0:NT * 2 * E].rearrange("p (t s e) -> p t e s", t=NT, s=2),
                                    AX.X, ALU.add).then_inc(done, 1)
                    freed(dve, sec, (("c_gate",), 0))
                    own = lg[:].unsqueeze(3).to_broadcast([P, NT, E, E])
                    other = lg[:].unsqueeze(2).to_broadcast([P, NT, E, E])
                    v.tensor_tensor(gt[:], other, own, ALU.is_gt)
                    link(v.tensor_tensor(eq[:], other, own, ALU.is_equal), "c")
                    link(v.tensor_tensor(eq[:], eq[:], before[:].unsqueeze(1).to_broadcast([P, NT, E, E]), ALU.mult), "c")
                    link(v.tensor_tensor(gt[:], gt[:], eq[:], ALU.add), "c")
                    link(v.tensor_reduce(rank[:], gt[:], AX.X, ALU.add), "c")
                    v.tensor_scalar(sel0[:], rank[:], 0.0, None, ALU.is_equal)
                    link(v.tensor_scalar(sel1[:], rank[:], 1.0, None, ALU.is_equal), "c")
                    v.tensor_reduce(top[:, 0, :], lg[:], AX.X, ALU.max)
                    link(v.tensor_tensor(gate[:], lg[:], sel1[:], ALU.mult), "c")
                    link(v.tensor_reduce(top[:, 1, :], gate[:], AX.X, ALU.add), "c")
                    v.tensor_tensor(top[:, 2, :], top[:, 1, :], top[:, 0, :], ALU.subtract).then_inc(dif_done, 1)

                def c_weights():
                    dve.wait_ge(exp_done, c + 1)
                    link(v.tensor_scalar(top[:, 4, :], top[:, 3, :], 1.0, None, ALU.add), "c")
                    link(v.reciprocal(top[:, 4, :], top[:, 4, :]), "c")
                    link(v.tensor_tensor(top[:, 5, :], top[:, 4, :], top[:, 3, :], ALU.mult), "c")
                    v.tensor_tensor(sel0[:], sel0[:], top[:, 4, :].unsqueeze(2).to_broadcast([P, NT, E]), ALU.mult)
                    link(v.tensor_tensor(sel1[:], sel1[:], top[:, 5, :].unsqueeze(2).to_broadcast([P, NT, E]), ALU.mult), "c")
                    link(v.tensor_tensor(gate[:], sel0[:], sel1[:], ALU.add), "c")

                def c_expert(e):
                    o, done = filled(("c_expert", e))
                    if e:
                        freed(dve, sec, (("c_expert", e - 1), 0))
                    for it in range(NT):
                        ins_ = v.scalar_tensor_tensor(acc[:, it, :], o[:, it * D:(it + 1) * D], gate[:, it, e:e + 1],
                                                      acc[:, it, :], ALU.mult, ALU.add)
                    ins_.then_inc(done, 1)

                def c_out():
                    freed(dve, sec, (("c_expert", E - 1), 0))
                    stats("c", tiles_of(acc), P, NT, st_y, mv_y, ve_y).then_inc(vc_done, 1)

                def c_y():
                    dve.wait_ge(rc_done, c + 1)
                    normed(tiles_of(y), tiles_of(acc), P, NT, mv_y, rs_y).then_inc(y_done, 1)
                    check("c")

                def check(s):
                    want = {"a": A_LINKS, "b": B_LINKS, "c": C_LINKS}[s]
                    assert count[s] == want, (s, count[s])

                return dict(w_split=w_split, w_need=w_need, a_proj=a_proj, a_lo=a_lo, a_max=a_max, a_pv=a_pv,
                            a_otlo=a_otlo, a_res=a_res, a_norm=a_norm, b_ln=b_ln, b_z=b_z, b_cln=b_cln, b_cn=b_cn,
                            b_ss=b_ss, b_xn=b_xn, b_lo=b_lo, b_max=b_max, b_maxc=b_maxc, b_mrow=b_mrow,
                            b_pv=b_pv, b_otlo=b_otlo, b_res=b_res, b_x2=b_x2, c_x2lo=c_x2lo, c_route=c_route,
                            c_weights=c_weights, c_expert=c_expert, c_out=c_out, c_y=c_y)

            walk(dve, steps_of)


def tables():
    inv = (np.float32(1.0) / np.float32(10000.0) ** (np.arange(0, DH, 2, dtype=np.float32) / np.float32(DH))).astype(np.float32)
    ang = np.arange(N, dtype=np.float32)[:, None] * inv[None, :]
    cos, sin = np.cos(ang).astype(np.float32), np.sin(ang).astype(np.float32)
    return {"cos": np.concatenate([cos, cos], 1), "sin": np.concatenate([-sin, sin], 1),
            "ident": np.eye(P, dtype=np.float32), "before": np.tril(np.ones((E, E), np.float32), -1)}


def kernel(**inputs):
    import concourse.bacc as bacc
    from concourse.bass_utils import run_bass_kernel_spmd

    i = {k: np.asarray(v) for k, v in inputs.items()}
    x = i["x"]
    arrays = {
        "x": x, "x_t": np.concatenate([x.transpose(0, 2, 1), np.zeros((1, D, N), x.dtype)]), "ctx": i["ctx_768"], "mask": i["mask_BxS2_bk0"],
        "q": i["L0_attn_Wq"], "kv": i["L0_attn_Wkv"], "o": i["L0_attn_Wo"],
        "xq": i["L0_xattn_Wq"].T, "xl": i["L0_xattn_Wlkv"].T, "xo": i["L0_xattn_Wo"].T, "xc": i["L0_xattn_Wkv"].T,
        "ex": i["L0_ffn_expert_w"].transpose(2, 0, 1).reshape(D, E * D), "gate": i["L0_ffn_gate_w"].T,
        "bo": i["L0_attn_bo"], "xbo": i["L0_xattn_bo"],
        "ln_g": i["L0_xattn_ln_l_g"].reshape(KC, P).T, "ln_b": i["L0_xattn_ln_l_b"].reshape(KC, P).T,
        "lc_g": i["L0_xattn_ln_x_g"].reshape(DC, 1), "lc_b": i["L0_xattn_ln_x_b"].reshape(DC, 1),
        "g_q": i["L0_xattn_qn_g"].reshape(DH, 1), "g_k": i["L0_xattn_kn_g"].reshape(DH, 1),
        **tables(),
    }
    nc = bacc.Bacc("TRN2", target_bir_lowering=False, num_devices=1)
    feeds, ins = {}, {}
    for name, a in arrays.items():
        a = np.ascontiguousarray(a)
        feeds[f"{name}_dram"] = a
        ins[name] = nc.dram_tensor(f"{name}_dram", a.shape, mybir.dt.from_np(a.dtype), kind="ExternalInput").ap()
    out = nc.dram_tensor("out_dram", (B, N, D), F32, kind="ExternalOutput").ap()
    build(nc, ins, out)
    r = run_bass_kernel_spmd(nc, [feeds], core_ids=[0])
    return r.results[0]["out_dram"]
```
